# Optimizing a Trainium2 kernel written in Bass

```python
import numpy as np
import jax
import jax.numpy as jnp

def _softmax(x, axis=-1):
    return jax.nn.softmax(x, axis=axis)

def _gelu(x):
    return jax.nn.gelu(x, approximate=True)

def _silu(x):
    return jax.nn.silu(x)

def _sigmoid(x):
    return jax.nn.sigmoid(x)

def _layernorm(x, axis=-1, eps=1e-05):
    m = jnp.mean(x, axis=axis, keepdims=True)
    v = jnp.var(x, axis=axis, keepdims=True)
    return (x - m) / jnp.sqrt(v + eps)

def _scatter_add(tgt, idx, src, axis=0):
    return tgt.at[idx].add(src)

def _segment_sum(src, seg, n):
    return jax.ops.segment_sum(src, seg, n)
kernel_name = 'mk_gnn_resnorm_d4_gnn_r8_b416d5'

def setup_inputs(seed: int=0):
    np.random.seed(seed)
    _w = jnp.asarray

    def _rec_inputs():
        import jax
        import jax.numpy as jnp
        _gk = jax.random.key(seed)
        x = -0.0001006 + 1 * jax.random.normal(jax.random.fold_in(_gk, 1), (6250, 48), jnp.float32)
        _s = jax.random.randint(jax.random.fold_in(_gk, 2), (100000,), 0, 6250, jnp.int32)
        _d = jax.random.randint(jax.random.fold_in(_gk, 3), (100000,), 0, 6250, jnp.int32)
        _loop = jnp.arange(6250, dtype=jnp.int32)
        src = jnp.concatenate([_s, _d, _loop])
        dst = jnp.concatenate([_d, _s, _loop])
        _o = jnp.argsort(dst, stable=True)
        src = src[_o]
        dst = dst[_o]
        edge_attr_40 = jax.random.uniform(jax.random.fold_in(_gk, 13), (206250, 40), jnp.float32, 0.0, 1)
        edge_weight = jax.random.uniform(jax.random.fold_in(_gk, 15), (206250,), jnp.float32, 0.0, 6.99999)
        edge_weight1 = -0.000414295 + 0.999828 * jax.random.normal(jax.random.fold_in(_gk, 16), (206250, 1), jnp.float32)
        node_type_119 = jax.random.randint(jax.random.fold_in(_gk, 17), (6250,), 0, 119, jnp.int32)
        node_vec = jax.random.uniform(jax.random.fold_in(_gk, 18), (6250,), jnp.float32, 0.0, 1.49999)
        return (x, src, dst, edge_attr_40, edge_weight, edge_weight1, node_type_119, node_vec)
    x, src, dst, edge_attr_40, edge_weight, edge_weight1, node_type_119, node_vec = _rec_inputs()

    def _L0_gnn_setup():
        import jax, jax.numpy as jnp
        import numpy as np
        N_NODES = 12500
        N_EDGES = 200000
        N_CLASSES = 48
        key = jax.random.key(seed)
        k1, k2, k3, k4 = jax.random.split(key, 4)
        soft_label = jax.random.normal(k1, (N_NODES, N_CLASSES), dtype=jnp.float32)
        e = jax.random.normal(k2, (N_EDGES, 1), dtype=jnp.float32)
        src = jax.random.randint(k3, (N_EDGES,), 0, N_NODES)
        dst = jax.random.randint(k4, (N_EDGES,), 0, N_NODES)
        return {'soft_label': soft_label, 'e': e, 'src': src, 'dst': dst}
    _L0_gnn_all = _L0_gnn_setup()
    _L0_gnn_in = {k: v for k, v in _L0_gnn_all.items() if k in ()}
    del _L0_gnn_all

    def _L1_gnn_setup():
        import jax, jax.numpy as jnp
        import numpy as np
        N_NODES = 12500
        N_EDGES = 200000
        D_IN = 48
        D_H = 48
        D_OUT = 48

        def _graph_conv(x, src, dst, w_rel, w_root, b, num_nodes):
            agg = jax.ops.segment_sum(x[src], dst, num_segments=num_nodes)
            return agg @ w_rel + x @ w_root + b
        key = jax.random.key(seed)
        ks = jax.random.split(key, 8)
        s = 0.05
        x = jax.random.normal(ks[0], (N_NODES, D_IN), dtype=jnp.float32)
        edge_index = jax.random.randint(ks[1], (2, N_EDGES), 0, N_NODES, dtype=jnp.int64)
        w_rel1 = jax.random.normal(ks[2], (D_IN, D_H), dtype=jnp.float32) * s
        w_root1 = jax.random.normal(ks[3], (D_IN, D_H), dtype=jnp.float32) * s
        b1 = jax.random.normal(ks[4], (D_H,), dtype=jnp.float32) * s
        w_rel2 = jax.random.normal(ks[5], (D_H, D_OUT), dtype=jnp.float32) * s
        w_root2 = jax.random.normal(ks[6], (D_H, D_OUT), dtype=jnp.float32) * s
        b2 = jax.random.normal(ks[7], (D_OUT,), dtype=jnp.float32) * s
        return {'x': x, 'edge_index': edge_index, 'w_rel1': w_rel1, 'w_root1': w_root1, 'b1': b1, 'w_rel2': w_rel2, 'w_root2': w_root2, 'b2': b2}
    _L1_gnn_all = _L1_gnn_setup()
    _L1_gnn_in = {k: v for k, v in _L1_gnn_all.items() if k in ('w_rel1', 'w_root1', 'b1', 'w_rel2', 'w_root2', 'b2')}
    del _L1_gnn_all

    def _L2_gnn_setup():
        import jax, jax.numpy as jnp
        import numpy as np
        CUTOFF = 6.0
        LN_EPS = 1e-05
        key = jax.random.key(seed)
        ks = jax.random.split(key, 16)
        N, E, H, R, NEL, G = (6250, 100000, 48, 40, 119, 32)
        inp = {'h': jax.random.normal(ks[0], (N, H), jnp.float32), 'edge_index': jax.random.randint(ks[1], (2, E), 0, N, jnp.int64), 'edge_attr': jax.random.uniform(ks[2], (E, R), jnp.float32), 'distances': jax.random.uniform(ks[3], (E,), jnp.float32) * 7.0, 'atom_z': jax.random.randint(ks[4], (N,), 0, NEL, jnp.int64), 'node_mult': jax.random.uniform(ks[5], (N,), jnp.float32) + 0.5, 'batch': jnp.zeros((N,), jnp.int64), 'W1': jax.random.normal(ks[6], (H, R), jnp.float32) / np.sqrt(R), 'b1': jax.random.normal(ks[7], (H,), jnp.float32) * 0.01, 'W2': jax.random.normal(ks[8], (H, H), jnp.float32) / np.sqrt(H), 'b2': jax.random.normal(ks[9], (H,), jnp.float32) * 0.01, 'emb': jax.random.normal(ks[10], (NEL, G), jnp.float32) * 0.01, 'adaptW': jax.random.normal(ks[11], (G, G), jnp.float32) * 0.01, 'gamma': jnp.ones((H,), jnp.float32), 'beta': jnp.zeros((H,), jnp.float32)}
        return inp
    _L2_gnn_all = _L2_gnn_setup()
    _L2_gnn_in = {k: v for k, v in _L2_gnn_all.items() if k in ('W1', 'b1', 'W2', 'b2', 'emb', 'adaptW', 'gamma', 'beta')}
    del _L2_gnn_all

    def _L3_gnn_setup():
        import jax, jax.numpy as jnp
        import numpy as np
        N_NODES = 12500
        N_EDGES = 200000
        C_IN = 48
        C_OUT = 48
        key = jax.random.key(seed)
        k_x, k_e, k_w = jax.random.split(key, 3)
        x = jax.random.normal(k_x, (N_NODES, C_IN), dtype=jnp.float32)
        edge_index = jax.random.randint(k_e, (2, N_EDGES), 0, N_NODES, dtype=jnp.int64)
        W = jax.random.normal(k_w, (C_IN, C_OUT), dtype=jnp.float32) * (1.0 / np.sqrt(C_IN))
        b = jnp.zeros((C_OUT,), dtype=jnp.float32)
        return {'x': x, 'edge_index': edge_index, 'W': W, 'b': b}
    _L3_gnn_all = _L3_gnn_setup()
    _L3_gnn_in = {k: v for k, v in _L3_gnn_all.items() if k in ('W', 'b')}
    del _L3_gnn_all
    return {'x': x, 'src': src, 'dst': dst, 'edge_attr_40': edge_attr_40, 'edge_weight': edge_weight, 'edge_weight1': edge_weight1, 'node_type_119': node_type_119, 'node_vec': node_vec, 'L1_gnn_w_rel1': _L1_gnn_in['w_rel1'], 'L1_gnn_w_root1': _L1_gnn_in['w_root1'], 'L1_gnn_b1': _L1_gnn_in['b1'], 'L1_gnn_w_rel2': _L1_gnn_in['w_rel2'], 'L1_gnn_w_root2': _L1_gnn_in['w_root2'], 'L1_gnn_b2': _L1_gnn_in['b2'], 'L2_gnn_W1': _L2_gnn_in['W1'], 'L2_gnn_b1': _L2_gnn_in['b1'], 'L2_gnn_W2': _L2_gnn_in['W2'], 'L2_gnn_b2': _L2_gnn_in['b2'], 'L2_gnn_emb': _L2_gnn_in['emb'], 'L2_gnn_adaptW': _L2_gnn_in['adaptW'], 'L2_gnn_gamma': _L2_gnn_in['gamma'], 'L2_gnn_beta': _L2_gnn_in['beta'], 'L3_gnn_W': _L3_gnn_in['W'], 'L3_gnn_b': _L3_gnn_in['b']}

def reference(x, src, dst, edge_attr_40, edge_weight, edge_weight1, node_type_119, node_vec, L1_gnn_w_rel1, L1_gnn_w_root1, L1_gnn_b1, L1_gnn_w_rel2, L1_gnn_w_root2, L1_gnn_b2, L2_gnn_W1, L2_gnn_b1, L2_gnn_W2, L2_gnn_b2, L2_gnn_emb, L2_gnn_adaptW, L2_gnn_gamma, L2_gnn_beta, L3_gnn_W, L3_gnn_b):
    import jax
    import jax.numpy as jnp

    def _L0_gnn_ref(soft_label, e, src, dst):
        import jax, jax.numpy as jnp
        import numpy as np
        N_NODES = 12500
        N_EDGES = 200000
        N_CLASSES = 48
        N = soft_label.shape[0]
        logits = e[:, 0]
        seg_max = jax.ops.segment_max(logits, dst, num_segments=N)
        seg_max = jnp.where(jnp.isfinite(seg_max), seg_max, 0.0)
        ex = jnp.exp(logits - seg_max[dst])
        seg_sum = jax.ops.segment_sum(ex, dst, num_segments=N)
        a = ex / seg_sum[dst]
        msg = soft_label[src] * a[:, None]
        rst = jax.ops.segment_sum(msg, dst, num_segments=N)
        return jax.nn.elu(rst)

    def _L1_gnn_ref(x, edge_index, w_rel1, w_root1, b1, w_rel2, w_root2, b2):
        import jax, jax.numpy as jnp
        import numpy as np
        N_NODES = 12500
        N_EDGES = 200000
        D_IN = 48
        D_H = 48
        D_OUT = 48

        def _graph_conv(x, src, dst, w_rel, w_root, b, num_nodes):
            agg = jax.ops.segment_sum(x[src], dst, num_segments=num_nodes)
            return agg @ w_rel + x @ w_root + b
        src, dst = (edge_index[0], edge_index[1])
        n = x.shape[0]
        h = jax.nn.relu(_graph_conv(x, src, dst, w_rel1, w_root1, b1, n))
        out = _graph_conv(h, src, dst, w_rel2, w_root2, b2, n)
        return out

    def _L2_gnn_ref(h, edge_index, edge_attr, distances, atom_z, node_mult, batch, W1, b1, W2, b2, emb, adaptW, gamma, beta):
        import jax, jax.numpy as jnp
        import numpy as np
        CUTOFF = 6.0
        LN_EPS = 1e-05
        src, dst = (edge_index[0], edge_index[1])
        N = h.shape[0]
        gate = jax.nn.silu(edge_attr @ W1.T + b1) @ W2.T + b2
        ei = emb[atom_z[src]]
        ej = emb[atom_z[dst]]
        adapt_logit = jnp.sum(ei * (ej @ adaptW.T), axis=-1, keepdims=True)
        gate = gate + adapt_logit
        cw = jnp.where(distances < CUTOFF, 0.5 * (jnp.cos(jnp.pi * distances / CUTOFF) + 1.0), 0.0)
        mj = node_mult[dst]
        msg = gate * h[dst] * (cw * mj)[:, None]
        agg = jax.ops.segment_sum(msg, src, num_segments=N)
        tot = jax.ops.segment_sum(mj, src, num_segments=N)
        agg = agg / jnp.clip(tot, 1e-08, None)[:, None]
        x = h + agg
        mu = jnp.mean(x, axis=-1, keepdims=True)
        var = jnp.mean(jnp.square(x - mu), axis=-1, keepdims=True)
        return (x - mu) / jnp.sqrt(var + LN_EPS) * gamma + beta

    def _L3_gnn_ref(x, edge_index, W, b):
        import jax, jax.numpy as jnp
        import numpy as np
        N_NODES = 12500
        N_EDGES = 200000
        C_IN = 48
        C_OUT = 48
        N = x.shape[0]
        loops = jnp.arange(N, dtype=edge_index.dtype)
        src = jnp.concatenate([edge_index[0], loops])
        dst = jnp.concatenate([edge_index[1], loops])
        deg = jax.ops.segment_sum(jnp.ones(src.shape, dtype=x.dtype), dst, num_segments=N)
        dinv = jnp.where(deg > 0, jax.lax.rsqrt(deg), 0.0)
        norm = dinv[src] * dinv[dst]
        h = x @ W
        msg = h[src] * norm[:, None]
        out = jax.ops.segment_sum(msg, dst, num_segments=N)
        return out + b
    edge_index = jnp.stack([src, dst])
    batch0 = jnp.zeros((6250,), jnp.int32)
    x = _layernorm(x + _L0_gnn_ref(x, edge_weight1, src, dst), axis=-1)
    x = _layernorm(x + _L1_gnn_ref(x, edge_index, L1_gnn_w_rel1, L1_gnn_w_root1, L1_gnn_b1, L1_gnn_w_rel2, L1_gnn_w_root2, L1_gnn_b2), axis=-1)
    x = _layernorm(x + _L2_gnn_ref(x, edge_index, edge_attr_40, edge_weight, node_type_119, node_vec, batch0, L2_gnn_W1, L2_gnn_b1, L2_gnn_W2, L2_gnn_b2, L2_gnn_emb, L2_gnn_adaptW, L2_gnn_gamma, L2_gnn_beta), axis=-1)
    x = _layernorm(x + _L3_gnn_ref(x, edge_index, L3_gnn_W, L3_gnn_b), axis=-1)
    return x

_drawn_inputs = setup_inputs


def setup_inputs(seed=0):
    import zlib

    import numpy as np

    out = dict(_drawn_inputs(seed))
    spreads = {'L2_gnn_gamma': (1.0, 0.2), 'L2_gnn_beta': (0.0, 0.1), 'L3_gnn_b': (0.0, 0.1)}
    factors = {'edge_attr_40': 6.49,
     'edge_weight': 6.472,
     'node_vec': 22.902,
     'L1_gnn_b2': 8.0,
     'L2_gnn_b1': 64.0,
     'L2_gnn_b2': 64.0,
     'L2_gnn_emb': 64.0,
     'L2_gnn_adaptW': 64.0}
    for name, (base, spread) in spreads.items():
        noise = np.random.default_rng([zlib.crc32(name.encode()), seed]).standard_normal(out[name].shape)
        drawn = base * np.exp(spread * noise) if base else spread * noise
        out[name] = jnp.asarray(drawn.astype(out[name].dtype))
    for name, factor in factors.items():
        out[name] = (out[name] * factor).astype(out[name].dtype)
    return out
```

```python
from contextlib import ExitStack

import concourse.bass as bass
from concourse import mybir

F32 = mybir.dt.float32
I32 = mybir.dt.int32
U32 = mybir.dt.uint32
ALU = mybir.AluOpType
ACT = mybir.ActivationFunctionType
AX = mybir.AxisListType

P = 128
H = 48
N = 6250
NT = -(-N // P)
NP = NT * P
E = 206250
HT = 13
LOOPS = 62
T = 2 * HT * LOOPS
EP = T * P
Q = 124
W = EP // Q
HE = HT * P
NEL = 119
G = 32
R = 40
CUTOFF = 6.0
EPS = 1e-5
BIG = 1e30
NTAB = 5
TROWS = NP + P
UW = H + 1 + G
AS = 64
PADN = NP - 1
ZR = 96
PI = 3.141592653589793


def build(nc, x_n, dst_r, dst_c, src_c, src_f,  e1_r, ew_c, attr_t, z_f, nv_n,
          emb_t, emb, adapt_t, w_rel1, w_root1, b1, w_rel2, w_root2, b2,
          m_w1t, m_b1, m_w2t, m_b2, gamma, beta, w3, b3, out):
    xu_tab = nc.dram_tensor("xu_tab", [NP, UW], F32).ap()
    u_edges = nc.dram_tensor("u_edges", [2 * LOOPS, P, HT * G], F32).ap()
    x_tabs = [nc.dram_tensor(f"x_tab{k}", [NP, H], F32).ap() for k in range(3)]
    rel_f = nc.dram_tensor("rel_f", [Q, W], F32).ap()
    sums = [nc.dram_tensor(f"sums{k}", [TROWS, H + 1], F32).ap() for k in range(NTAB)]

    with ExitStack() as ctx:
        def sb(name, shape, dt=F32):
            return ctx.enter_context(nc.sbuf_tensor(name, shape, dt))

        def sem(name):
            return ctx.enter_context(nc.semaphore(name))

        X = sb("X", [P, NT, H])
        HN = sb("HN", [P, NT, H])
        HMV = sb("HMV", [P, NT + 1, H + 1 + G])
        rel_c = sb("rel_c", [P, T])
        ex_c = sb("ex_c", [P, T])
        cw_c = sb("cw_c", [P, T])
        src_i = sb("src_i", [P, T], I32)
        pcol = sb("pcol", [1, T], I32)
        hcol = sb("hcol", [1, T], I32)
        deg = sb("deg", [P, NT])
        dinv = sb("dinv", [P, NT])
        nv = sb("nv", [P, NT])
        iota_f = sb("iota_f", [P, 2 * P])
        iota_p = sb("iota_p", [P, 2])
        dump_i = sb("dump_i", [P, 1])
        ident = sb("ident", [P, P])
        lower = sb("lower", [P, P])
        zero = sb("zero", [P, 512])
        wcat = sb("wcat", [P, 2, H])
        w1t = sb("w1t", [R, ZR])
        b1c = sb("b1c", [H, 1])
        w2b = sb("w2b", [P, H])
        w3s = sb("w3s", [H, H])
        b3b = sb("b3b", [P, H])
        gam = sb("gam", [P, H])
        bet = sb("bet", [P, H])
        st = sb("st", [P, 6, NT])
        iota_i = sb("iota_i", [P, 2 * P], I32)
        ip_i = sb("ip_i", [P, 2], I32)
        ev = sb("ev", [NEL, 2 * G])
        embt = sb("embt", [G, NEL])
        adt = sb("adt", [G, G])
        half_pi = sb("half_pi", [P, 1])
        wide_neg = sb("wide_neg", [Q, 2])
        prev_i = sb("prev_i", [Q, 1], I32)
        next_i = sb("next_i", [Q, 1], I32)
        prev_f = sb("prev_f", [Q, 1])
        next_f = sb("next_f", [Q, 1])
        pen = sb("pen", [Q, 3])
        carry = sb("carry", [Q, 4])
        crow = sb("crow", [1, 4, Q])
        cst = sb("cst", [1, 2, Q])
        cscan = sb("cscan", [1, 2, Q])
        cin = sb("cin", [Q, 2])
        base_r = sb("base_r", [Q, HT], I32)
        diff = sb("diff", [P, HT])[:, :]
        diff2 = sb("diff2", [P, HT])[:, :]
        HMV_flat = HMV[:, :, :].rearrange("p a b -> p (a b)")
        WORK = 31200
        work = sb("work", [P, WORK])

        def carve(at, rows, *shape):
            n = 1
            for s in shape:
                n *= s
            assert at[0] + n <= WORK, (at[0] + n, WORK)
            v = work[0:rows, at[0]:at[0] + n]
            at[0] += n
            if len(shape) == 2:
                v = v.rearrange("p (a b) -> p a b", b=shape[1])
            if len(shape) == 3:
                v = v.rearrange("p (a b c) -> p a b c", b=shape[1], c=shape[2])
            return v

        ps = ctx.enter_context(nc.psum_tensor("ps", [P, 8 * 512], F32))

        a = [0]
        dr_i = carve(a, Q, W)
        dr_f = carve(a, Q, W)
        e1_s = carve(a, Q, W)
        rst_f = carve(a, Q, W)
        rst_b = carve(a, Q, W)
        mx_f = carve(a, Q, W)
        mx_b = carve(a, Q, W)
        base_i = carve(a, P, T)
        dc_i = carve(a, P, T)
        tmp_c = carve(a, P, T)
        ohz = carve(a, NEL, NP)
        z_b = carve(a, NEL, NP)
        a = [0]
        a_used = None
        a = [0]
        idx_st = carve(a, P, 2, HT)
        G_ring = carve(a, P, 2, HT, UW)
        oh = carve(a, P, 2 * HT, 2 * P)
        a = [0]
        attr_s = [carve(a, R, HE) for _ in range(2)]
        src_b = [carve(a, P, HT, P) for _ in range(2)]
        rel_b = [carve(a, P, HE) for _ in range(2)]
        oh_t = [carve(a, P, 2, HE) for _ in range(2)]
        eq = [carve(a, P, HT, P) for _ in range(2)]
        eql = carve(a, P, HT, P)
        s1t = [carve(a, P, HE) for _ in range(2)]
        hg = carve(a, P, HT, UW)
        u_s = [carve(a, P, HT, G) for _ in range(2)]
        uv = carve(a, P, HT, G)
        adp = carve(a, P, HT)
        msg = [carve(a, P, HT, H + 1) for _ in range(2)]
        smm = [carve(a, P, HT, H + 1) for _ in range(2)]
        first = carve(a, P, HT)
        srcf = carve(a, P, HT)
        sidx = [carve(a, P, HT) for _ in range(2)]
        zt = carve([0], P, (TROWS // P) * (H + 1))
        a = [0]
        cat = carve(a, P, NT, 2 * H + 1)
        cat_t = carve(a, P, NT, P)
        ta = carve(a, P, NT, H)
        tb = carve(a, P, NT, H)
        agg = carve(a, P, NT, H + 1)
        ld = [carve(a, P, NT, H + 1) for _ in range(2)]
        tc = carve([a[0] - 2 * NT * (H + 1)], P, NT, H)
        xu = carve([WORK - NT * UW], P, NT, UW)

        edges_init = sem("edges_init")
        edge_ends = sem("edge_ends")
        pool_turn = sem("pool_turn")
        oh_plain = sem("oh_plain")
        eq_step = sem("eq_step")
        msg_step = sem("msg_step")
        prep_loaded = sem("prep_loaded")
        wts_loaded = sem("wts_loaded")
        consts_made = sem("consts_made")
        rel_rows_made = sem("rel_rows_made")
        rel_stored = sem("rel_stored")
        zeros_made = sem("zeros_made")
        tabs_zeroed = sem("tabs_zeroed")
        ident_made = sem("ident_made")
        ohz_made = sem("ohz_made")
        ev_mm = sem("ev_mm")
        ev_made = sem("ev_made")
        uv_mm = sem("uv_mm")
        uv_taken = sem("uv_taken")
        carry_out = sem("carry_out")
        carry_rows = sem("carry_rows")
        carry_scanned = sem("carry_scanned")
        carry_back = sem("carry_back")
        shifted = sem("shifted")
        exp_made = sem("exp_made")
        ex_turned = sem("ex_turned")
        ex_taken = sem("ex_taken")
        cos_arg = sem("cos_arg")
        cos_made = sem("cos_made")
        acc_free = sem("acc_free")
        acc_done = sem("acc_done")
        xu_made = sem("xu_made")
        xu_stored = sem("xu_stored")
        sqrt_in = sem("sqrt_in")
        sqrt_out = sem("sqrt_out")
        elu_in = sem("elu_in")
        elu_out = sem("elu_out")
        cat_made = sem("cat_made")
        cat_turned = sem("cat_turned")
        cat_taken = sem("cat_taken")
        conv_done = sem("conv_done")
        rows_made = sem("rows_made")
        rows_stored = sem("rows_stored")
        hmv_made = sem("hmv_made")
        s1_ones = sem("s1_ones")
        sums_added = sem("sums_added")
        sums_in = [sem("sums_in0"), sem("sums_in1")]
        out_made = sem("out_made")
        out_stored = sem("out_stored")
        dve_step = sem("dve_step")
        act_step = sem("act_step")

        passes = []
        for k in range(4):
            passes.append({s: [sem(f"{s}{k}_{h}") for h in range(2)]
                           for s in ("idx_ready", "gathered", "used", "oh_ready")})
        u_free = [sem("u_free0"), sem("u_free1")]
        u_stored = [sem("u_stored0"), sem("u_stored1")]

        def pair(name):
            return [sem(f"{name}0"), sem(f"{name}1")]

        e_in = pair("e_in")
        z_mm = sem("z_mm")
        z_used = pair("z_used")
        silu_done = sem("silu_done")
        oht_made = pair("oht_made")
        picked = pair("picked")
        hg_taken = sem("hg_taken")
        eq_made = pair("eq_made")
        gate_mm = pair("gate_mm")
        msg_made = pair("msg_made")
        summed = pair("summed")
        smm_taken = sem("smm_taken")
        sidx_made = pair("sidx_made")
        scattered = [sem(f"scattered{k}") for k in range(NTAB)]

        CH = HE // 4
        N_WTS = 15
        N_PREP = 9

        def wait(eng, s, v):
            if not (isinstance(v, int) and v <= 0):
                eng.wait_ge(s, v)

        def last_messages(eng, g, h):
            wait(eng, msg_made[1 - h], g + h)

        def bc(ap, n):
            return ap.unsqueeze(2).to_broadcast([ap.shape[0], ap.shape[1], n])

        def bm(ap, n):
            return ap.unsqueeze(1).to_broadcast([ap.shape[0], n, ap.shape[1]])

        def scatters_before(s, g):
            k = s % NTAB
            per = len(range(k, 2 * HT, NTAB))
            return g * per + s // NTAB

        def scatters_through(k, h, g):
            per = len(range(k, 2 * HT, NTAB))
            return g * per + len(range(k, (h + 1) * HT, NTAB))

        z_ps = [ps[0:ZR, 512 * b:512 * b + CH] for b in (0, 3, 7, 0)]

        def ps_run(bank, off, n, w):
            c = 512 * bank + off
            return ps[:, c:c + n * w].rearrange("p (a b) -> p a b", b=w)

        gate_runs = [(0, 10, ps_run(3, 0, 10, H)), (10, 3, ps_run(7, 0, 3, H))]
        sum_runs = [(0, 10, ps_run(4, 0, 10, H + 1)), (10, 3, ps_run(1, 0, 3, H + 1))]
        pick_runs = [(0, 6, ps_run(5, 0, 6, UW)), (6, 6, ps_run(6, 0, 6, UW)), (12, 1, ps_run(2, 0, 1, UW))]

        def slot(runs, k):
            for k0, n, v in runs:
                if k0 <= k < k0 + n:
                    return v[:, k - k0, :]

        acc = ps[:, 0:NT * AS].rearrange("p (i c) -> p i c", c=AS)
        conv_ps = [ps[:, 512 * (3 + b):512 * (3 + b) + 10 * H].rearrange("p (a b) -> p a b", b=H) for b in range(5)]

        block = ctx.enter_context(nc.Block())

        @block.sync
        def _(sp):
            for dst, src in ((dr_i.bitcast(I32), dst_r), (e1_s, e1_r), (dc_i.bitcast(I32), dst_c),
                             (base_i.bitcast(I32), dst_c[0:1, :].to_broadcast([P, T])),
                             (src_i[:, :], src_c), (cw_c[:, :], ew_c), (X[:, :, :], x_n), (nv[:, :], nv_n),
                             (z_b.bitcast(I32), z_f.unsqueeze(0).to_broadcast([NEL, NP]))):
                sp.dma_start(dst, src).then_inc(prep_loaded, 16)
            sp.wait_ge(edges_init, 1)
            with nc.allow_non_contiguous_dma(reason="one element per row, once"):
                sp.dma_start(prev_i[1:Q, :], dst_r[0:Q - 1, W - 1:W]).then_inc(edge_ends, 16)
                sp.dma_start(next_i[0:Q - 1, :], dst_r[1:Q, 0:1]).then_inc(edge_ends, 16)
            for dst, src in ((wcat[0:H, 0, :], w_rel1), (wcat[H:2 * H, 0, :], w_root1), (wcat[2 * H:2 * H + 1, 0, :], b1.unsqueeze(0)),
                             (wcat[0:H, 1, :], w_rel2), (wcat[H:2 * H, 1, :], w_root2), (wcat[2 * H:2 * H + 1, 1, :], b2.unsqueeze(0)),
                             (w1t[:, 0:H], m_w1t), (b1c[:, :], m_b1.unsqueeze(1)), (w2b[0:H, :], m_w2t), (w2b[H:H + 1, :], m_b2.unsqueeze(0)),
                             (w3s[:, :], w3), (b3b[:, :], b3.unsqueeze(0).to_broadcast([P, H])),
                             (gam[:, :], gamma.unsqueeze(0).to_broadcast([P, H])), (bet[:, :], beta.unsqueeze(0).to_broadcast([P, H])),
                             (ev[:, 0:G], emb), (embt[:, :], emb_t), (adt[:, :], adapt_t)):
                sp.dma_start(dst, src).then_inc(wts_loaded, 16)
            sp.wait_ge(rel_rows_made, 1)
            sp.dma_start(rel_f, rst_f).then_inc(rel_stored, 16)
            sp.wait_ge(xu_made, 1)
            sp.dma_start(xu_tab.rearrange("(i p) f -> p i f", p=P), xu).then_inc(xu_stored, 16)
            sp.sem_inc(u_free[0], 1)
            sp.sem_inc(u_free[1], 1)
            with sp.Fori(0, LOOPS) as g:
                for h in range(2):
                    sp.wait_ge(passes[0]["gathered"][h], (g + 1) * (16 * HT))
                    sp.dma_start(u_edges[bass.ds(g * 2 + h, 1)].rearrange("a p f -> (a p) f").rearrange("p (k f) -> p k f", f=G),
                                 G_ring[:, h, :, H + 1:UW]).then_inc(u_stored[h], 16)
                    sp.wait_ge(u_stored[h], (g + 1) * 16)
                    sp.sem_inc(u_free[h], 1)
            sp.wait_ge(u_stored[0], 16 * LOOPS)
            sp.wait_ge(u_stored[1], 16 * LOOPS)
            for k in range(2):
                sp.wait_ge(rows_made, k + 1)
                src_rows = X if k == 0 else HN
                sp.dma_start(x_tabs[k].rearrange("(i p) f -> p i f", p=P), src_rows[:, :, :]).then_inc(rows_stored, 16)
            sp.wait_ge(zeros_made, 1)
            for k in range(NTAB):
                sp.dma_start(sums[k].rearrange("(p a) f -> p (a f)", p=P), zt).then_inc(tabs_zeroed, 16)
            sp.wait_ge(rel_stored, 16)
            sp.wait_ge(hmv_made, 1)

            def edge_loads(g, h):
                n0 = g * (2 * HE) + h * HE
                wait(sp, z_used[h], g)
                wait(sp, sidx_made[h], g)
                wait(sp, oht_made[h], g)
                wait(sp, msg_made[h], g)
                sp.dma_start(attr_s[h], attr_t[:, bass.ds(n0, HE)]).then_inc(e_in[h], 16)
                sp.dma_start(src_b[h].rearrange("p a b -> p (a b)").bitcast(I32),
                             src_f[bass.ds(n0, HE)].unsqueeze(0).to_broadcast([P, HE])).then_inc(e_in[h], 16)
                sp.dma_start(rel_b[h], rel_f.rearrange("q w -> (q w)")[bass.ds(n0, HE)].unsqueeze(0).to_broadcast([P, HE])).then_inc(e_in[h], 16)
                sp.dma_start(u_s[h].rearrange("p a b -> p (a b)"),
                             u_edges[bass.ds(g * 2 + h, 1)].rearrange("a p f -> (a p) f")).then_inc(e_in[h], 16)

            edge_loads(0, 0)
            edge_loads(0, 1)
            with sp.Fori(1, LOOPS) as g:
                for h in range(2):
                    edge_loads(g, h)
            for k in range(NTAB):
                sp.wait_ge(scattered[k], 16 * scatters_before(k, LOOPS))
            sp.wait_ge(msg_made[1], LOOPS)
            for k in range(NTAB):
                if k >= 2:
                    sp.wait_ge(sums_added, k - 1)
                sp.dma_start(ld[k % 2], sums[k][0:NP, :].rearrange("(i p) f -> p i f", p=P)).then_inc(sums_in[k % 2], 16)
            sp.wait_ge(rows_made, 3)
            sp.dma_start(x_tabs[2].rearrange("(i p) f -> p i f", p=P), HN[:, :, :]).then_inc(rows_stored, 16)
            sp.wait_ge(out_made, 1)
            full = N // P
            sp.dma_start(out[0:full * P, :].rearrange("(i p) f -> p i f", p=P), X[:, 0:full, :]).then_inc(out_stored, 16)
            sp.dma_start(out[full * P:N, :], X[0:N - full * P, full, :]).then_inc(out_stored, 16)
            sp.wait_ge(out_stored, 32)

        @block.gpsimd
        def _(pool):
            nc.gpsimd.iota(iota_i[:, :], [[1, 2 * P]], base=0, channel_multiplier=0).then_inc(consts_made, 1)
            nc.gpsimd.iota(ip_i[:, :], [[P, 2]], base=0, channel_multiplier=1).then_inc(consts_made, 1)

            def gather_pass(k, table, width, stored, value):
                pz = passes[k]
                pool.wait_ge(stored, value)
                with pool.Fori(0, LOOPS) as g:
                    for h in range(2):
                        pool.wait_ge(pz["idx_ready"][h], g + 1)
                        pool.wait_ge(pz["used"][h], g + 1)
                        if k == 0:
                            pool.wait_ge(u_free[h], g + 1)
                        pool.sem_inc(pool_turn, 1)
                        for j in range(HT):
                            pool.indirect_dma_start(G_ring[:, h, j, 0:width], None, table,
                                                    bass.IndirectOffsetOnAxis(ap=idx_st.bitcast(U32)[:, h, j:j + 1], axis=0)
                                                    ).then_inc(pz["gathered"][h], 16)

            gather_pass(0, xu_tab, UW, xu_stored, 16)
            gather_pass(1, x_tabs[0], H, rows_stored, 16)
            gather_pass(2, x_tabs[1], H, rows_stored, 32)
            pool.wait_ge(tabs_zeroed, 16 * NTAB)

            def scatter(g):
                for h in range(2):
                    pool.wait_ge(sidx_made[h], g + 1)
                    pool.wait_ge(smm_taken, g * 2 + h + 1)
                    for j in range(HT):
                        s = h * HT + j
                        wait(pool, scattered[s % NTAB], scatters_before(s, g) * 16)
                        pool.sem_inc(pool_turn, 1)
                        pool.indirect_dma_start(sums[s % NTAB], bass.IndirectOffsetOnAxis(ap=sidx[h].bitcast(U32)[:, j:j + 1], axis=0),
                                                smm[h][:, j, :], None, compute_op=ALU.add).then_inc(scattered[s % NTAB], 16)
            scatter(0)
            with pool.Fori(1, LOOPS) as g:
                scatter(g)
            gather_pass(3, x_tabs[2], H, rows_stored, 48)

        @block.scalar
        def _(act):
            def sqrt_step(n):
                act.wait_ge(sqrt_in, n)
                nc.scalar.activation(st[:, 2, :], st[:, 1, :], ACT.Sqrt).then_inc(sqrt_out, 1)

            def stage(k):
                pz = passes[k]
                with act.Fori(0, LOOPS) as g:
                    for h in range(2):
                        act.wait_ge(pz["used"][h], g + 1)
                        nc.scalar.copy(idx_st.bitcast(I32)[:, h, :], src_i[:, bass.ds(g * (2 * HT) + h * HT, HT)]).then_inc(pz["idx_ready"][h], 1)

            def conv(m, K):
                for b in range(13):
                    n = min(4, NT - 4 * b)
                    act.wait_ge(cat_turned, 13 * m + b + 1)
                    nc.scalar.copy(cat_t[0:K, 4 * b:4 * b + n, :].rearrange("p a b -> p (a b)"),
                                   ps[0:K, 512 * (b % 3):512 * (b % 3) + n * P]).then_inc(cat_taken, 1)

            act.wait_ge(shifted, 1)
            nc.scalar.activation(rst_b, mx_b, ACT.Exp).then_inc(exp_made, 1)
            act.wait_ge(cos_arg, 1)
            nc.scalar.activation(tmp_c, tmp_c, ACT.Sin, scale=-PI / CUTOFF, bias=half_pi[:, :]).then_inc(cos_made, 1)
            act.wait_ge(ex_taken, 1)
            stage(0)
            act.wait_ge(elu_in, 1)
            nc.scalar.activation(tb, tb, ACT.Exp).then_inc(elu_out, 1)
            sqrt_step(1)
            act.wait_ge(rows_made, 1)
            stage(1)
            conv(0, 2 * H + 1)
            act.wait_ge(rows_made, 2)
            stage(2)
            conv(1, 2 * H + 1)
            sqrt_step(2)
            act.wait_ge(s1_ones, 1)
            act.wait_ge(hmv_made, 1)

            def take_sums(g, h):
                act.wait_ge(summed[h], g + 1)
                for k in range(NTAB):
                    wait(act, scattered[k], scatters_through(k, h, g - 1) * 16 if not (isinstance(g, int) and g == 0) else 0)
                for i, (k0, n, v) in enumerate(sum_runs):
                    ins = nc.scalar.copy(smm[h][:, k0:k0 + n, :], v)
                ins.then_inc(smm_taken, 1)

            def third(g, first=False):
                for h in range(2):
                    act.wait_ge(picked[h], g + 1)
                    last_messages(act, g, h)
                    for k0, n, v in pick_runs:
                        ins = nc.scalar.copy(hg[:, k0:k0 + n, :], v)
                    ins.then_inc(hg_taken, 1)
                    wait(act, gate_mm[h], g)
                    for c in range(4):
                        act.wait_ge(z_mm, g * 8 + (4 * h + c + 1))
                        nc.scalar.activation(s1t[h][0:H, c * CH:(c + 1) * CH], z_ps[c][0:H, :], ACT.Silu, bias=b1c[:, 0:1]).then_inc(silu_done, 1)
                    if h == 1:
                        take_sums(g, 0)
                    elif not first:
                        take_sums(g - 1, 1)

            third(0, first=True)
            with act.Fori(1, LOOPS) as g:
                third(g)
            take_sums(LOOPS - 1, 1)
            sqrt_step(3)
            sqrt_step(4)
            act.wait_ge(cat_made, 3)
            conv(2, H)
            sqrt_step(5)
            act.wait_ge(rows_made, 3)
            stage(3)
            sqrt_step(6)

        @block.tensor
        def _(pe):
            pe.wait_ge(wts_loaded, 16 * 17)
            nc.tensor.matmul(ps[0:NEL, 7 * 512:7 * 512 + G], embt[:, :], adt[:, :], start=True, stop=True).then_inc(ev_mm, 1)
            pe.wait_ge(ev_made, 1)
            pe.wait_ge(ohz_made, 1)
            for i in range(NT):
                ins = nc.tensor.matmul(ps[:, i * AS:(i + 1) * AS], ohz[:, i * P:(i + 1) * P], ev[:, :], start=True, stop=True)
            ins.then_inc(uv_mm, 1)
            pe.wait_ge(carry_out, 1)
            for c in range(4):
                ins = nc.tensor.transpose(ps[0:1, 7 * 512 + c * Q:7 * 512 + (c + 1) * Q], carry[:, c:c + 1], ident[0:Q, 0:Q])
            ins.then_inc(carry_rows, 1)
            pe.wait_ge(carry_scanned, 1)
            for c in range(2):
                ins = nc.tensor.transpose(ps[0:Q, 7 * 512 + 4 * Q + 4 * c:7 * 512 + 4 * Q + 4 * c + 1], cscan[0:1, c, :], ident[0:1, 0:1])
            ins.then_inc(carry_back, 1)
            pe.wait_ge(exp_made, 1)
            pe.wait_ge(uv_taken, 1)
            for b in range(HT):
                ins = nc.tensor.transpose(ps[:, b * P:b * P + Q], rst_b[:, b * P:(b + 1) * P], ident[0:Q, 0:Q])
            ins.then_inc(ex_turned, 1)

            def scatter_pass(k):
                pz = passes[k]
                pe.wait_ge(acc_free, k + 1)
                for b in range(7):
                    nc.tensor.matmul(ps[:, b * 512:(b + 1) * 512], zero[:, 0:P], zero[:, :], start=True, stop=False,
                                     skip_group_check=True)
                for h in range(2):
                    pe.sem_inc(pz["used"][h], 1)
                with pe.Fori(0, LOOPS) as g:
                    for h in range(2):
                        pe.wait_ge(pz["oh_ready"][h], g + 1)
                        pe.wait_ge(pz["gathered"][h], (g + 1) * (16 * HT))
                        for j in range(HT):
                            c = pe.value_load(pcol[0:1, bass.ds(g * (2 * HT) + (h * HT + j), 1)], min_val=0, max_val=(NT - 1) * AS)
                            o = oh[:, h * HT + j, :]
                            nc.tensor.matmul(ps[:, bass.ds(c, H + 1)], o[:, 0:P], G_ring[:, h, j, 0:H + 1], start=False, stop=False,
                                             skip_group_check=True)
                            ins = nc.tensor.matmul(ps[:, bass.ds(c + AS, H + 1)], o[:, P:2 * P], G_ring[:, h, j, 0:H + 1],
                                                   start=False, stop=False, skip_group_check=True)
                        ins.then_inc(pz["used"][h], 1)
                pe.wait_ge(pz["used"][1], LOOPS + 1)
                pe.nop().then_inc(acc_done, 1)

            def conv(m, source, K, rhs):
                pe.wait_ge(cat_made, m + 1)
                for b in range(13 + 1):
                    if b < 13:
                        if b >= 3:
                            pe.wait_ge(cat_taken, 13 * m + b - 2)
                        for i in range(4 * b, min(4 * b + 4, NT)):
                            c = 512 * (b % 3) + (i % 4) * P
                            ins = nc.tensor.transpose(ps[0:K, c:c + P], source[:, i, :], ident[:, :])
                        ins.then_inc(cat_turned, 1)
                    if b >= 1:
                        pe.wait_ge(cat_taken, 13 * m + b)
                        for i in range(4 * b - 4, min(4 * b, NT)):
                            ins = nc.tensor.matmul(conv_ps[i // 10][:, i % 10, :], cat_t[0:K, i, :], rhs, start=True, stop=True)
                ins.then_inc(conv_done, 1)

            scatter_pass(0)
            scatter_pass(1)
            conv(0, cat, 2 * H + 1, wcat[0:2 * H + 1, 0, :])
            scatter_pass(2)
            conv(1, cat, 2 * H + 1, wcat[0:2 * H + 1, 1, :])

            def first_product(g, h):
                pe.wait_ge(e_in[h], (g + 1) * 64)
                last_messages(pe, g, h)
                for c in range(4):
                    wait(pe, silu_done, g * 8 + (4 * h + max(c - 2, 0)))
                    ins = nc.tensor.matmul(z_ps[c], w1t[:, :], attr_s[h][:, c * CH:(c + 1) * CH], start=True, stop=True)
                    ins.then_inc(z_mm, 1)
                pe.wait_ge(z_mm, g * 8 + (4 * h + 4))
                pe.nop().then_inc(z_used[h], 1)

            def pick(g, h):
                pe.wait_ge(oht_made[h], g + 1)
                wait(pe, hg_taken, g * 2 + h)
                for j in range(HT):
                    c = pe.value_load(hcol[0:1, bass.ds(g * (2 * HT) + (h * HT + j), 1)], min_val=0, max_val=(NT - 1) * UW)
                    hm = HMV_flat
                    nc.tensor.matmul(slot(pick_runs, j), oh_t[h][:, 0, j * P:(j + 1) * P], hm[:, bass.ds(c, UW)], start=True, stop=False)
                    ins = nc.tensor.matmul(slot(pick_runs, j), oh_t[h][:, 1, j * P:(j + 1) * P], hm[:, bass.ds(c + UW, UW)],
                                           start=False, stop=True)
                ins.then_inc(picked[h], 1)

            def combine(g, h):
                pe.wait_ge(msg_made[h], g + 1)
                pe.wait_ge(eq_made[h], g + 1)
                wait(pe, smm_taken, g * 2 + h)
                for j in range(HT):
                    ins = nc.tensor.matmul(slot(sum_runs, j), eq[h][:, j, :], msg[h][:, j, :], start=True, stop=True)
                ins.then_inc(summed[h], 1)

            def gates(g, h):
                pe.wait_ge(silu_done, g * 8 + (4 * h + 4))
                for j in range(HT):
                    ins = nc.tensor.matmul(slot(gate_runs, j), s1t[h][0:H + 1, j * P:(j + 1) * P], w2b[0:H + 1, :], start=True, stop=True)
                ins.then_inc(gate_mm[h], 1)

            def third(g, first=False):
                for h in range(2):
                    pick(g, h)
                    if h == 1:
                        combine(g, 0)
                    elif not first:
                        combine(g - 1, 1)
                    first_product(g, h)
                    gates(g, h)

            pe.wait_ge(hmv_made, 1)
            third(0, first=True)
            with pe.Fori(1, LOOPS) as g:
                third(g)
            combine(LOOPS - 1, 1)
            conv(2, X, H, w3s[:, :])
            scatter_pass(3)

        @block.vector
        def _(dve):
            V = nc.vector
            n_step = [0]

            def step(ins):
                n_step[0] += 1
                ins.then_inc(dve_step, 1)
                dve.wait_ge(dve_step, n_step[0])

            def tt(o, x, y, op):
                step(V.tensor_tensor(o, x, y, op))

            def ts(o, x, s1, op0, s2=None, op1=None):
                step(V.tensor_scalar(o, x, s1, s2, op0, op1) if op1 is not None else V.tensor_scalar(o, x, s1, None, op0))

            step(V.memset(zero[:, :], 0.0))
            step(V.memset(HMV[:, NT, :], 0.0))
            step(V.memset(w1t[:, :], 0.0))
            step(V.memset(wide_neg[:, :], -1.0))
            step(V.tensor_copy(prev_i[:, :], wide_neg[:, 0:1]))
            V.tensor_copy(next_i[:, :], wide_neg[:, 1:2]).then_inc(edges_init, 1)
            step(V.memset(half_pi[:, :], PI / 2))
            dve.wait_ge(consts_made, 2)
            step(V.tensor_copy(iota_f[:, :], iota_i[:, :]))
            step(V.tensor_copy(iota_p[:, :], ip_i[:, :]))
            ts(dump_i[:, :], iota_p[:, 0:1], float(NP), ALU.add)
            ts(ident[:, :], iota_f[:, 0:P], iota_p[:, 0:1], ALU.is_equal)
            ts(lower[:, :], iota_f[:, 0:P], iota_p[:, 0:1], ALU.is_lt)
            dve.wait_ge(prep_loaded, 16 * 9)
            V.tensor_scalar(ohz, z_b.bitcast(I32), iota_p[0:NEL, 0:1], None, ALU.is_equal).then_inc(ohz_made, 1)
            dve.wait_ge(ev_mm, 1)
            V.tensor_copy(ev[:, G:2 * G], ps[0:NEL, 7 * 512:7 * 512 + G]).then_inc(ev_made, 1)
            bi = base_i.bitcast(I32)
            ts(bi, bi, -P, ALU.bitwise_and)
            tt(rel_c[:, :], dc_i.bitcast(I32), bi, ALU.subtract)
            ts(pcol[:, :], bi[0:1, :], AS / P, ALU.mult)
            ts(hcol[:, :], bi[0:1, :], UW / P, ALU.mult)
            dri = dr_i.bitcast(I32)
            ts(base_r[:, :], dri.rearrange("q (b e) -> q b e", e=P)[:, :, 0], -P, ALU.bitwise_and)
            V.tensor_tensor(rst_f.rearrange("q (b e) -> q b e", e=P), dri.rearrange("q (b e) -> q b e", e=P),
                            bc(base_r[:, :], P), ALU.subtract).then_inc(rel_rows_made, 1)
            step(V.tensor_copy(dr_f, dri))
            dve.wait_ge(edge_ends, 32)
            step(V.tensor_copy(prev_f[:, :], prev_i[:, :]))
            step(V.tensor_copy(next_f[:, :], next_i[:, :]))
            step(V.memset(rst_b, -BIG))
            tt(rst_b[:, 0:W - 1], dr_f[:, 0:W - 1], dr_f[:, 1:W], ALU.not_equal)
            ts(rst_b[:, 0:W - 1], rst_b[:, 0:W - 1], -BIG, ALU.mult)
            dve.wait_ge(rel_stored, 16)
            step(V.memset(rst_f, -BIG))
            step(V.tensor_copy(rst_f[:, 1:W], rst_b[:, 0:W - 1]))
            step(V.tensor_tensor_scan(mx_f, rst_f, e1_s, -BIG, ALU.add, ALU.max))
            step(V.tensor_tensor_scan(mx_b[:, ::-1], rst_b[:, ::-1], e1_s[:, ::-1], -BIG, ALU.add, ALU.max))
            d0, d1 = dr_f[:, 0:1], dr_f[:, W - 1:W]
            tt(pen[:, 0:1], prev_f[:, :], d0, ALU.not_equal)
            tt(pen[:, 1:2], next_f[:, :], d1, ALU.not_equal)
            tt(pen[:, 2:3], d0, d1, ALU.not_equal)
            ts(pen[:, :], pen[:, :], -BIG, ALU.mult)
            step(V.tensor_copy(carry[:, 0:1], mx_f[:, W - 1:W]))
            tt(carry[:, 1:2], pen[:, 0:1], pen[:, 2:3], ALU.add)
            step(V.tensor_copy(carry[:, 2:3], mx_b[:, 0:1]))
            V.tensor_tensor(carry[:, 3:4], pen[:, 1:2], pen[:, 2:3], ALU.add).then_inc(carry_out, 1)
            dve.wait_ge(carry_rows, 1)
            step(V.tensor_copy(crow[:, :, :], ps[0:1, 7 * 512:7 * 512 + 4 * Q].rearrange("p (a b) -> p a b", b=Q)))
            step(V.memset(cscan[:, :, :], -BIG))
            step(V.tensor_tensor_scan(cst[:, 0, :], crow[:, 1, :], crow[:, 0, :], -BIG, ALU.add, ALU.max))
            step(V.tensor_tensor_scan(cst[:, 1, ::-1], crow[:, 3, ::-1], crow[:, 2, ::-1], -BIG, ALU.add, ALU.max))
            step(V.tensor_copy(cscan[:, 0, 1:Q], cst[:, 0, 0:Q - 1]))
            V.tensor_copy(cscan[:, 1, 0:Q - 1], cst[:, 1, 1:Q]).then_inc(carry_scanned, 1)
            dve.wait_ge(carry_back, 1)
            for c in range(2):
                tt(cin[:, c:c + 1], ps[0:Q, 7 * 512 + 4 * Q + 4 * c:7 * 512 + 4 * Q + 4 * c + 1], pen[:, c:c + 1], ALU.add)
            tt(mx_f, mx_f, mx_b, ALU.max)
            for c, d in ((0, d0), (1, d1)):
                ts(mx_b, dr_f, d, ALU.not_equal, -BIG, ALU.mult)
                step(V.scalar_tensor_tensor(out=mx_f, in0=mx_b, scalar=cin[:, c:c + 1], in1=mx_f, op0=ALU.add, op1=ALU.max))
            V.tensor_tensor(mx_b, e1_s, mx_f, ALU.subtract).then_inc(shifted, 1)
            ts(dc_i.bitcast(I32), cw_c[:, :], 0.5 / CUTOFF, ALU.mult)
            step(V.scalar_tensor_tensor(out=tmp_c, in0=dc_i.bitcast(I32), scalar=-2 * CUTOFF, in1=cw_c[:, :], op0=ALU.mult, op1=ALU.add))
            step(V.scalar_tensor_tensor(out=tmp_c, in0=tmp_c, scalar=-1.0, in1=tmp_c, op0=ALU.mult, op1=ALU.max))
            ts(tmp_c, tmp_c, -CUTOFF, ALU.add)
            V.scalar_tensor_tensor(out=tmp_c, in0=tmp_c, scalar=-1.0, in1=tmp_c, op0=ALU.mult, op1=ALU.max).then_inc(cos_arg, 1)
            dve.wait_ge(cos_made, 1)
            ts(tmp_c, tmp_c, -0.5, ALU.mult, 0.5, ALU.add)
            step(V.scalar_tensor_tensor(out=cw_c[:, :], in0=cw_c[:, :], scalar=CUTOFF, in1=tmp_c, op0=ALU.is_lt, op1=ALU.mult))
            dve.wait_ge(uv_mm, 1)
            step(V.tensor_copy(xu[:, :, H + 1:UW], acc[:, :, 0:G]))
            V.tensor_copy(HMV[:, 0:NT, H + 1:UW], acc[:, :, G:2 * G]).then_inc(uv_taken, 1)
            step(V.tensor_copy(xu[:, :, 0:H], X[:, :, :]))
            V.memset(xu[:, :, H:H + 1], 1.0).then_inc(xu_made, 1)
            dve.wait_ge(ex_turned, 1)
            step(V.tensor_copy(ex_c[:, :].rearrange("p (q b) -> p b q", b=HT),
                               ps[:, 0:HT * P].rearrange("p (b q) -> p b q", q=P)[:, :, 0:Q]))
            V.memset(idx_st.rearrange("p a b -> p (a b)"), 0.0).then_inc(ex_taken, 1)
            dve.wait_ge(xu_stored, 16)
            V.engine_nop().then_inc(acc_free, 1)

            def one_hots(k):
                pz = passes[k]
                rows = bm(iota_f[:, :], HT)
                with dve.Fori(0, LOOPS) as g:
                    for h in range(2):
                        t0 = g * (2 * HT) + h * HT
                        dve.wait_ge(pz["used"][h], g + 1)
                        o = oh[:, h * HT:(h + 1) * HT, :]
                        ins = V.tensor_tensor(o, rows, bc(rel_c[:, bass.ds(t0, HT)], 2 * P), ALU.is_equal)
                        if k == 0:
                            ins.then_inc(oh_plain, 1)
                            dve.wait_ge(oh_plain, g * 2 + h + 1)
                            ins = V.tensor_tensor(o, o, bc(ex_c[:, bass.ds(t0, HT)], 2 * P), ALU.mult)
                        ins.then_inc(pz["oh_ready"][h], 1)

            n_norm = [0]

            def layernorm(v, o, sq, gain=None, shift=None):
                n_norm[0] += 1
                step(V.tensor_reduce(st[:, 0, :], v, AX.X, ALU.add))
                ts(st[:, 0, :], st[:, 0, :], -1.0 / H, ALU.mult)
                tt(v, v, bc(st[:, 0, :], H), ALU.add)
                tt(sq, v, v, ALU.mult)
                step(V.tensor_reduce(st[:, 1, :], sq, AX.X, ALU.add))
                V.tensor_scalar(st[:, 1, :], st[:, 1, :], 1.0 / H, EPS, ALU.mult, ALU.add).then_inc(sqrt_in, 1)
                dve.wait_ge(sqrt_out, n_norm[0])
                step(V.reciprocal(st[:, 3, :], st[:, 2, :]))
                tt(o, v, bc(st[:, 3, :], H), ALU.mult)
                if gain is not None:
                    tt(o, o, bm(gain, NT), ALU.mult)
                    tt(o, o, bm(shift, NT), ALU.add)

            def conv_out():
                for a, b in ((0, 5), ):
                    pass

            one_hots(0)
            dve.wait_ge(acc_done, 1)
            step(V.tensor_copy(agg, acc[:, :, 0:H + 1]))
            ts(st[:, 4, :], agg[:, :, H], 1e-30, ALU.max)
            step(V.reciprocal(st[:, 5, :], st[:, 4, :]))
            tt(ta, agg[:, :, 0:H], bc(st[:, 5, :], H), ALU.mult)
            V.tensor_scalar(tb, ta, 0.0, None, ALU.min).then_inc(elu_in, 1)
            dve.wait_ge(elu_in, 1)
            ts(ta, ta, 0.0, ALU.max)
            dve.wait_ge(elu_out, 1)
            step(V.scalar_tensor_tensor(out=ta, in0=tb, scalar=-1.0, in1=ta, op0=ALU.add, op1=ALU.add))
            tt(ta, ta, X[:, :, :], ALU.add)
            layernorm(ta, X[:, :, :], tb)
            dve.wait_ge(u_stored[0], 16 * LOOPS)
            dve.wait_ge(u_stored[1], 16 * LOOPS)
            step(V.memset(G_ring[:, :, :, H:H + 1].rearrange("p a b c -> p a (b c)"), 1.0))
            V.engine_nop().then_inc(acc_free, 1)
            V.engine_nop().then_inc(rows_made, 1)

            def make_cat(first):
                dve.wait_ge(acc_done, 2 if first else 3)
                step(V.tensor_copy(cat[:, :, 0:H], acc[:, :, 0:H]))
                if first:
                    ts(deg[:, :], acc[:, :, H], 1.0, ALU.add)
                step(V.tensor_copy(cat[:, :, H:2 * H], (X if first else HN)[:, :, :]))
                V.memset(cat[:, :, 2 * H:2 * H + 1], 1.0).then_inc(cat_made, 1)

            one_hots(1)
            make_cat(True)
            dve.wait_ge(conv_done, 1)
            for b in range(5):
                n = min(10, NT - 10 * b)
                ts(HN[:, 10 * b:10 * b + n, :], conv_ps[b][:, 0:n, :], 0.0, ALU.max)
            step(V.memset(G_ring[:, :, :, H:H + 1].rearrange("p a b c -> p a (b c)"), 1.0))
            V.engine_nop().then_inc(rows_made, 1)
            V.engine_nop().then_inc(acc_free, 1)
            one_hots(2)
            make_cat(False)
            dve.wait_ge(conv_done, 2)
            for b in range(5):
                n = min(10, NT - 10 * b)
                tt(ta[:, 10 * b:10 * b + n, :], conv_ps[b][:, 0:n, :], X[:, 10 * b:10 * b + n, :], ALU.add)
            layernorm(ta, X[:, :, :], tb)
            step(V.memset(zt, 0.0))
            V.engine_nop().then_inc(zeros_made, 1)
            dve.wait_ge(tabs_zeroed, 16 * NTAB)
            tt(HMV[:, 0:NT, 0:H], X[:, :, :], bc(nv[:, :], H), ALU.mult)
            step(V.tensor_copy(HMV[:, 0:NT, H], nv[:, :]))
            step(V.memset(s1t[0], 1.0))
            V.memset(s1t[1], 1.0).then_inc(s1_ones, 1)
            V.engine_nop().then_inc(hmv_made, 1)

            def own(s, v):
                dve.wait_ge(s, v)

            def turned_one_hots(g, h):
                dve.wait_ge(e_in[h], (g + 1) * 64)
                wait(dve, picked[h], g)
                V.tensor_scalar(oh_t[h][:, 0, :], rel_b[h], iota_p[:, 0:1], None, ALU.is_equal)
                V.tensor_scalar(oh_t[h][:, 1, :], rel_b[h], iota_p[:, 1:2], None, ALU.is_equal).then_inc(oht_made[h], 1)

            def equals(g, h):
                n = g * 2 + h
                t0 = g * (2 * HT) + h * HT
                dve.wait_ge(e_in[h], (g + 1) * 64)
                wait(dve, summed[h], g)
                V.tensor_tensor(eq[h], src_b[h].bitcast(I32), bc(src_i[:, bass.ds(t0, HT)], P), ALU.is_equal).then_inc(eq_made[h], 1)
                own(eq_made[h], g + 1)
                V.tensor_tensor(eql, eq[h], bm(lower[:, :], HT), ALU.mult).then_inc(eq_step, 1)
                V.tensor_copy(srcf, src_i[:, bass.ds(t0, HT)]).then_inc(eq_step, 1)
                own(eq_step, n * 5 + 2)
                V.tensor_reduce(first, eql, AX.X, ALU.add).then_inc(eq_step, 1)
                V.tensor_scalar(diff, srcf, -1.0, dump_i[:, 0:1], ALU.mult, ALU.add).then_inc(eq_step, 1)
                own(eq_step, n * 5 + 4)
                V.scalar_tensor_tensor(out=diff2, in0=first, scalar=0.0, in1=diff, op0=ALU.is_gt, op1=ALU.mult).then_inc(eq_step, 1)
                own(eq_step, n * 5 + 5)
                if not (isinstance(g, int) and g == 0):
                    for k in range(NTAB):
                        dve.wait_ge(scattered[k], scatters_through(k, h, g - 1) * 16)
                V.tensor_tensor(sidx[h].bitcast(I32), diff2, srcf, ALU.add).then_inc(sidx_made[h], 1)

            def messages(g, h):
                n = g * 2 + h
                t0 = g * (2 * HT) + h * HT
                dve.wait_ge(hg_taken, n + 1)
                dve.wait_ge(gate_mm[h], g + 1)
                wait(dve, summed[h], g)
                m = msg[h]
                V.tensor_tensor(uv, u_s[h], hg[:, :, H + 1:UW], ALU.mult).then_inc(msg_step, 1)
                own(msg_step, n * 5 + 1)
                V.tensor_reduce(adp, uv, AX.X, ALU.add).then_inc(msg_step, 1)
                own(msg_step, n * 5 + 2)
                for k0, c, v in gate_runs:
                    V.tensor_tensor(m[:, k0:k0 + c, 0:H], v, bc(adp[:, k0:k0 + c], H), ALU.add).then_inc(msg_step, 1)
                own(msg_step, n * 5 + 4)
                V.tensor_tensor(m[:, :, 0:H], m[:, :, 0:H], hg[:, :, 0:H], ALU.mult).then_inc(msg_step, 1)
                V.tensor_copy(m[:, :, H], hg[:, :, H])
                own(msg_step, n * 5 + 5)
                V.tensor_tensor(m[:, :, 0:H], m[:, :, 0:H], bc(cw_c[:, bass.ds(t0, HT)], H), ALU.mult).then_inc(msg_made[h], 1)

            def third(g, first=False, last=False):
                for h in range(2):
                    if h == 1:
                        messages(g, 0)
                        if not last:
                            turned_one_hots(g + 1, 0)
                    else:
                        if not first:
                            messages(g - 1, 1)
                        turned_one_hots(g, 1)
                    equals(g, h)

            turned_one_hots(0, 0)
            third(0, first=True)
            with dve.Fori(1, LOOPS - 1) as g:
                third(g)
            third(LOOPS - 1, last=True)
            messages(LOOPS - 1, 1)
            for k in range(NTAB):
                dve.wait_ge(sums_in[k % 2], 16 * (k // 2 + 1))
                if k == 0:
                    V.tensor_copy(agg, ld[0]).then_inc(sums_added, 1)
                else:
                    V.tensor_tensor(agg, agg, ld[k % 2], ALU.add).then_inc(sums_added, 1)
                dve.wait_ge(sums_added, k + 1)
            ts(st[:, 4, :], agg[:, :, H], 1e-8, ALU.max)
            step(V.reciprocal(st[:, 5, :], st[:, 4, :]))
            tt(ta, agg[:, :, 0:H], bc(st[:, 5, :], H), ALU.mult)
            tt(ta, ta, X[:, :, :], ALU.add)
            layernorm(ta, tb, tc, gam[:, :], bet[:, :])
            tt(ta, tb, X[:, :, :], ALU.add)
            layernorm(ta, X[:, :, :], tb)
            V.engine_nop().then_inc(cat_made, 1)
            V.tensor_copy(st[:, 1, :], deg[:, :]).then_inc(sqrt_in, 1)
            n_norm[0] += 1
            dve.wait_ge(sqrt_out, n_norm[0])
            step(V.reciprocal(dinv[:, :], st[:, 2, :]))
            dve.wait_ge(conv_done, 3)
            for b in range(5):
                n = min(10, NT - 10 * b)
                tt(HN[:, 10 * b:10 * b + n, :], conv_ps[b][:, 0:n, :], bc(dinv[:, 10 * b:10 * b + n], H), ALU.mult)
            step(V.memset(G_ring[:, :, :, H:H + 1].rearrange("p a b c -> p a (b c)"), 1.0))
            V.engine_nop().then_inc(rows_made, 1)
            V.engine_nop().then_inc(acc_free, 1)
            one_hots(3)
            dve.wait_ge(acc_done, 4)
            tt(ta, acc[:, :, 0:H], HN[:, :, :], ALU.add)
            tt(ta, ta, bc(dinv[:, :], H), ALU.mult)
            tt(ta, ta, bm(b3b[:, :], NT), ALU.add)
            tt(ta, ta, X[:, :, :], ALU.add)
            layernorm(ta, X[:, :, :], tb)
            V.engine_nop().then_inc(out_made, 1)


_INS = ["x_n", "dst_r", "dst_c", "src_c", "src_f", "e1_r", "ew_c", "attr_t", "z_f", "nv_n",
        "emb_t", "emb", "adapt_t", "w_rel1", "w_root1", "b1", "w_rel2", "w_root2", "b2",
        "m_w1t", "m_b1", "m_w2t", "m_b2", "gamma", "beta", "w3", "b3"]


def kernel(**inputs):
    import numpy as _np
    import concourse.bacc as _bacc
    from concourse import mybir as _mybir
    from concourse.bass_utils import run_bass_kernel_spmd as _run

    def arr(name):
        return _np.asarray(inputs[name])

    def pad(a, n, fill=0):
        return _np.concatenate([a, _np.full((n - a.shape[0],) + a.shape[1:], fill, a.dtype)])

    dst, src = pad(arr("dst"), EP, PADN), pad(arr("src"), EP, PADN)
    lay = {
        "x_n": pad(arr("x"), NP).reshape(NT, P, H).transpose(1, 0, 2),
        "dst_r": dst.reshape(Q, W), "dst_c": dst.reshape(T, P).T, "src_c": src.reshape(T, P).T,
        "src_f": src,
        "e1_r": pad(arr("edge_weight1")[:, 0], EP).reshape(Q, W),
        "ew_c": pad(arr("edge_weight"), EP).reshape(T, P).T,
        "attr_t": pad(arr("edge_attr_40"), EP).T,
        "z_f": pad(arr("node_type_119"), NP), "nv_n": pad(arr("node_vec"), NP).reshape(NT, P).T,
        "emb_t": arr("L2_gnn_emb").T, "emb": arr("L2_gnn_emb"), "adapt_t": arr("L2_gnn_adaptW").T,
        "w_rel1": arr("L1_gnn_w_rel1"), "w_root1": arr("L1_gnn_w_root1"), "b1": arr("L1_gnn_b1"),
        "w_rel2": arr("L1_gnn_w_rel2"), "w_root2": arr("L1_gnn_w_root2"), "b2": arr("L1_gnn_b2"),
        "m_w1t": arr("L2_gnn_W1").T, "m_b1": arr("L2_gnn_b1"), "m_w2t": arr("L2_gnn_W2").T,
        "m_b2": arr("L2_gnn_b2"), "gamma": arr("L2_gnn_gamma"), "beta": arr("L2_gnn_beta"),
        "w3": arr("L3_gnn_W"), "b3": arr("L3_gnn_b"),
    }
    nc = _bacc.Bacc("TRN2", target_bir_lowering=False, num_devices=1)
    arrays, args = {}, []
    for name in _INS:
        a = _np.ascontiguousarray(lay[name])
        arrays[f"in_{name}_dram"] = a
        args.append(nc.dram_tensor(f"in_{name}_dram", a.shape, _mybir.dt.from_np(a.dtype), kind="ExternalInput").ap())
    args.append(nc.dram_tensor("out_0_dram", (N, H), _mybir.dt.float32, kind="ExternalOutput").ap())
    build(nc, *args)
    r = _run(nc, [arrays], core_ids=[0])
    return r.results[0]["out_0_dram"]
```

```python
from contextlib import ExitStack

import concourse.bass as bass
from concourse import mybir

F32 = mybir.dt.float32
I32 = mybir.dt.int32
U32 = mybir.dt.uint32
BF16 = mybir.dt.bfloat16
F16 = mybir.dt.float16
ALU = mybir.AluOpType
ACT = mybir.ActivationFunctionType
AX = mybir.AxisListType

P = 128
H = 48
N = 6250
NT = -(-N // P)
NP = NT * P
E = 206250
HT = 13
LOOPS = 62
T = 2 * HT * LOOPS
EP = T * P
Q = 124
W = EP // Q
HE = HT * P
NEL = 119
G = 32
R = 40
CUTOFF = 6.0
EPS = 1e-5
BIG = 1e30
NTAB = 5
TROWS = NP + P
UW = H + 1 + G
DW = 10
DH = 64
AR = DH + DW - 1
WN = DW * NT
AB = 4
AW = H + 2
PADN = NP - 1
PT = 7
PC = PT * P
LN3 = 1.0986122886681098
PI = 3.141592653589793


def build(nc, x_n, dst_r, dst_c, src_c, src_f,  e1_r, ew_c, attr_t, z_f, nv_n,
          emb_t, emb, adapt_t, w_rel1, w_root1, b1, w_rel2, w_root2, b2,
          m_w1t, m_b1, m_w2t, m_b2, gamma, beta, w3, b3, out):
    xu_tab = nc.dram_tensor("xu_tab", [NP, UW], F32).ap()
    u_edges = nc.dram_tensor("u_edges", [2 * LOOPS, P, HT * G], F32).ap()
    adj = nc.dram_tensor("adj", [P, (NP + DH) * NT], BF16).ap()
    rel_f = nc.dram_tensor("rel_f", [Q, W], BF16).ap()
    sums = [nc.dram_tensor(f"sums{k}", [TROWS, H + 1], F32).ap() for k in range(NTAB)]

    with ExitStack() as ctx:
        def sb(name, shape, dt=F32):
            return ctx.enter_context(nc.sbuf_tensor(name, shape, dt))

        def sem(name):
            return ctx.enter_context(nc.semaphore(name))

        X = sb("X", [P, NT, H])
        HN = sb("HN", [P, NT, H])
        HMV = sb("HMV", [P, NT + 1, 3, UW], BF16)
        ACC = sb("ACC", [P, NT + 1, AW])
        rel_c = sb("rel_c", [P, T])
        ex_c = sb("ex_c", [P, T])
        cw_c = sb("cw_c", [P, T])
        src_i = sb("src_i", [P, T + HT], I32)
        hoff = sb("hoff", [1, Q], I32)
        coff = sb("coff", [1, Q], I32)
        acol = sb("acol", [1, Q], I32)
        hcol = sb("hcol", [1, Q + 1], I32)
        deg = sb("deg", [P, NT])
        dinv = sb("dinv", [P, NT])
        nv = sb("nv", [P, NT])
        iota_f = sb("iota_f", [P, 2 * P])
        iota_p = sb("iota_p", [P, 2])
        dump_i = sb("dump_i", [P, 1])
        ident = sb("ident", [P, P])
        ident_b = sb("ident_b", [P, P], BF16)
        zero = sb("zero", [P, 512])
        iota_b = sb("iota_b", [P, 2 * P], BF16)
        rank_w = sb("rank_w", [P, 2])
        rank_b = sb("rank_b", [P, 1], BF16)
        rank_c = sb("rank_c", [P, 1])
        wcat = sb("wcat", [P, 2, H])
        w1t = sb("w1t", [2 * R, 2 * H])
        b1c = sb("b1c", [2 * H, 1])
        w2b = sb("w2b", [2 * H + 1, 2 * H])
        w3s = sb("w3s", [H, H])
        b3b = sb("b3b", [P, H])
        gam = sb("gam", [P, H])
        bet = sb("bet", [P, H])
        st = sb("st", [P, 6, NT])
        iota_i = sb("iota_i", [P, 2 * P], I32)
        ip_i = sb("ip_i", [P, 2], I32)
        ev = sb("ev", [NEL, 2 * G])
        embt = sb("embt", [G, NEL])
        adt = sb("adt", [G, G])
        half_pi = sb("half_pi", [P, 1])
        wide_neg = sb("wide_neg", [Q, 2])
        prev_i = sb("prev_i", [Q, 1], I32)
        next_i = sb("next_i", [Q, 1], I32)
        prev_f = sb("prev_f", [Q, 1])
        next_f = sb("next_f", [Q, 1])
        pen = sb("pen", [Q, 3])
        carry = sb("carry", [Q, 4])
        crow = sb("crow", [1, 4, Q])
        cst = sb("cst", [1, 2, Q])
        cscan = sb("cscan", [1, 2, Q])
        cin = sb("cin", [Q, 2])
        base_r = sb("base_r", [Q, 1], I32)
        base_c = sb("base_c", [P, Q], I32)
        rel_r = sb("rel_r", [Q, W], BF16)
        diff = sb("diff", [P, HT])[:, :]
        diff2 = sb("diff2", [P, HT])[:, :]
        ACC_flat = ACC[:, :, :].rearrange("p a b -> p (a b)")
        HMV_flat = HMV[:, :, :, :].rearrange("p a c b -> p (a c b)")
        WORK = 28290
        work = sb("work", [P, WORK])

        def carve(at, rows, *shape):
            n = 1
            for s in shape:
                n *= s
            assert at[0] + n <= WORK, (at[0] + n, WORK)
            v = work[0:rows, at[0]:at[0] + n]
            at[0] += n
            if len(shape) == 2:
                v = v.rearrange("p (a b) -> p a b", b=shape[1])
            if len(shape) == 3:
                v = v.rearrange("p (a b c) -> p a b c", b=shape[1], c=shape[2])
            return v

        ps = ctx.enter_context(nc.psum_tensor("ps", [P, 8 * 512], F32))

        a = [0]
        dr_i = carve(a, Q, W)
        dr_f = carve(a, Q, W)
        e1_s = carve(a, Q, W)
        rst_f = carve(a, Q, W)
        rst_b = carve(a, Q, W)
        mx_f = carve(a, Q, W)
        mx_b = carve(a, Q, W)
        v_rest = work[:, 0:NT * G].rearrange("p (a b) -> p a b", b=G)
        base_i = carve(a, P, T)
        dc_i = carve(a, P, T)
        tmp_c = ACC_flat[:, 0:T]
        ohz = carve(a, NEL, NP)
        z_b = ohz
        xu = carve([NT * G], P, NT, UW)
        prep_end = a[0]
        a = [0]
        a = [0]
        idx_st = carve(a, P, 2, HT)
        G_ring = carve(a, P, 2, HT, UW)
        G_parts = G_ring.bitcast(BF16)
        oh = carve(a, P, 2 * HT, P).bitcast(BF16)
        gw = [carve(a, P, HT, H + 1) for _ in range(2)]
        gw_r = carve(a, P, HT, H + 1)
        gw_p = [carve(a, P, HT, 74).bitcast(BF16) for _ in range(2)]
        fold_s = [carve(a, P, 2, AW) for _ in range(2)]
        win_s = carve(a, P, 2, HT)
        low_s = carve(a, P, 2, HT)
        iota_h = carve(a, P, WN // 2).bitcast(F16)
        win_oh = [carve(a, P, HT, WN // 2).bitcast(BF16) for _ in range(2)]
        low_oh = [carve(a, P, HT, P // 2).bitcast(BF16) for _ in range(2)]
        piece = [carve(a, P, AR * NT // 2 + 1).bitcast(BF16) for _ in range(2)]
        a = [max(a[0], prep_end)]
        win_c = carve(a, P, T + HT)
        low_c = carve(a, P, T + HT)
        toff = carve(a, 1, T).bitcast(I32)
        a = [0]
        attr_s = [carve(a, 2 * R, PC) for _ in range(2)]
        src_b = [carve(a, P, HT, P) for _ in range(2)]
        rel_b = [carve(a, P, HE // 2).bitcast(BF16) for _ in range(2)]
        oh_t = [carve(a, P, 2, HE // 2).bitcast(BF16) for _ in range(2)]
        hwin = [carve(a, P, 3 * UW).bitcast(BF16) for _ in range(2)]
        eq = [carve(a, P, HT, P // 2).bitcast(BF16) for _ in range(2)]
        s1t = [carve(a, 2 * H + 1, PC) for _ in range(2)]
        hg = carve(a, P, HT, UW)
        u_s = [carve(a, P, HT, G) for _ in range(2)]
        uv = carve(a, P, HT, G)
        adp = carve(a, P, HT)
        msg = carve(a, P, HT, H + 1)
        msg_r = carve(a, P, HT, H + 1)
        msg_p = [carve(a, P, HT, 74).bitcast(BF16) for _ in range(2)]
        smm = [carve(a, P, HT, H + 2) for _ in range(2)]
        first = carve(a, P, HT)
        srcf = carve(a, P, HT)
        sidx = [carve(a, P, HT) for _ in range(2)]
        a = [0]
        parts = carve(a, P, NT, 3 * H // 2).bitcast(BF16)
        cat = carve(a, P, NT, 2 * H + 1)
        cat_t = carve([a[0]], P, NT, P)
        t_at = [a[0]]
        ta = carve(t_at, P, NT, H)
        tb = carve(t_at, P, NT, H)
        a[0] += NT * P
        l_at = [a[0]]
        blocks = [carve(a, P, P * NT // 2).bitcast(BF16).rearrange("p (d a) -> p d a", a=NT) for _ in range(AB)]
        agg = carve(l_at, P, NT, H + 1)
        ld = [carve(l_at, P, NT, H + 1) for _ in range(2)]
        tc = cat[:, :, 0:H]

        def pair(name):
            return [sem(f"{name}0"), sem(f"{name}1")]

        edges_init = sem("edges_init")
        rank_arg = sem("rank_arg")
        rank_made = sem("rank_made")
        gw_step = sem("gw_step")
        edge_ends = sem("edge_ends")
        pool_turn = sem("pool_turn")
        idx_step = sem("idx_step")
        msg_step = sem("msg_step")
        prep_loaded = sem("prep_loaded")
        wts_loaded = sem("wts_loaded")
        consts_made = sem("consts_made")
        rel_rows_made = sem("rel_rows_made")
        rel_stored = sem("rel_stored")
        zeros_made = sem("zeros_made")
        tabs_zeroed = sem("tabs_zeroed")
        ident_made = sem("ident_made")
        ohz_made = sem("ohz_made")
        ev_mm = sem("ev_mm")
        ev_made = sem("ev_made")
        uv_mm = sem("uv_mm")
        uv_taken = sem("uv_taken")
        carry_out = sem("carry_out")
        carry_rows = sem("carry_rows")
        carry_scanned = sem("carry_scanned")
        carry_back = sem("carry_back")
        shifted = sem("shifted")
        exp_made = sem("exp_made")
        ex_turned = sem("ex_turned")
        ex_taken = sem("ex_taken")
        cos_arg = sem("cos_arg")
        cos_made = sem("cos_made")
        iota_h_made = sem("iota_h_made")
        stage_step = sem("stage_step")
        win_ready = pair("win_ready")
        win_mm = sem("win_mm")
        win_taken = sem("win_taken")
        cleared = pair("cleared")
        carried = sem("carried")
        adj_stored = sem("adj_stored")
        store_turn = sem("store_turn")
        piece_done = sem("piece_done")
        first_pass_over = sem("first_pass_over")
        block_in = [sem(f"block_in{r}") for r in range(AB)]
        block_used = sem("block_used")
        block_summed = sem("block_summed")
        fold_step = sem("fold_step")
        hwin_made = pair("hwin_made")
        xu_made = sem("xu_made")
        xu_stored = sem("xu_stored")
        sqrt_in = sem("sqrt_in")
        sqrt_out = sem("sqrt_out")
        elu_in = sem("elu_in")
        elu_out = sem("elu_out")
        cat_made = sem("cat_made")
        cat_turned = sem("cat_turned")
        cat_taken = sem("cat_taken")
        conv_done = sem("conv_done")
        rows_made = sem("rows_made")
        rows_stored = sem("rows_stored")
        hmv_made = sem("hmv_made")
        s1_ones = sem("s1_ones")
        sums_used = sem("sums_used")
        sums_added = sem("sums_added")
        sums_in = [sem("sums_in0"), sem("sums_in1")]
        out_made = sem("out_made")
        out_stored = sem("out_stored")
        dve_step = sem("dve_step")
        act_step = sem("act_step")

        passes = []
        for k in range(1):
            passes.append({s: [sem(f"{s}{k}_{h}") for h in range(2)]
                           for s in ("idx_ready", "gathered", "used", "oh_ready")})
        u_free = [sem("u_free0"), sem("u_free1")]
        u_stored = [sem("u_stored0"), sem("u_stored1")]

        e_in = pair("e_in")
        z_mm = sem("z_mm")
        z_used = pair("z_used")
        silu_done = sem("silu_done")
        oht_made = pair("oht_made")
        picked = pair("picked")
        hg_taken = sem("hg_taken")
        eq_made = pair("eq_made")
        gate_mm = pair("gate_mm")
        msg_made = pair("msg_made")
        summed = pair("summed")
        smm_taken = sem("smm_taken")
        sidx_made = pair("sidx_made")
        scattered = [sem(f"scattered{k}") for k in range(NTAB)]

        CH = PC // 2
        TAIL = -(-(NP + DH - N) * NT // 1024)

        def wait(eng, s, v):
            if not (isinstance(v, int) and v <= 0):
                eng.wait_ge(s, v)

        def last_messages(eng, g, h):
            wait(eng, msg_made[1 - h], g + h)

        def bc(ap, n):
            return ap.unsqueeze(2).to_broadcast([ap.shape[0], ap.shape[1], n])

        def bm(ap, n):
            return ap.unsqueeze(1).to_broadcast([ap.shape[0], n, ap.shape[1]])

        def scatters_before(s, g):
            k = s % NTAB
            per = len(range(k, 2 * HT, NTAB))
            return g * per + s // NTAB

        def scatters_through(k, h, g):
            per = len(range(k, 2 * HT, NTAB))
            return g * per + len(range(k, (h + 1) * HT, NTAB))

        z_ps = [ps[0:2 * H, 512 * b:512 * b + CH] for b in (3, 7)]

        def ps_run(bank, off, n, w):
            c = 512 * bank + off
            return ps[:, c:c + n * w].rearrange("p (a b) -> p a b", b=w)

        gate_pairs = [(ps_run(3, 0, 5, 2 * H) if q < 5 else ps_run(7, 0, 2, 2 * H))[:, q % 5, :] for q in range(PT)]
        gate_runs = [(0, 5, ps_run(3, 0, 5, 2 * H)[:, :, 0:H]), (5, 2, ps_run(7, 0, 2, 2 * H)[:, :, 0:H]),
                     (7, 4, ps_run(3, 0, 5, 2 * H)[:, 1:5, H:2 * H]), (11, 2, ps_run(7, 0, 2, 2 * H)[:, :, H:2 * H])]
        sum_runs = [(0, 10, ps_run(4, 0, 10, H + 2)), (10, 3, ps_run(1, 0, 3, H + 2))]
        pick_runs = [(0, 6, ps_run(5, 0, 6, UW)), (6, 6, ps_run(6, 0, 6, UW)), (12, 1, ps_run(2, 0, 1, UW))]

        def slot(runs, k):
            for k0, n, v in runs:
                if k0 <= k < k0 + n:
                    return v[:, k - k0, :]

        part_sums = [ps[:, 1024 * h:1024 * (h + 1)].rearrange("p (w c) -> p w c", c=512) for h in range(2)]
        win_ps = [ps[:, 512 * (4 + j):512 * (4 + j) + WN] for j in range(4)]
        uv_ps = ps[:, 0:NT * 2 * G].rearrange("p (i c) -> p i c", c=2 * G)
        conv_ps = [ps[:, 512 * (3 + b):512 * (3 + b) + 10 * H].rearrange("p (a b) -> p a b", b=H) for b in range(5)]

        block = ctx.enter_context(nc.Block())

        @block.sync
        def _(sp):
            for dst, src in ((dr_i.bitcast(I32), dst_r), (e1_s, e1_r), (dc_i.bitcast(I32), dst_c),
                             (base_i.bitcast(I32), dst_c[0:1, :].to_broadcast([P, T])),
                             (src_i[:, 0:T], src_c), (cw_c[:, :], ew_c), (X[:, :, :], x_n), (nv[:, :], nv_n),
                             (z_b.bitcast(I32), z_f.unsqueeze(0).to_broadcast([NEL, NP]))):
                sp.dma_start(dst, src).then_inc(prep_loaded, 16)
            sp.wait_ge(edges_init, 1)
            with nc.allow_non_contiguous_dma(reason="one element per row, once"):
                sp.dma_start(prev_i[1:Q, :], dst_r[0:Q - 1, W - 1:W]).then_inc(edge_ends, 16)
                sp.dma_start(next_i[0:Q - 1, :], dst_r[1:Q, 0:1]).then_inc(edge_ends, 16)
            for dst, src in ((wcat[0:H, 0, :], w_rel1), (wcat[H:2 * H, 0, :], w_root1), (wcat[2 * H:2 * H + 1, 0, :], b1.unsqueeze(0)),
                             (wcat[0:H, 1, :], w_rel2), (wcat[H:2 * H, 1, :], w_root2), (wcat[2 * H:2 * H + 1, 1, :], b2.unsqueeze(0)),
                             (w1t[0:R, 0:H], m_w1t), (w1t[R:2 * R, H:2 * H], m_w1t),
                             (b1c[0:H, :], m_b1.unsqueeze(1)), (b1c[H:2 * H, :], m_b1.unsqueeze(1)),
                             (w2b[0:H, 0:H], m_w2t), (w2b[H:2 * H, H:2 * H], m_w2t),
                             (w2b[2 * H:2 * H + 1, 0:H], m_b2.unsqueeze(0)), (w2b[2 * H:2 * H + 1, H:2 * H], m_b2.unsqueeze(0)),
                             (w3s[:, :], w3), (b3b[:, :], b3.unsqueeze(0).to_broadcast([P, H])),
                             (gam[:, :], gamma.unsqueeze(0).to_broadcast([P, H])), (bet[:, :], beta.unsqueeze(0).to_broadcast([P, H])),
                             (ev[:, 0:G], emb), (embt[:, :], emb_t), (adt[:, :], adapt_t)):
                sp.dma_start(dst, src).then_inc(wts_loaded, 16)
            sp.wait_ge(rel_rows_made, 1)
            sp.dma_start(rel_f, rel_r[:, :]).then_inc(rel_stored, 16)
            sp.wait_ge(zeros_made, 1)
            for k in range(NTAB):
                flat = sums[k].rearrange("(p a) f -> p (a f)", p=P)
                for c in range(5):
                    sp.dma_start(flat[:, c * 490:(c + 1) * 490], zero[:, 0:490]).then_inc(tabs_zeroed, 16)
            sp.wait_ge(xu_made, 1)
            sp.dma_start(xu_tab.rearrange("(i p) f -> p i f", p=P), xu).then_inc(xu_stored, 16)
            for k in range(TAIL):
                c = N * NT + k * 1024
                n = min(1024, (NP + DH) * NT - c)
                sp.dma_start(adj[:, c:c + n], zero[:, :].bitcast(BF16)[:, 0:n]).then_inc(adj_stored, 16)
            sp.sem_inc(u_free[0], 1)
            sp.sem_inc(u_free[1], 1)
            with sp.Fori(0, LOOPS) as g:
                for h in range(2):
                    sp.wait_ge(passes[0]["gathered"][h], (g + 1) * (16 * HT))
                    sp.dma_start(u_edges[bass.ds(g * 2 + h, 1)].rearrange("a p f -> (a p) f").rearrange("p (k f) -> p k f", f=G),
                                 G_ring[:, h, :, H + 1:UW]).then_inc(u_stored[h], 16)
                    sp.wait_ge(u_stored[h], (g + 1) * 16)
                    sp.sem_inc(u_free[h], 1)
                    c = sp.value_load(hoff[0:1, bass.ds(g * 2 + h, 1)], min_val=0, max_val=(N - 1) * NT)
                    sp.wait_ge(piece_done, g * 2 + (h + 1))
                    sp.sem_inc(store_turn, 1)
                    sp.wait_ge(adj_stored, g * 32 + (16 * (TAIL + h)))
                    sp.sem_inc(store_turn, 1)
                    sp.dma_start(adj[:, bass.ds(c, DH * NT)], piece[h][:, 0:DH * NT]).then_inc(adj_stored, 16)
            sp.wait_ge(u_stored[0], 16 * LOOPS)
            sp.wait_ge(u_stored[1], 16 * LOOPS)

            def load_blocks(k):
                def load(i, r):
                    use = k * NT + i
                    wait(sp, block_used, use - AB + 1)
                    sp.sem_inc(store_turn, 1)
                    sp.dma_start(blocks[r], adj[:, bass.ds(i * (P * NT), P * NT)].rearrange("p (d a) -> p d a", a=NT)
                                 ).then_inc(block_in[r], 16)
                for i in range(AB):
                    load(i, (k * NT + i) % AB)
                with sp.Fori(1, NT // AB) as s:
                    for r in range(AB):
                        load(s * AB + r, (k * NT + r) % AB)
                for i in range(NT // AB * AB, NT):
                    load(i, (k * NT + i) % AB)

            sp.wait_ge(first_pass_over, 1)
            load_blocks(0)
            load_blocks(1)
            sp.wait_ge(rel_stored, 16)
            sp.wait_ge(hmv_made, 1)

            def edge_loads(g, h):
                n0 = g * (2 * HE) + h * HE
                wait(sp, z_used[h], g)
                wait(sp, eq_made[h], g)
                wait(sp, oht_made[h], g)
                wait(sp, msg_made[h], g)
                sp.dma_start(attr_s[h][0:R, :], attr_t[:, bass.ds(n0, PC)]).then_inc(e_in[h], 16)
                sp.dma_start(attr_s[h][R:2 * R, :], attr_t[:, bass.ds(n0 + (HE - PC), PC)]).then_inc(e_in[h], 16)
                sp.dma_start(src_b[h].rearrange("p a b -> p (a b)").bitcast(I32),
                             src_f[bass.ds(n0, HE)].unsqueeze(0).to_broadcast([P, HE])).then_inc(e_in[h], 16)
                sp.dma_start(rel_b[h], rel_f.rearrange("q w -> (q w)")[bass.ds(n0, HE)].unsqueeze(0).to_broadcast([P, HE])).then_inc(e_in[h], 16)
                sp.dma_start(u_s[h].rearrange("p a b -> p (a b)"),
                             u_edges[bass.ds(g * 2 + h, 1)].rearrange("a p f -> (a p) f")).then_inc(e_in[h], 16)

            edge_loads(0, 0)
            edge_loads(0, 1)
            with sp.Fori(1, LOOPS) as g:
                for h in range(2):
                    edge_loads(g, h)
            for k in range(NTAB):
                sp.wait_ge(scattered[k], 16 * scatters_before(k, LOOPS))
            sp.wait_ge(msg_made[1], LOOPS)
            for k in range(NTAB):
                if k >= 2:
                    sp.wait_ge(sums_added, k - 1)
                sp.dma_start(ld[k % 2], sums[k][0:NP, :].rearrange("(i p) f -> p i f", p=P)).then_inc(sums_in[k % 2], 16)
            sp.wait_ge(sums_used, 1)
            load_blocks(2)
            sp.wait_ge(out_made, 1)
            full = N // P
            sp.dma_start(out[0:full * P, :].rearrange("(i p) f -> p i f", p=P), X[:, 0:full, :]).then_inc(out_stored, 16)
            sp.dma_start(out[full * P:N, :], X[0:N - full * P, full, :]).then_inc(out_stored, 16)
            sp.wait_ge(out_stored, 32)

        @block.gpsimd
        def _(pool):
            nc.gpsimd.iota(iota_i[:, :], [[1, 2 * P]], base=0, channel_multiplier=0).then_inc(consts_made, 1)
            nc.gpsimd.iota(ip_i[:, :], [[P, 2]], base=0, channel_multiplier=1).then_inc(consts_made, 1)

            def gather_pass(k, table, width, stored, value):
                pz = passes[k]
                pool.wait_ge(stored, value)
                with pool.Fori(0, LOOPS) as g:
                    for h in range(2):
                        pool.wait_ge(pz["idx_ready"][h], g + 1)
                        pool.wait_ge(pz["used"][h], g + 1)
                        if k == 0:
                            pool.wait_ge(u_free[h], g + 1)
                        pool.sem_inc(pool_turn, 1)
                        for j in range(HT):
                            pool.indirect_dma_start((G_ring if k == 0 else G_parts)[:, h, j, 0:width], None, table,
                                                    bass.IndirectOffsetOnAxis(ap=idx_st.bitcast(U32)[:, h, j:j + 1], axis=0)
                                                    ).then_inc(pz["gathered"][h], 16)

            gather_pass(0, xu_tab, UW, xu_stored, 16)
            pool.wait_ge(tabs_zeroed, 80 * NTAB)

            def scatter(g):
                for h in range(2):
                    pool.wait_ge(sidx_made[h], g + 1)
                    pool.wait_ge(smm_taken, g * 2 + h + 1)
                    for j in range(HT):
                        s = h * HT + j
                        wait(pool, scattered[s % NTAB], scatters_before(s, g) * 16)
                        pool.sem_inc(pool_turn, 1)
                        pool.indirect_dma_start(sums[s % NTAB], bass.IndirectOffsetOnAxis(ap=sidx[h].bitcast(U32)[:, j:j + 1], axis=0),
                                                smm[h][:, j, 0:H + 1], None, compute_op=ALU.add).then_inc(scattered[s % NTAB], 16)
            scatter(0)
            with pool.Fori(1, LOOPS) as g:
                scatter(g)

        @block.scalar
        def _(act):
            def sqrt_step(n):
                act.wait_ge(sqrt_in, n)
                nc.scalar.activation(st[:, 2, :], st[:, 1, :], ACT.Sqrt).then_inc(sqrt_out, 1)

            def stage(k):
                pz = passes[k]

                def indices(g, h):
                    act.wait_ge(pz["used"][h], g + 1)
                    nc.scalar.copy(idx_st.bitcast(I32)[:, h, :], src_i[:, bass.ds(g * (2 * HT) + h * HT, HT)]).then_inc(pz["idx_ready"][h], 1)

                def columns(g, h):
                    wait(act, win_ready[h], g)
                    nc.scalar.copy(win_s[:, h, :], win_c[:, bass.ds(g * (2 * HT) + h * HT, HT)])
                    nc.scalar.copy(low_s[:, h, :], low_c[:, bass.ds(g * (2 * HT) + h * HT, HT)]).then_inc(stage_step, 1)

                def windows(g, h, first=False):
                    act.wait_ge(cleared[h], g + 1)
                    if not first:
                        c = act.value_load(coff[0:1, bass.ds(g * 2 + h, 1)], min_val=0, max_val=(DH - 1) * NT)
                        nc.scalar.copy(piece[h][:, 0:NT], piece[1 - h][:, bass.ds(c, NT)]).then_inc(carried, 1)
                    else:
                        act.nop().then_inc(carried, 1)
                    for j in range(HT):
                        if j == 3:
                            columns(g + h, 1 - h)
                            indices(g + h, 1 - h)
                        c = act.value_load(toff[0:1, bass.ds(g * (2 * HT) + (h * HT + j), 1)], min_val=0, max_val=(DH - 1) * NT)
                        act.wait_ge(win_mm, g * (2 * HT) + (h * HT + j + 1))
                        ins = nc.scalar.copy(piece[h][:, bass.ds(c, WN)], win_ps[(h * HT + j) % 4])
                        ins.then_inc(win_taken, 1)
                    act.wait_ge(win_taken, g * (2 * HT) + (h + 1) * HT)
                    act.nop().then_inc(piece_done, 1)

                def both(g, first=False):
                    for h in range(2):
                        windows(g, h, first and h == 0)

                indices(0, 0)
                columns(0, 0)
                both(0, first=True)
                with act.Fori(1, LOOPS) as g:
                    both(g)

            def conv(m, K):
                for b in range(13):
                    n = min(4, NT - 4 * b)
                    act.wait_ge(cat_turned, 13 * m + b + 1)
                    nc.scalar.copy(cat_t[0:K, 4 * b:4 * b + n, :].rearrange("p a b -> p (a b)"),
                                   ps[0:K, 512 * (b % 3):512 * (b % 3) + n * P]).then_inc(cat_taken, 1)

            act.wait_ge(rank_arg, 1)
            nc.scalar.activation(rank_w[:, :], rank_w[:, :], ACT.Exp).then_inc(rank_made, 1)
            act.wait_ge(shifted, 1)
            nc.scalar.activation(rst_b, mx_b, ACT.Exp).then_inc(exp_made, 1)
            act.wait_ge(cos_arg, 1)
            nc.scalar.activation(tmp_c, tmp_c, ACT.Sin, scale=-PI / CUTOFF, bias=half_pi[:, :]).then_inc(cos_made, 1)
            act.wait_ge(ex_taken, 1)
            stage(0)
            act.wait_ge(elu_in, 1)
            nc.scalar.activation(tb, tb, ACT.Exp).then_inc(elu_out, 1)
            sqrt_step(1)
            conv(0, 2 * H + 1)
            conv(1, 2 * H + 1)
            sqrt_step(2)
            act.wait_ge(s1_ones, 1)
            act.wait_ge(hmv_made, 1)

            def window(g, h):
                c = act.value_load(hcol[0:1, bass.ds(g * 2 + h, 1)], min_val=0, max_val=(NT - 1) * 3 * UW)
                nc.scalar.copy(hwin[h], HMV_flat[:, bass.ds(c, 6 * UW)]).then_inc(hwin_made[h], 1)

            window(0, 0)
            def take_sums(g, h):
                act.wait_ge(summed[h], g + 1)
                for k in range(NTAB):
                    wait(act, scattered[k], scatters_through(k, h, g - 1) * 16 if not (isinstance(g, int) and g == 0) else 0)
                for i, (k0, n, v) in enumerate(sum_runs):
                    ins = nc.scalar.copy(smm[h][:, k0:k0 + n, :], v)
                ins.then_inc(smm_taken, 1)

            def third(g, first=False):
                for h in range(2):
                    act.wait_ge(picked[h], g + 1)
                    last_messages(act, g, h)
                    for k0, n, v in pick_runs:
                        ins = nc.scalar.copy(hg[:, k0:k0 + n, :], v)
                    ins.then_inc(hg_taken, 1)
                    if h == 0:
                        wait(act, picked[1], g)
                    window(g + h, 1 - h)
                    wait(act, gate_mm[h], g)
                    for c in range(2):
                        act.wait_ge(z_mm, g * 4 + (2 * h + c + 1))
                        nc.scalar.activation(s1t[h][0:2 * H, c * CH:(c + 1) * CH], z_ps[c], ACT.Silu, bias=b1c[:, 0:1]).then_inc(silu_done, 1)
                    if h == 1:
                        take_sums(g, 0)
                    elif not first:
                        take_sums(g - 1, 1)

            third(0, first=True)
            with act.Fori(1, LOOPS) as g:
                third(g)
            take_sums(LOOPS - 1, 1)
            sqrt_step(3)
            sqrt_step(4)
            act.wait_ge(cat_made, 3)
            conv(2, H)
            sqrt_step(5)
            sqrt_step(6)

        @block.tensor
        def _(pe):
            pe.wait_ge(wts_loaded, 16 * 21)
            nc.tensor.matmul(ps[0:NEL, 7 * 512:7 * 512 + G], embt[:, :], adt[:, :], start=True, stop=True).then_inc(ev_mm, 1)
            pe.wait_ge(ev_made, 1)
            pe.wait_ge(ohz_made, 1)
            for i in range(NT):
                ins = nc.tensor.matmul(uv_ps[:, i, :], ohz[:, i * P:(i + 1) * P], ev[:, :], start=True, stop=True)
            ins.then_inc(uv_mm, 1)
            pe.wait_ge(carry_out, 1)
            for c in range(4):
                ins = nc.tensor.transpose(ps[0:1, 7 * 512 + c * Q:7 * 512 + (c + 1) * Q], carry[:, c:c + 1], ident[0:Q, 0:Q])
            ins.then_inc(carry_rows, 1)
            pe.wait_ge(carry_scanned, 1)
            for c in range(2):
                ins = nc.tensor.transpose(ps[0:Q, 7 * 512 + 4 * Q + 4 * c:7 * 512 + 4 * Q + 4 * c + 1], cscan[0:1, c, :], ident[0:1, 0:1])
            ins.then_inc(carry_back, 1)
            pe.wait_ge(exp_made, 1)
            pe.wait_ge(uv_taken, 1)
            for b in range(HT):
                ins = nc.tensor.transpose(ps[:, b * P:b * P + Q], rst_b[:, b * P:(b + 1) * P], ident[0:Q, 0:Q])
            ins.then_inc(ex_turned, 1)

            def first_pass():
                pz = passes[0]
                for h in range(2):
                    pe.sem_inc(pz["used"][h], 1)
                width = 3 * (H + 1) + 1

                def window(g, h, j):
                    n = g * (2 * HT) + (h * HT + j)
                    c = pe.value_load(toff[0:1, bass.ds(n, 1)], min_val=0, max_val=(DH - 1) * NT)
                    if j == 0:
                        pe.wait_ge(win_ready[h], g + 1)
                        pe.wait_ge(carried, g * 2 + (h + 1))
                    o = win_ps[(h * HT + j) % 4]
                    nc.tensor.matmul(o, low_oh[h][:, j, :], win_oh[h][:, j, :], start=True, stop=False)
                    wait(pe, win_taken, n)
                    nc.tensor.matmul(o[:, 0:NT], ident_b[:, :], piece[h][:, bass.ds(c, NT)], start=False, stop=True).then_inc(win_mm, 1)

                def sums(g, h):
                    for j in range(HT):
                        window(g, h, j)
                    pe.wait_ge(pz["oh_ready"][h], g + 1)
                    pe.wait_ge(pz["gathered"][h], (g + 1) * (16 * HT))
                    for j in range(HT):
                        for w in range(2):
                            ins = nc.tensor.matmul(part_sums[h][:, w, 0:width], oh[:, h * HT + j, w * P:(w + 1) * P],
                                                   gw_p[h][:, j, 0:width], start=(j == 0), stop=(j == HT - 1))
                    ins.then_inc(pz["used"][h], 1)

                sums(0, 0)
                sums(0, 1)
                with pe.Fori(1, LOOPS) as g:
                    sums(g, 0)
                    sums(g, 1)

            def product(k):
                pe.wait_ge(rows_made, k + 1)

                def block(i, r, turn):
                    n = k * NT + i
                    pe.wait_ge(block_in[r], turn)
                    wait(pe, block_summed, n - AB + 1)
                    for a in range(NT):
                        ins = nc.tensor.matmul(ps[:, 512 * r:512 * r + 3 * H], blocks[r][:, :, a], parts[:, a, :],
                                               start=(a == 0), stop=(a == NT - 1))
                    ins.then_inc(block_used, 1)

                def turn(n):
                    return (n // AB + 1) * 16
                for i in range(AB):
                    block(i, (k * NT + i) % AB, turn(k * NT + i))
                with pe.Fori(1, NT // AB) as s:
                    for r in range(AB):
                        block(s * AB + r, (k * NT + r) % AB, s * 16 + turn(k * NT + r))
                for i in range(NT // AB * AB, NT):
                    block(i, (k * NT + i) % AB, turn(k * NT + i))

            def conv(m, source, K, rhs):
                pe.wait_ge(cat_made, m + 1)
                for b in range(13 + 1):
                    if b < 13:
                        if b >= 3:
                            pe.wait_ge(cat_taken, 13 * m + b - 2)
                        for i in range(4 * b, min(4 * b + 4, NT)):
                            c = 512 * (b % 3) + (i % 4) * P
                            ins = nc.tensor.transpose(ps[0:K, c:c + P], source[:, i, :], ident[:, :])
                        ins.then_inc(cat_turned, 1)
                    if b >= 1:
                        pe.wait_ge(cat_taken, 13 * m + b)
                        for i in range(4 * b - 4, min(4 * b, NT)):
                            ins = nc.tensor.matmul(conv_ps[i // 10][:, i % 10, :], cat_t[0:K, i, :], rhs, start=True, stop=True)
                ins.then_inc(conv_done, 1)

            first_pass()
            product(0)
            conv(0, cat, 2 * H + 1, wcat[0:2 * H + 1, 0, :])
            product(1)
            conv(1, cat, 2 * H + 1, wcat[0:2 * H + 1, 1, :])

            def first_product(g, h):
                pe.wait_ge(e_in[h], (g + 1) * 80)
                last_messages(pe, g, h)
                for c in range(2):
                    ins = nc.tensor.matmul(z_ps[c], w1t[:, :], attr_s[h][:, c * CH:(c + 1) * CH], start=True, stop=True)
                    ins.then_inc(z_mm, 1)
                pe.wait_ge(z_mm, g * 4 + (2 * h + 2))
                pe.nop().then_inc(z_used[h], 1)

            def pick(g, h):
                pe.wait_ge(oht_made[h], g + 1)
                pe.wait_ge(hwin_made[h], g + 1)
                wait(pe, hg_taken, g * 2 + h)
                for j in range(HT):
                    for w in range(2):
                        for part in range(3):
                            ins = nc.tensor.matmul(slot(pick_runs, j), oh_t[h][:, w, j * P:(j + 1) * P],
                                                   hwin[h][:, (3 * w + part) * UW:(3 * w + part + 1) * UW],
                                                   start=(w == 0 and part == 0), stop=(w == 1 and part == 2))
                ins.then_inc(picked[h], 1)

            def combine(g, h):
                pe.wait_ge(msg_made[h], g + 1)
                pe.wait_ge(eq_made[h], g + 1)
                wait(pe, smm_taken, g * 2 + h)
                for j in range(HT):
                    o = slot(sum_runs, j)
                    for part in range(3):
                        nc.tensor.matmul(o[:, 0:H + 1], eq[h][:, j, :], msg_p[h][:, j, part * (H + 1):(part + 1) * (H + 1)],
                                         start=(part == 0), stop=(part == 2))
                    ins = nc.tensor.matmul(o[:, H + 1:H + 2], eq[h][:, j, :], rank_b[:, :], start=True, stop=True)
                ins.then_inc(summed[h], 1)

            def gates(g, h):
                pe.wait_ge(silu_done, g * 4 + (2 * h + 2))
                for q in range(PT):
                    ins = nc.tensor.matmul(gate_pairs[q], s1t[h][:, q * P:(q + 1) * P], w2b[:, :], start=True, stop=True)
                ins.then_inc(gate_mm[h], 1)

            def third(g, first=False):
                for h in range(2):
                    pick(g, h)
                    if h == 1:
                        combine(g, 0)
                    elif not first:
                        combine(g - 1, 1)
                    first_product(g, h)
                    gates(g, h)

            pe.wait_ge(hmv_made, 1)
            third(0, first=True)
            with pe.Fori(1, LOOPS) as g:
                third(g)
            combine(LOOPS - 1, 1)
            conv(2, X, H, w3s[:, :])
            product(2)

        @block.vector
        def _(dve):
            V = nc.vector
            n_step = [0]

            def step(ins):
                n_step[0] += 1
                ins.then_inc(dve_step, 1)
                dve.wait_ge(dve_step, n_step[0])

            def tt(o, x, y, op):
                step(V.tensor_tensor(o, x, y, op))

            def ts(o, x, s1, op0, s2=None, op1=None):
                step(V.tensor_scalar(o, x, s1, s2, op0, op1) if op1 is not None else V.tensor_scalar(o, x, s1, None, op0))

            def split(p, v, rest):
                step(V.tensor_copy(p[0], v))
                tt(rest, v, p[0], ALU.subtract)
                step(V.tensor_copy(p[1], rest))
                tt(p[2], rest, p[1], ALU.subtract)

            V.memset(zero[:, :], 0.0).then_inc(zeros_made, 1)
            step(V.memset(HMV[:, NT, :, :], 0.0))
            step(V.memset(w1t[:, :], 0.0))
            step(V.memset(w2b[:, :], 0.0))
            step(V.memset(wide_neg[:, :], -1.0))
            step(V.tensor_copy(prev_i[:, :], wide_neg[:, 0:1]))
            V.tensor_copy(next_i[:, :], wide_neg[:, 1:2]).then_inc(edges_init, 1)
            step(V.memset(half_pi[:, :], PI / 2))
            dve.wait_ge(consts_made, 2)
            step(V.tensor_copy(iota_f[:, :], iota_i[:, :]))
            step(V.tensor_copy(iota_p[:, :], ip_i[:, :]))
            ts(dump_i[:, :], iota_p[:, 0:1], float(NP), ALU.add)
            ts(ident[:, :], iota_f[:, 0:P], iota_p[:, 0:1], ALU.is_equal)
            step(V.tensor_copy(ident_b[:, :], ident[:, :]))
            step(V.tensor_copy(iota_b[:, :], iota_i[:, :]))
            ts(rank_w[:, 0:1], iota_p[:, 0:1], -LN3, ALU.mult, 63 * LN3, ALU.add)
            V.tensor_scalar(rank_w[:, 1:2], iota_p[:, 0:1], LN3, -63 * LN3, ALU.mult, ALU.add).then_inc(rank_arg, 1)
            dve.wait_ge(rank_made, 1)
            step(V.tensor_copy(rank_b[:, :], rank_w[:, 0:1]))
            step(V.tensor_copy(rank_c[:, :], rank_w[:, 1:2]))
            dve.wait_ge(prep_loaded, 16 * 9)
            V.tensor_scalar(ohz, z_b.bitcast(I32), iota_p[0:NEL, 0:1], None, ALU.is_equal).then_inc(ohz_made, 1)
            dve.wait_ge(ev_mm, 1)
            V.tensor_copy(ev[:, G:2 * G], ps[0:NEL, 7 * 512:7 * 512 + G]).then_inc(ev_made, 1)
            bi = base_i.bitcast(I32)
            biq = bi.rearrange("p (q k) -> p q k", k=HT)
            ts(hoff[:, :], biq[0:1, :, 0], NT, ALU.mult)
            tt(toff[:, :].rearrange("p (q k) -> p q k", k=HT), biq[0:1, :, :], biq[0:1, :, 0].unsqueeze(2).to_broadcast([1, Q, HT]), ALU.subtract)
            ts(toff[:, :], toff[:, :], NT, ALU.mult)
            step(V.memset(coff[:, :], 0))
            tt(coff[:, 1:Q], hoff[:, 1:Q], hoff[:, 0:Q - 1], ALU.subtract)
            tt(win_c[:, 0:T], dc_i.bitcast(I32), bi, ALU.subtract)
            step(V.memset(src_i[:, T:T + HT], 0))
            step(V.memset(win_c[:, T:T + HT], 0.0))
            ts(low_c[:, 0:T].bitcast(I32), src_i[:, 0:T], 7, ALU.logical_shift_right)
            step(V.scalar_tensor_tensor(out=win_c[:, 0:T], in0=win_c[:, 0:T], scalar=float(NT), in1=low_c[:, 0:T].bitcast(I32), op0=ALU.mult, op1=ALU.add))
            ts(low_c.bitcast(I32), src_i[:, 0:T + HT], P - 1, ALU.bitwise_and)
            step(V.tensor_copy(low_c, low_c.bitcast(I32)))
            ts(base_c[:, :], bi.rearrange("p (q k) -> p q k", k=HT)[:, :, 0], -P, ALU.bitwise_and)
            tt(rel_c[:, :].rearrange("p (q k) -> p q k", k=HT), dc_i.bitcast(I32).rearrange("p (q k) -> p q k", k=HT),
               bc(base_c[:, :], HT), ALU.subtract)
            ts(acol[:, :], base_c[0:1, :], AW / P, ALU.mult)
            step(V.memset(hcol[:, :], 0))
            ts(hcol[:, 0:Q], base_c[0:1, :], 3 * UW / P, ALU.mult)
            dri = dr_i.bitcast(I32)
            ts(base_r[:, :], dri[:, 0:1], -P, ALU.bitwise_and)
            V.tensor_tensor(rel_r[:, :], dri, base_r[:, :].to_broadcast([Q, W]), ALU.subtract).then_inc(rel_rows_made, 1)
            step(V.tensor_copy(dr_f, dri))
            dve.wait_ge(edge_ends, 32)
            step(V.tensor_copy(prev_f[:, :], prev_i[:, :]))
            step(V.tensor_copy(next_f[:, :], next_i[:, :]))
            step(V.memset(rst_b, -BIG))
            tt(rst_b[:, 0:W - 1], dr_f[:, 0:W - 1], dr_f[:, 1:W], ALU.not_equal)
            ts(rst_b[:, 0:W - 1], rst_b[:, 0:W - 1], -BIG, ALU.mult)
            step(V.memset(rst_f, -BIG))
            step(V.tensor_copy(rst_f[:, 1:W], rst_b[:, 0:W - 1]))
            step(V.tensor_tensor_scan(mx_f, rst_f, e1_s, -BIG, ALU.add, ALU.max))
            step(V.tensor_tensor_scan(mx_b[:, ::-1], rst_b[:, ::-1], e1_s[:, ::-1], -BIG, ALU.add, ALU.max))
            d0, d1 = dr_f[:, 0:1], dr_f[:, W - 1:W]
            tt(pen[:, 0:1], prev_f[:, :], d0, ALU.not_equal)
            tt(pen[:, 1:2], next_f[:, :], d1, ALU.not_equal)
            tt(pen[:, 2:3], d0, d1, ALU.not_equal)
            ts(pen[:, :], pen[:, :], -BIG, ALU.mult)
            step(V.tensor_copy(carry[:, 0:1], mx_f[:, W - 1:W]))
            tt(carry[:, 1:2], pen[:, 0:1], pen[:, 2:3], ALU.add)
            step(V.tensor_copy(carry[:, 2:3], mx_b[:, 0:1]))
            V.tensor_tensor(carry[:, 3:4], pen[:, 1:2], pen[:, 2:3], ALU.add).then_inc(carry_out, 1)
            dve.wait_ge(carry_rows, 1)
            step(V.tensor_copy(crow[:, :, :], ps[0:1, 7 * 512:7 * 512 + 4 * Q].rearrange("p (a b) -> p a b", b=Q)))
            step(V.memset(cscan[:, :, :], -BIG))
            step(V.tensor_tensor_scan(cst[:, 0, :], crow[:, 1, :], crow[:, 0, :], -BIG, ALU.add, ALU.max))
            step(V.tensor_tensor_scan(cst[:, 1, ::-1], crow[:, 3, ::-1], crow[:, 2, ::-1], -BIG, ALU.add, ALU.max))
            step(V.tensor_copy(cscan[:, 0, 1:Q], cst[:, 0, 0:Q - 1]))
            V.tensor_copy(cscan[:, 1, 0:Q - 1], cst[:, 1, 1:Q]).then_inc(carry_scanned, 1)
            dve.wait_ge(carry_back, 1)
            for c in range(2):
                tt(cin[:, c:c + 1], ps[0:Q, 7 * 512 + 4 * Q + 4 * c:7 * 512 + 4 * Q + 4 * c + 1], pen[:, c:c + 1], ALU.add)
            tt(mx_f, mx_f, mx_b, ALU.max)
            for c, d in ((0, d0), (1, d1)):
                ts(mx_b, dr_f, d, ALU.not_equal, -BIG, ALU.mult)
                step(V.scalar_tensor_tensor(out=mx_f, in0=mx_b, scalar=cin[:, c:c + 1], in1=mx_f, op0=ALU.add, op1=ALU.max))
            V.tensor_tensor(mx_b, e1_s, mx_f, ALU.subtract).then_inc(shifted, 1)
            ts(dc_i.bitcast(I32), cw_c[:, :], 0.5 / CUTOFF, ALU.mult)
            step(V.scalar_tensor_tensor(out=tmp_c, in0=dc_i.bitcast(I32), scalar=-2 * CUTOFF, in1=cw_c[:, :], op0=ALU.mult, op1=ALU.add))
            step(V.scalar_tensor_tensor(out=tmp_c, in0=tmp_c, scalar=-1.0, in1=tmp_c, op0=ALU.mult, op1=ALU.max))
            ts(tmp_c, tmp_c, -CUTOFF, ALU.add)
            V.scalar_tensor_tensor(out=tmp_c, in0=tmp_c, scalar=-1.0, in1=tmp_c, op0=ALU.mult, op1=ALU.max).then_inc(cos_arg, 1)
            dve.wait_ge(cos_made, 1)
            ts(tmp_c, tmp_c, -0.5, ALU.mult, 0.5, ALU.add)
            step(V.scalar_tensor_tensor(out=cw_c[:, :], in0=cw_c[:, :], scalar=CUTOFF, in1=tmp_c, op0=ALU.is_lt, op1=ALU.mult))
            dve.wait_ge(uv_mm, 1)
            step(V.tensor_copy(xu[:, :, H + 1:UW], uv_ps[:, :, 0:G]))
            step(V.tensor_copy(xu[:, :, 0:H], X[:, :, :]))
            step(V.memset(xu[:, :, H:H + 1], 1.0))
            V.engine_nop().then_inc(xu_made, 1)
            split([HMV[:, 0:NT, c, H + 1:UW] for c in range(3)], uv_ps[:, :, G:2 * G], v_rest)
            V.engine_nop().then_inc(uv_taken, 1)
            dve.wait_ge(ex_turned, 1)
            step(V.tensor_copy(ex_c[:, :].rearrange("p (q b) -> p b q", b=HT),
                               ps[:, 0:HT * P].rearrange("p (b q) -> p b q", q=P)[:, :, 0:Q]))
            V.memset(idx_st.rearrange("p a b -> p (a b)"), 0.0).then_inc(ex_taken, 1)
            dve.wait_ge(xu_stored, 16)

            folds = [0]

            def scatter_operands(k):
                pz = passes[k]
                ns = 1 if k == 0 else 0
                n_fold = folds[0]
                folds[0] += 2 * LOOPS

                def fold(g, h):
                    n = (g * 2 + h + n_fold) * 3
                    dve.wait_ge(pz["used"][h], g + 2)
                    c = dve.value_load(acol[0:1, bass.ds(g * 2 + h, 1)], min_val=0, max_val=(NT - 1) * AW)
                    v = part_sums[h][:, :, 0:3 * (H + ns)].rearrange("p w (c f) -> p w f c", c=3)
                    if k == 0:
                        V.tensor_copy(fold_s[h][:, :, H + 1], part_sums[h][:, :, 3 * (H + 1)]).then_inc(fold_step, 1)
                    else:
                        V.engine_nop().then_inc(fold_step, 1)
                    V.tensor_reduce(fold_s[h][:, :, 0:H + ns], v, AX.X, ALU.add).then_inc(fold_step, 1)
                    dve.wait_ge(fold_step, n + 2)
                    V.tensor_tensor(ACC_flat[:, bass.ds(c, 2 * AW)], ACC_flat[:, bass.ds(c, 2 * AW)],
                                    fold_s[h].rearrange("p a b -> p (a b)"), ALU.add).then_inc(fold_step, 1)

                def operands(g, h, first=False):
                    t0 = g * (2 * HT) + h * HT
                    if k == 0:
                        dve.wait_ge(stage_step, g * 2 + (h + 1))
                        wait(dve, win_mm, g * (2 * HT) + (h - 1) * HT)
                        for j in range(HT):
                            V.tensor_scalar(win_oh[h][:, j, :], iota_h, win_s[:, h, j:j + 1], None, ALU.is_equal)
                            ins = V.tensor_scalar(low_oh[h][:, j, :], iota_b[:, 0:P], low_s[:, h, j:j + 1], None, ALU.is_equal)
                        ins.then_inc(win_ready[h], 1)
                        if not isinstance(g, int):
                            dve.wait_ge(adj_stored, g * 32 + 16 * (TAIL + h - 1))
                        V.memset(piece[h], 0.0).then_inc(cleared[h], 1)
                    dve.wait_ge(pz["used"][h], g + 1)
                    ins = V.tensor_tensor(oh[:, h * HT:(h + 1) * HT, :], bm(iota_b[:, :], HT), bc(rel_c[:, bass.ds(t0, HT)], 2 * P), ALU.is_equal)
                    if k > 0:
                        ins.then_inc(pz["oh_ready"][h], 1)
                    if h == 1:
                        fold(g, 0)
                    elif not first:
                        fold(g - 1, 1)
                    if k == 0:
                        n = g * 2 + h
                        dve.wait_ge(pz["gathered"][h], (g + 1) * (16 * HT))
                        p = [gw_p[h][:, :, c * (H + 1):(c + 1) * (H + 1)] for c in range(3)]
                        V.tensor_tensor(gw[h], G_ring[:, h, :, 0:H + 1], bc(ex_c[:, bass.ds(t0, HT)], H + 1), ALU.mult).then_inc(gw_step, 1)
                        dve.wait_ge(gw_step, n * 4 + 1)
                        V.tensor_copy(p[0], gw[h]).then_inc(gw_step, 1)
                        dve.wait_ge(gw_step, n * 4 + 2)
                        V.tensor_tensor(gw_r, gw[h], p[0], ALU.subtract).then_inc(gw_step, 1)
                        dve.wait_ge(gw_step, n * 4 + 3)
                        V.tensor_copy(p[1], gw_r).then_inc(gw_step, 1)
                        dve.wait_ge(gw_step, n * 4 + 4)
                        V.tensor_tensor(p[2], gw_r, p[1], ALU.subtract).then_inc(pz["oh_ready"][h], 1)

                step(V.memset(ACC[:, :, :], 0.0))
                for c in range(0, WN, P):
                    n = min(P, WN - c)
                    ts(iota_h[:, c:c + n], iota_f[:, 0:n], float(c), ALU.add)
                for h in range(2):
                    step(V.memset(fold_s[h], 0.0))
                    if k == 0:
                        step(V.memset(gw_p[h][:, :, 3 * (H + 1)], 1.0))
                operands(0, 0, first=True)
                operands(0, 1)
                with dve.Fori(1, LOOPS) as g:
                    operands(g, 0)
                    operands(g, 1)
                fold(LOOPS - 1, 1)
                dve.wait_ge(fold_step, folds[0] * 3)
                dve.wait_ge(adj_stored, 16 * (TAIL + 2 * LOOPS))

            def table_rows(v):
                split([parts[:, :, c * H:(c + 1) * H] for c in range(3)], v, tb)

            def take_products(k):
                def take(i, r):
                    n = k * NT + i
                    dve.wait_ge(block_used, n + 1)
                    v = ps[:, 512 * r:512 * r + 3 * H].rearrange("p (c f) -> p f c", c=3)
                    V.tensor_reduce(ACC_flat[:, bass.ds(i * AW, H)], v, AX.X, ALU.add).then_inc(block_summed, 1)
                with dve.Fori(0, NT // AB) as s:
                    for r in range(AB):
                        take(s * AB + r, (k * NT + r) % AB)
                for i in range(NT // AB * AB, NT):
                    take(i, (k * NT + i) % AB)
                dve.wait_ge(block_summed, (k + 1) * NT)

            n_norm = [0]

            def layernorm(v, o, sq, gain=None, shift=None):
                n_norm[0] += 1
                step(V.tensor_reduce(st[:, 0, :], v, AX.X, ALU.add))
                ts(st[:, 0, :], st[:, 0, :], -1.0 / H, ALU.mult)
                tt(v, v, bc(st[:, 0, :], H), ALU.add)
                tt(sq, v, v, ALU.mult)
                step(V.tensor_reduce(st[:, 1, :], sq, AX.X, ALU.add))
                V.tensor_scalar(st[:, 1, :], st[:, 1, :], 1.0 / H, EPS, ALU.mult, ALU.add).then_inc(sqrt_in, 1)
                dve.wait_ge(sqrt_out, n_norm[0])
                step(V.reciprocal(st[:, 3, :], st[:, 2, :]))
                tt(o, v, bc(st[:, 3, :], H), ALU.mult)
                if gain is not None:
                    tt(o, o, bm(gain, NT), ALU.mult)
                    tt(o, o, bm(shift, NT), ALU.add)

            scatter_operands(0)
            V.engine_nop().then_inc(first_pass_over, 1)
            ts(deg[:, :], ACC[:, 0:NT, H + 1], 1.0, ALU.add)
            ts(st[:, 4, :], ACC[:, 0:NT, H], 1e-30, ALU.max)
            step(V.reciprocal(st[:, 5, :], st[:, 4, :]))
            tt(ta, ACC[:, 0:NT, 0:H], bc(st[:, 5, :], H), ALU.mult)
            V.tensor_scalar(tb, ta, 0.0, None, ALU.min).then_inc(elu_in, 1)
            dve.wait_ge(elu_in, 1)
            ts(ta, ta, 0.0, ALU.max)
            dve.wait_ge(elu_out, 1)
            step(V.scalar_tensor_tensor(out=ta, in0=tb, scalar=-1.0, in1=ta, op0=ALU.add, op1=ALU.add))
            tt(ta, ta, X[:, :, :], ALU.add)
            layernorm(ta, X[:, :, :], tb)
            dve.wait_ge(u_stored[0], 16 * LOOPS)
            dve.wait_ge(u_stored[1], 16 * LOOPS)
            table_rows(X[:, :, :])
            V.engine_nop().then_inc(rows_made, 1)

            def make_cat(first):
                step(V.tensor_copy(cat[:, :, 0:H], ACC[:, 0:NT, 0:H]))
                step(V.tensor_copy(cat[:, :, H:2 * H], (X if first else HN)[:, :, :]))
                V.memset(cat[:, :, 2 * H:2 * H + 1], 1.0).then_inc(cat_made, 1)

            take_products(0)
            make_cat(True)
            dve.wait_ge(conv_done, 1)
            for b in range(5):
                n = min(10, NT - 10 * b)
                ts(HN[:, 10 * b:10 * b + n, :], conv_ps[b][:, 0:n, :], 0.0, ALU.max)
            table_rows(HN[:, :, :])
            V.engine_nop().then_inc(rows_made, 1)
            take_products(1)
            make_cat(False)
            dve.wait_ge(conv_done, 2)
            for b in range(5):
                n = min(10, NT - 10 * b)
                tt(ta[:, 10 * b:10 * b + n, :], conv_ps[b][:, 0:n, :], X[:, 10 * b:10 * b + n, :], ALU.add)
            layernorm(ta, X[:, :, :], tb)
            tt(ta, X[:, :, :], bc(nv[:, :], H), ALU.mult)
            for v, c0, c1, rest in ((ta, 0, H, tb), (nv[:, :].unsqueeze(2), H, H + 1, st[:, 0, :].unsqueeze(2))):
                split([HMV[:, 0:NT, c, c0:c1] for c in range(3)], v, rest)
            step(V.memset(s1t[0], 1.0))
            V.memset(s1t[1], 1.0).then_inc(s1_ones, 1)
            V.engine_nop().then_inc(hmv_made, 1)

            def own(s, v):
                dve.wait_ge(s, v)

            def turned_one_hots(g, h):
                dve.wait_ge(e_in[h], (g + 1) * 80)
                wait(dve, picked[h], g)
                V.tensor_scalar(oh_t[h][:, 0, :], rel_b[h], iota_p[:, 0:1], None, ALU.is_equal)
                V.tensor_scalar(oh_t[h][:, 1, :], rel_b[h], iota_p[:, 1:2], None, ALU.is_equal).then_inc(oht_made[h], 1)

            def equals(g, h):
                t0 = g * (2 * HT) + h * HT
                dve.wait_ge(e_in[h], (g + 1) * 80)
                wait(dve, summed[h], g)
                V.tensor_tensor(eq[h], src_b[h].bitcast(I32), bc(src_i[:, bass.ds(t0, HT)], P), ALU.is_equal).then_inc(eq_made[h], 1)

            def targets(g, h):
                n = g * 2 + h
                t0 = g * (2 * HT) + h * HT
                dve.wait_ge(smm_taken, n + 1)
                V.tensor_scalar(first, smm[h][:, :, H + 1], rank_c[:, 0:1], 2.0, ALU.mult, ALU.is_gt).then_inc(idx_step, 1)
                V.tensor_copy(srcf, src_i[:, bass.ds(t0, HT)]).then_inc(idx_step, 1)
                own(idx_step, n * 4 + 2)
                V.tensor_scalar(diff, srcf, -1.0, dump_i[:, 0:1], ALU.mult, ALU.add).then_inc(idx_step, 1)
                own(idx_step, n * 4 + 3)
                V.tensor_tensor(diff2, first, diff, ALU.mult).then_inc(idx_step, 1)
                own(idx_step, n * 4 + 4)
                if not (isinstance(g, int) and g == 0):
                    for k in range(NTAB):
                        dve.wait_ge(scattered[k], scatters_through(k, h, g - 1) * 16)
                V.tensor_tensor(sidx[h].bitcast(I32), diff2, srcf, ALU.add).then_inc(sidx_made[h], 1)

            def messages(g, h):
                n = g * 2 + h
                t0 = g * (2 * HT) + h * HT
                dve.wait_ge(hg_taken, n + 1)
                dve.wait_ge(gate_mm[h], g + 1)
                m = msg
                V.tensor_tensor(uv, u_s[h], hg[:, :, H + 1:UW], ALU.mult).then_inc(msg_step, 1)
                own(msg_step, n * 11 + 1)
                V.tensor_reduce(adp, uv, AX.X, ALU.add).then_inc(msg_step, 1)
                own(msg_step, n * 11 + 2)
                for k0, c, v in gate_runs:
                    V.tensor_tensor(m[:, k0:k0 + c, 0:H], v, bc(adp[:, k0:k0 + c], H), ALU.add).then_inc(msg_step, 1)
                own(msg_step, n * 11 + 6)
                V.tensor_tensor(m[:, :, 0:H], m[:, :, 0:H], hg[:, :, 0:H], ALU.mult).then_inc(msg_step, 1)
                V.tensor_copy(m[:, :, H], hg[:, :, H])
                own(msg_step, n * 11 + 7)
                V.tensor_tensor(m[:, :, 0:H], m[:, :, 0:H], bc(cw_c[:, bass.ds(t0, HT)], H), ALU.mult).then_inc(msg_step, 1)
                own(msg_step, n * 11 + 8)
                wait(dve, summed[h], g)
                p = [msg_p[h][:, :, c * (H + 1):(c + 1) * (H + 1)] for c in range(3)]
                V.tensor_copy(p[0], m).then_inc(msg_step, 1)
                own(msg_step, n * 11 + 9)
                V.tensor_tensor(msg_r, m, p[0], ALU.subtract).then_inc(msg_step, 1)
                own(msg_step, n * 11 + 10)
                V.tensor_copy(p[1], msg_r).then_inc(msg_step, 1)
                own(msg_step, n * 11 + 11)
                V.tensor_tensor(p[2], msg_r, p[1], ALU.subtract).then_inc(msg_made[h], 1)

            def third(g, first=False, last=False):
                for h in range(2):
                    if h == 1:
                        messages(g, 0)
                        if not last:
                            turned_one_hots(g + 1, 0)
                    else:
                        if not first:
                            messages(g - 1, 1)
                        turned_one_hots(g, 1)
                    equals(g, h)
                    if h == 1:
                        targets(g, 0)
                    elif not first:
                        targets(g - 1, 1)

            turned_one_hots(0, 0)
            third(0, first=True)
            with dve.Fori(1, LOOPS - 1) as g:
                third(g)
            third(LOOPS - 1, last=True)
            messages(LOOPS - 1, 1)
            targets(LOOPS - 1, 1)
            for k in range(NTAB):
                dve.wait_ge(sums_in[k % 2], 16 * (k // 2 + 1))
                if k == 0:
                    V.tensor_copy(agg, ld[0]).then_inc(sums_added, 1)
                else:
                    V.tensor_tensor(agg, agg, ld[k % 2], ALU.add).then_inc(sums_added, 1)
                dve.wait_ge(sums_added, k + 1)
            ts(st[:, 4, :], agg[:, :, H], 1e-8, ALU.max)
            step(V.reciprocal(st[:, 5, :], st[:, 4, :]))
            tt(ta, agg[:, :, 0:H], bc(st[:, 5, :], H), ALU.mult)
            V.engine_nop().then_inc(sums_used, 1)
            tt(ta, ta, X[:, :, :], ALU.add)
            layernorm(ta, tb, tc, gam[:, :], bet[:, :])
            tt(ta, tb, X[:, :, :], ALU.add)
            layernorm(ta, X[:, :, :], tb)
            V.engine_nop().then_inc(cat_made, 1)
            V.tensor_copy(st[:, 1, :], deg[:, :]).then_inc(sqrt_in, 1)
            n_norm[0] += 1
            dve.wait_ge(sqrt_out, n_norm[0])
            step(V.reciprocal(dinv[:, :], st[:, 2, :]))
            dve.wait_ge(conv_done, 3)
            for b in range(5):
                n = min(10, NT - 10 * b)
                tt(HN[:, 10 * b:10 * b + n, :], conv_ps[b][:, 0:n, :], bc(dinv[:, 10 * b:10 * b + n], H), ALU.mult)
            table_rows(HN[:, :, :])
            V.engine_nop().then_inc(rows_made, 1)
            take_products(2)
            tt(ta, ACC[:, 0:NT, 0:H], HN[:, :, :], ALU.add)
            tt(ta, ta, bc(dinv[:, :], H), ALU.mult)
            tt(ta, ta, bm(b3b[:, :], NT), ALU.add)
            tt(ta, ta, X[:, :, :], ALU.add)
            layernorm(ta, X[:, :, :], tb)
            V.engine_nop().then_inc(out_made, 1)


_INS = ["x_n", "dst_r", "dst_c", "src_c", "src_f", "e1_r", "ew_c", "attr_t", "z_f", "nv_n",
        "emb_t", "emb", "adapt_t", "w_rel1", "w_root1", "b1", "w_rel2", "w_root2", "b2",
        "m_w1t", "m_b1", "m_w2t", "m_b2", "gamma", "beta", "w3", "b3"]


def kernel(**inputs):
    import numpy as _np
    import concourse.bacc as _bacc
    from concourse import mybir as _mybir
    from concourse.bass_utils import run_bass_kernel_spmd as _run

    def arr(name):
        return _np.asarray(inputs[name])

    def pad(a, n, fill=0):
        return _np.concatenate([a, _np.full((n - a.shape[0],) + a.shape[1:], fill, a.dtype)])

    dst, src = pad(arr("dst"), EP, PADN), pad(arr("src"), EP, PADN)
    lay = {
        "x_n": pad(arr("x"), NP).reshape(NT, P, H).transpose(1, 0, 2),
        "dst_r": dst.reshape(Q, W), "dst_c": dst.reshape(T, P).T, "src_c": src.reshape(T, P).T,
        "src_f": src,
        "e1_r": pad(arr("edge_weight1")[:, 0], EP).reshape(Q, W),
        "ew_c": pad(arr("edge_weight"), EP).reshape(T, P).T,
        "attr_t": pad(arr("edge_attr_40"), EP).T,
        "z_f": pad(arr("node_type_119"), NP), "nv_n": pad(arr("node_vec"), NP).reshape(NT, P).T,
        "emb_t": arr("L2_gnn_emb").T, "emb": arr("L2_gnn_emb"), "adapt_t": arr("L2_gnn_adaptW").T,
        "w_rel1": arr("L1_gnn_w_rel1"), "w_root1": arr("L1_gnn_w_root1"), "b1": arr("L1_gnn_b1"),
        "w_rel2": arr("L1_gnn_w_rel2"), "w_root2": arr("L1_gnn_w_root2"), "b2": arr("L1_gnn_b2"),
        "m_w1t": arr("L2_gnn_W1").T, "m_b1": arr("L2_gnn_b1"), "m_w2t": arr("L2_gnn_W2").T,
        "m_b2": arr("L2_gnn_b2"), "gamma": arr("L2_gnn_gamma"), "beta": arr("L2_gnn_beta"),
        "w3": arr("L3_gnn_W"), "b3": arr("L3_gnn_b"),
    }
    nc = _bacc.Bacc("TRN2", target_bir_lowering=False, num_devices=1)
    arrays, args = {}, []
    for name in _INS:
        a = _np.ascontiguousarray(lay[name])
        arrays[f"in_{name}_dram"] = a
        args.append(nc.dram_tensor(f"in_{name}_dram", a.shape, _mybir.dt.from_np(a.dtype), kind="ExternalInput").ap())
    args.append(nc.dram_tensor("out_0_dram", (N, H), _mybir.dt.float32, kind="ExternalOutput").ap())
    build(nc, *args)
    r = _run(nc, [arrays], core_ids=[0])
    return r.results[0]["out_0_dram"]
```

```python
from contextlib import ExitStack

import concourse.bass as bass
from concourse import mybir

F32 = mybir.dt.float32
I32 = mybir.dt.int32
U32 = mybir.dt.uint32
BF16 = mybir.dt.bfloat16
F16 = mybir.dt.float16
ALU = mybir.AluOpType
ACT = mybir.ActivationFunctionType
AX = mybir.AxisListType

P = 128
H = 48
N = 6250
NT = -(-N // P)
NP = NT * P
HT = 13
LOOPS = 62
T = 2 * HT * LOOPS
EP = T * P
Q = 124
W = EP // Q
HE = HT * P
NEL = 119
G = 32
R = 40
CUTOFF = 6.0
EPS = 1e-5
BIG = 1e30
NTAB = 5
TROWS = NP + P
UW = H + 1 + G
DW = 10
SUMS_STEP = 2
DH = 64
OW = P + DH
AR = DH + DW - 1
WN = DW * NT
AB = 4
AW = H + 2
PADN = NP - 1
PT = 7
PC = PT * P
LN3 = 1.0986122886681098
PI = 3.141592653589793


def build(nc, x_n, dst_r, dst_c, src_c, src_f, e1_r, e1_c, ew_c, attr_t, z_f, nv_n,
          emb_t, emb, adapt_t, w_rel1, w_root1, b1, w_rel2, w_root2, b2,
          m_w1t, m_b1, m_w2t, m_b2, gamma, beta, w3, b3, out):
    xu_tab = nc.dram_tensor("xu_tab", [NP, UW], F32).ap()
    u_edges = nc.dram_tensor("u_edges", [2 * LOOPS, P, HT * G], F32).ap()
    adj = nc.dram_tensor("adj", [P, (NP + DH) * NT], BF16).ap()
    rel_f = nc.dram_tensor("rel_f", [Q, W], BF16).ap()
    sums = [nc.dram_tensor(f"sums{k}", [TROWS, H + 1], F32).ap() for k in range(NTAB)]
    max_tab = nc.dram_tensor("max_tab", [NP, 1], F32).ap()
    row_tab = nc.dram_tensor("row_tab", [NP, H], F32).ap()
    hmv_tab = nc.dram_tensor("hmv_tab", [NP, UW], F32).ap()
    hg_edges = nc.dram_tensor("hg_edges", [2 * LOOPS, P, HT * UW], F32).ap()

    with ExitStack() as ctx:
        def sb(name, shape, dt=F32):
            return ctx.enter_context(nc.sbuf_tensor(name, shape, dt))

        def sem(name):
            return ctx.enter_context(nc.semaphore(name))

        X = sb("X", [P, NT, H])
        HN = sb("HN", [P, NT, H])
        hmv_words = sb("hmv_words", [P, (NT + 1) * 3 * UW // 2])
        HMV_flat = hmv_words[:, :].bitcast(BF16)
        HMV = HMV_flat.rearrange("p (a c b) -> p a c b", c=3, b=UW)
        ACC = sb("ACC", [P, NT + 1, AW])
        rel_c = sb("rel_c", [P, T])
        ex_c = sb("ex_c", [P, T])
        cw_c = sb("cw_c", [P, T])
        src_i = sb("src_i", [P, T + 2 * HT], I32)
        hoff = sb("hoff", [1, Q], I32)
        coff = sb("coff", [1, Q], I32)
        acol = sb("acol", [1, Q], I32)
        hcol = sb("hcol", [1, Q + 1], I32)
        deg = sb("deg", [P, NT])
        dinv = sb("dinv", [P, NT])
        nv = sb("nv", [P, NT])
        iota_f = sb("iota_f", [P, 2 * P])
        iota_p = sb("iota_p", [P, 2])
        dump_i = sb("dump_i", [P, 1])
        ident = sb("ident", [P, P])
        ident_b = sb("ident_b", [P, P], BF16)
        zero = sb("zero", [P, 512])
        iota_b = sb("iota_b", [P, 2 * P], BF16)
        rank_w = sb("rank_w", [P, 2])
        rank_b = sb("rank_b", [P, 1], BF16)
        rank_c = sb("rank_c", [P, 1])
        wcat = sb("wcat", [P, 2, H])
        w1t = sb("w1t", [2 * R, 2 * H])
        b1c = sb("b1c", [2 * H, 1])
        w2b = sb("w2b", [2 * H + 1, 2 * H])
        w3s = sb("w3s", [H, H])
        b3b = sb("b3b", [P, H])
        gam = sb("gam", [P, H])
        bet = sb("bet", [P, H])
        st = sb("st", [P, 6, NT])
        iota_i = sb("iota_i", [P, 2 * P], I32)
        ip_i = sb("ip_i", [P, 2], I32)
        ev = sb("ev", [NEL, 2 * G])
        embt = sb("embt", [G, NEL])
        adt = sb("adt", [G, G])
        half_pi = sb("half_pi", [P, 1])
        row_ends = sb("row_ends", [Q, 2])
        prev_i = sb("prev_i", [Q, 1], I32)
        next_i = sb("next_i", [Q, 1], I32)
        prev_f = sb("prev_f", [Q, 1])
        next_f = sb("next_f", [Q, 1])
        pen = sb("pen", [Q, 3])
        carry = sb("carry", [Q, 4])
        crow = sb("crow", [1, 4, Q])
        cst = sb("cst", [1, 2, Q])
        cscan = sb("cscan", [1, 2, Q])
        cin = sb("cin", [Q, 2])
        base_r = sb("base_r", [Q, 1], I32)
        base_c = sb("base_c", [P, Q], I32)
        rel_r = sb("rel_r", [Q, W], BF16)
        bad = sb("bad", [P, 8])
        bad_1 = sb("bad_1", [P, 1])
        flag = sb("flag", [1, 1], I32)
        to_dump = sb("to_dump", [P, HT])[:, :]
        moved = sb("moved", [P, HT])[:, :]
        sum_row = rel_c[:, :]
        ACC_flat = ACC[:, :, :].rearrange("p a b -> p (a b)")
        WORK = 28270
        work = sb("work", [P, WORK])

        def carve(at, rows, *shape):
            n = 1
            for s in shape:
                n *= s
            assert at[0] + n <= WORK, (at[0] + n, WORK)
            v = work[0:rows, at[0]:at[0] + n]
            at[0] += n
            if len(shape) == 2:
                v = v.rearrange("p (a b) -> p a b", b=shape[1])
            if len(shape) == 3:
                v = v.rearrange("p (a b c) -> p a b c", b=shape[1], c=shape[2])
            return v

        a = [0]
        g_idx_s = carve(a, P, 1)
        g_zero = carve(a, P, 1)
        g_rows = carve(a, P, UW)
        g_wrows = carve(a, P, AW)
        g_e1 = carve(a, P, T)
        g_dst_i = carve(a, P, T)
        g_dst = carve(a, P, T)
        g_src = carve(a, P, T)
        g_nodes = carve(a, P, NP)
        g_node_c = carve(a, P, NT)
        g_max = carve(a, P, NT)
        g_max_q = carve(a, P, NT)
        at_oh = a[0]
        g_oh = carve(a, P, NP)
        g_hmv = carve([at_oh], P, NT, UW)
        a = [at_oh]
        g_dst_b = carve(a, P, W)
        g_e1_b = carve(a, P, W)
        g_pen = carve(a, P, W)
        ps = ctx.enter_context(nc.psum_tensor("ps", [P, 8 * 512], F32))

        a = [0]
        dr_i = carve(a, Q, W)
        dr_f = carve(a, Q, W)
        e1_s = carve(a, Q, W)
        rst_f = carve(a, Q, W)
        rst_b = carve(a, Q, W)
        mx_f = carve(a, Q, W)
        mx_b = carve(a, Q, W)
        v_rest = work[:, 0:NT * G].rearrange("p (a b) -> p a b", b=G)
        base_i = carve(a, P, T)
        dc_i = carve(a, P, T)
        tmp_c = ACC_flat[:, 0:T]
        ohz = carve(a, NEL, NP)
        z_b = ohz
        xu = hmv_words[:, 0:NT * UW].rearrange("p (a b) -> p a b", b=UW)
        prep_end = a[0]
        a = [0]
        a = [0]
        idx_st = carve(a, P, 2, HT)
        G_ring = carve(a, P, 2, HT, UW)
        oh = carve(a, P, 2 * HT, P).bitcast(BF16)
        gw = [carve(a, P, HT, H + 1) for _ in range(2)]
        gw_r = carve(a, P, HT, H + 1)
        gw_p = [carve(a, P, HT, 74).bitcast(BF16) for _ in range(2)]
        fold_s = [carve(a, P, 2, AW) for _ in range(2)]
        win_s = carve(a, P, 2, HT)
        low_s = carve(a, P, 2, HT)
        iota_h = carve(a, P, WN // 2).bitcast(F16)
        win_oh = [carve(a, P, HT, WN // 2).bitcast(BF16) for _ in range(2)]
        low_oh = [carve(a, P, HT, P // 2).bitcast(BF16) for _ in range(2)]
        piece = [carve(a, P, AR * NT // 2 + 1).bitcast(BF16) for _ in range(2)]
        a = [max(a[0], prep_end)]
        win_c = carve(a, P, T + 2 * HT)
        low_c = carve(a, P, T + 2 * HT)
        toff = carve(a, 1, T).bitcast(I32)
        a = [0]
        attr_s = [carve(a, 2 * R, PC) for _ in range(2)]
        src_b = [carve(a, P, HT, P) for _ in range(2)]
        rel_b = [carve(a, P, HE // 2).bitcast(BF16) for _ in range(2)]
        oh_t = [carve(a, P, 2, HE // 2).bitcast(BF16) for _ in range(2)]
        hwin = [carve(a, P, 3 * UW).bitcast(BF16) for _ in range(2)]
        eq = [carve(a, P, HT, P // 2).bitcast(BF16) for _ in range(2)]
        s1t = [carve(a, 2 * H + 1, PC) for _ in range(2)]
        hg = [carve(a, P, HT, UW) for _ in range(2)]
        gate = [carve(a, P, HT, H) for _ in range(2)]
        u_s = [carve(a, P, HT, G) for _ in range(2)]
        uv = carve(a, P, HT, G)
        adp = carve(a, P, HT)
        msg = carve(a, P, HT, H + 1)
        msg_r = carve(a, P, HT, H + 1)
        msg_p = [carve(a, P, HT, 74).bitcast(BF16) for _ in range(2)]
        smm = [carve(a, P, HT, H + 2) for _ in range(2)]
        first = carve(a, P, HT)
        srcf = carve(a, P, HT)
        sidx = [carve(a, P, HT) for _ in range(2)]
        a = [0]
        parts = carve(a, P, NT, 3 * H // 2).bitcast(BF16)
        cat = carve(a, P, NT, 2 * H + 1)
        cat_t = carve([a[0]], P, NT, P)
        t_at = [a[0]]
        ta = carve(t_at, P, NT, H)
        tb = carve(t_at, P, NT, H)
        edge_a, edge_b = cat_t[:, :, :].rearrange("p a b -> p (a b)")[:, 0:T], cat_t[:, :, :].rearrange("p a b -> p (a b)")[:, T:2 * T]
        a[0] += NT * P
        l_at = [a[0]]
        blocks = [carve(a, P, P * NT // 2).bitcast(BF16).rearrange("p (d a) -> p d a", a=NT) for _ in range(AB)]
        agg = carve(l_at, P, NT, H + 1)
        ld = [carve(l_at, P, NT, H + 1) for _ in range(2)]
        tc = cat[:, :, 0:H]

        def pair(name):
            return [sem(f"{name}0"), sem(f"{name}1")]

        edges_init = sem("edges_init")
        rank_arg = sem("rank_arg")
        rank_made = sem("rank_made")
        gw_step = sem("gw_step")
        edge_ends = sem("edge_ends")
        pool_turn = sem("pool_turn")
        idx_step = sem("idx_step")
        msg_step = sem("msg_step")
        edges_loaded = sem("edges_loaded")
        types_loaded = sem("types_loaded")
        emb_loaded = sem("emb_loaded")
        prep_loaded = sem("prep_loaded")
        wts_loaded = sem("wts_loaded")
        consts_made = sem("consts_made")
        rel_rows_made = sem("rel_rows_made")
        rel_stored = sem("rel_stored")
        zeros_made = sem("zeros_made")
        tabs_zeroed = sem("tabs_zeroed")
        ohz_made = sem("ohz_made")
        ev_mm = sem("ev_mm")
        ev_made = sem("ev_made")
        uv_mm = sem("uv_mm")
        uv_taken = sem("uv_taken")
        carry_out = sem("carry_out")
        carry_rows = sem("carry_rows")
        carry_scanned = sem("carry_scanned")
        carry_back = sem("carry_back")
        shifted = sem("shifted")
        exp_made = sem("exp_made")
        ex_turned = sem("ex_turned")
        ex_taken = sem("ex_taken")
        cos_arg = sem("cos_arg")
        cos_made = sem("cos_made")
        stage_step = sem("stage_step")
        win_ready = pair("win_ready")
        win_mm = sem("win_mm")
        win_taken = sem("win_taken")
        cleared = sem("cleared")
        carried = sem("carried")
        adj_stored = sem("adj_stored")
        store_turn = sem("store_turn")
        piece_done = sem("piece_done")
        first_pass_over = sem("first_pass_over")
        block_in = [sem(f"block_in{r}") for r in range(AB)]
        block_used = sem("block_used")
        block_summed = sem("block_summed")
        fold_step = sem("fold_step")
        hwin_made = pair("hwin_made")
        xu_made = sem("xu_made")
        xu_stored = sem("xu_stored")
        sqrt_in = sem("sqrt_in")
        sqrt_out = sem("sqrt_out")
        elu_in = sem("elu_in")
        elu_out = sem("elu_out")
        cat_made = sem("cat_made")
        cat_turned = sem("cat_turned")
        cat_taken = sem("cat_taken")
        conv_done = sem("conv_done")
        rows_made = sem("rows_made")
        hmv_made = sem("hmv_made")
        s1_ones = sem("s1_ones")
        sums_used = sem("sums_used")
        sums_added = sem("sums_added")
        sums_in = [sem("sums_in0"), sem("sums_in1")]
        out_made = sem("out_made")
        out_stored = sem("out_stored")
        dve_step = sem("dve_step")

        flag_made = sem("flag_made")
        g_ready = sem("g_ready")
        g_iota = sem("g_iota")
        g_in = sem("g_in")
        g_seg_in = sem("g_seg_in")
        g_seg_used = sem("g_seg_used")
        g_max_made = sem("g_max_made")
        g_args = sem("g_args")
        g_exps = sem("g_exps")
        g_tab = sem("g_tab")
        g_step = sem("g_step")
        g_max_step = sem("g_max_step")
        g_hg_in = sem("g_hg_in")
        g_turn = sem("g_turn")
        g_loops = [{s: sem(f"g_{s}{m}") for s in ("idx", "row") + (("oh", "mm") if m not in (0, 4) else ()) + (("st",) if m in (1, 4) else ())}
                   for m in range(6)]
        idx_ready = pair("idx_ready")
        gathered = pair("gathered")
        used = pair("used")
        oh_ready = pair("oh_ready")
        u_free = [sem("u_free0"), sem("u_free1")]
        u_stored = [sem("u_stored0"), sem("u_stored1")]

        e_in = pair("e_in")
        z_mm = sem("z_mm")
        z_used = pair("z_used")
        silu_done = sem("silu_done")
        oht_made = pair("oht_made")
        picked = pair("picked")
        hg_taken = sem("hg_taken")
        eq_made = pair("eq_made")
        gate_mm = pair("gate_mm")
        gates_taken = sem("gates_taken")
        u_in = pair("u_in")
        msg_made = pair("msg_made")
        summed = pair("summed")
        smm_taken = sem("smm_taken")
        sidx_made = pair("sidx_made")
        scattered = [sem(f"scattered{k}") for k in range(NTAB)]

        TABLES_ZEROED = 16 * 5 * NTAB
        G_MAX, G_FIRST, G_TARGETS = 0, 1, 4
        CH = PC // 2
        TAIL = -(-(NP + DH - N) * NT // 1024)

        def wait(eng, s, v):
            if not (isinstance(v, int) and v <= 0):
                eng.wait_ge(s, v)

        def bc(ap, n):
            return ap.unsqueeze(2).to_broadcast([ap.shape[0], ap.shape[1], n])

        def bm(ap, n):
            return ap.unsqueeze(1).to_broadcast([ap.shape[0], n, ap.shape[1]])

        def scatters_before(s, g):
            k = s % NTAB
            per = len(range(k, 2 * HT, NTAB))
            return g * per + s // NTAB

        def scatters_through(k, h, g):
            per = len(range(k, 2 * HT, NTAB))
            return g * per + len(range(k, (h + 1) * HT, NTAB))

        z_ps = [ps[0:2 * H, 512 * b:512 * b + CH] for b in (3, 7)]

        def ps_run(bank, off, n, w):
            c = 512 * bank + off
            return ps[:, c:c + n * w].rearrange("p (a b) -> p a b", b=w)

        gate_pairs = [(ps_run(3, 0, 5, 2 * H) if q < 5 else ps_run(7, 0, 2, 2 * H))[:, q % 5, :] for q in range(PT)]
        gate_runs = [(0, 5, ps_run(3, 0, 5, 2 * H)[:, :, 0:H]), (5, 2, ps_run(7, 0, 2, 2 * H)[:, :, 0:H]),
                     (7, 4, ps_run(3, 0, 5, 2 * H)[:, 1:5, H:2 * H]), (11, 2, ps_run(7, 0, 2, 2 * H)[:, :, H:2 * H])]
        sum_runs = [(0, 10, ps_run(4, 0, 10, H + 2)), (10, 3, ps_run(1, 0, 3, H + 2))]
        pick_runs = [(0, 6, ps_run(5, 0, 6, UW)), (6, 6, ps_run(6, 0, 6, UW)), (12, 1, ps_run(2, 0, 1, UW))]

        def slot(runs, k):
            for k0, n, v in runs:
                if k0 <= k < k0 + n:
                    return v[:, k - k0, :]

        g_sums = ps[:, 0:NT * 64].rearrange("p (i c) -> p i c", c=64)
        part_sums = [ps[:, 1024 * h:1024 * (h + 1)].rearrange("p (w c) -> p w c", c=512) for h in range(2)]
        win_ps = [ps[:, 512 * (4 + j):512 * (4 + j) + WN] for j in range(4)]

        def window_bank(j):
            return {HT - 2: 0, HT - 1: 3}.get(j, j % 4)

        uv_ps = ps[:, 0:NT * 2 * G].rearrange("p (i c) -> p i c", c=2 * G)
        conv_ps = [ps[:, 512 * (3 + b):512 * (3 + b) + 10 * H].rearrange("p (a b) -> p a b", b=H) for b in range(5)]

        def read_flag(eng):
            eng.wait_ge(flag_made, 1)
            return eng.value_load(flag[0:1, 0:1], min_val=0, max_val=1)

        block = ctx.enter_context(nc.Block())

        @block.sync
        def _(sp):
            for dst, src in ((dr_i.bitcast(I32), dst_r), (e1_s, e1_r), (dc_i.bitcast(I32), dst_c),
                             (base_i.bitcast(I32), dst_c[0:1, :].to_broadcast([P, T])), (src_i[:, 0:T], src_c)):
                sp.dma_start(dst, src).then_inc(edges_loaded, 16)
            sp.dma_start(z_b.bitcast(I32), z_f.unsqueeze(0).to_broadcast([NEL, NP])).then_inc(types_loaded, 16)
            sp.wait_ge(edges_init, 1)
            with nc.allow_non_contiguous_dma(reason="one element per row, once"):
                sp.dma_start(prev_i[1:Q, :], dst_r[0:Q - 1, W - 1:W]).then_inc(edge_ends, 16)
                sp.dma_start(next_i[0:Q - 1, :], dst_r[1:Q, 0:1]).then_inc(edge_ends, 16)
            for dst, src in ((ev[:, 0:G], emb), (embt[:, :], emb_t), (adt[:, :], adapt_t)):
                sp.dma_start(dst, src).then_inc(emb_loaded, 16)
            for dst, src in ((X[:, :, :], x_n), (nv[:, :], nv_n), (cw_c[:, :], ew_c)):
                sp.dma_start(dst, src).then_inc(prep_loaded, 16)
            for dst, src in ((wcat[0:H, 0, :], w_rel1), (wcat[H:2 * H, 0, :], w_root1), (wcat[2 * H:2 * H + 1, 0, :], b1.unsqueeze(0)),
                             (wcat[0:H, 1, :], w_rel2), (wcat[H:2 * H, 1, :], w_root2), (wcat[2 * H:2 * H + 1, 1, :], b2.unsqueeze(0)),
                             (w1t[0:R, 0:H], m_w1t), (w1t[R:2 * R, H:2 * H], m_w1t),
                             (b1c[0:H, :], m_b1.unsqueeze(1)), (b1c[H:2 * H, :], m_b1.unsqueeze(1)),
                             (w2b[0:H, 0:H], m_w2t), (w2b[H:2 * H, H:2 * H], m_w2t),
                             (w2b[2 * H:2 * H + 1, 0:H], m_b2.unsqueeze(0)), (w2b[2 * H:2 * H + 1, H:2 * H], m_b2.unsqueeze(0)),
                             (w3s[:, :], w3), (b3b[:, :], b3.unsqueeze(0).to_broadcast([P, H])),
                             (gam[:, :], gamma.unsqueeze(0).to_broadcast([P, H])), (bet[:, :], beta.unsqueeze(0).to_broadcast([P, H]))):
                sp.dma_start(dst, src).then_inc(wts_loaded, 16)
            sp.wait_ge(rel_rows_made, 1)
            sp.dma_start(rel_f, rel_r[:, :]).then_inc(rel_stored, 16)
            sp.wait_ge(zeros_made, 1)
            for k in range(NTAB):
                flat = sums[k].rearrange("(p a) f -> p (a f)", p=P)
                for c in range(5):
                    sp.dma_start(flat[:, c * 490:(c + 1) * 490], zero[:, 0:490]).then_inc(tabs_zeroed, 16)
            sp.wait_ge(xu_made, 1)
            sp.dma_start(xu_tab.rearrange("(i p) f -> p i f", p=P), xu).then_inc(xu_stored, 16)
            for k in range(TAIL):
                c = N * NT + k * 1024
                n = min(1024, (NP + DH) * NT - c)
                sp.dma_start(adj[:, c:c + n], zero[:, :].bitcast(BF16)[:, 0:n]).then_inc(adj_stored, 16)
            path = read_flag(sp)
            with sp.If(path < 1):
                sp.sem_inc(u_free[0], 1)
                sp.sem_inc(u_free[1], 1)
                with sp.Fori(0, LOOPS) as g:
                    for h in range(2):
                        sp.wait_ge(gathered[h], (g + 1) * (16 * HT))
                        sp.dma_start(u_edges[bass.ds(g * 2 + h, 1)].rearrange("a p f -> (a p) f").rearrange("p (k f) -> p k f", f=G),
                                     G_ring[:, h, :, H + 1:UW]).then_inc(u_stored[h], 16)
                        sp.wait_ge(u_stored[h], (g + 1) * 16)
                        sp.sem_inc(u_free[h], 1)
                        c = sp.value_load(hoff[0:1, bass.ds(g * 2 + h, 1)], min_val=0, max_val=(N - 1) * NT)
                        sp.wait_ge(piece_done, g * 2 + (h + 1))
                        sp.sem_inc(store_turn, 1)
                        sp.wait_ge(adj_stored, g * 32 + (16 * (TAIL + h)))
                        sp.sem_inc(store_turn, 1)
                        sp.dma_start(adj[:, bass.ds(c, DH * NT)], piece[h][:, 0:DH * NT]).then_inc(adj_stored, 16)
                sp.wait_ge(u_stored[0], 16 * LOOPS)
                sp.wait_ge(u_stored[1], 16 * LOOPS)

                def load_blocks(k):
                    def load(i, r):
                        use = k * NT + i
                        wait(sp, block_used, use - AB + 1)
                        sp.sem_inc(store_turn, 1)
                        sp.dma_start(blocks[r], adj[:, bass.ds(i * (P * NT), P * NT)].rearrange("p (d a) -> p d a", a=NT)
                                     ).then_inc(block_in[r], 16)
                    for i in range(AB):
                        load(i, (k * NT + i) % AB)
                    with sp.Fori(1, NT // AB) as s:
                        for r in range(AB):
                            load(s * AB + r, (k * NT + r) % AB)
                    for i in range(NT // AB * AB, NT):
                        load(i, (k * NT + i) % AB)

            with sp.If(path < 1):
                sp.wait_ge(first_pass_over, 1)
                load_blocks(0)
                load_blocks(1)

            def store_rows(m, dst_rows, c0, c1):
                sp.sem_inc(g_loops[m]["st"], 16)
                with sp.Fori(0, 2 * LOOPS) as q:
                    for j in range(HT):
                        sp.wait_ge(g_loops[m]["row"], q * (16 * HT) + 16 * (j + 1))
                        sp.sem_inc(store_turn, 1)
                        sp.dma_start(dst_rows[bass.ds(q, 1)].rearrange("a p f -> (a p) f")[:, j * (c1 - c0):(j + 1) * (c1 - c0)],
                                     g_rows[:, c0:c1]).then_inc(g_loops[m]["st"], 16)

            def general_rows(n, table, rows):
                sp.wait_ge(g_ready, n)
                sp.dma_start(table.rearrange("(i p) f -> p i f", p=P), rows).then_inc(g_tab, 16)
                sp.dma_start(g_dst_i.bitcast(I32), dst_c).then_inc(g_in, 16)

            with sp.If(path > 0):
                sp.wait_ge(g_ready, 1)
                sp.dma_start(g_dst_i.bitcast(I32), dst_c).then_inc(g_in, 16)
                sp.dma_start(g_e1, e1_c).then_inc(g_in, 16)
                with sp.Fori(0, Q) as q:
                    sp.wait_ge(g_seg_used, q + 1)
                    sp.sem_inc(store_turn, 1)
                    sp.dma_start(g_dst_b.bitcast(I32), dst_r[bass.ds(q, 1), :].to_broadcast([P, W])).then_inc(g_seg_in, 16)
                    sp.dma_start(g_e1_b, e1_r[bass.ds(q, 1), :].to_broadcast([P, W])).then_inc(g_seg_in, 16)
                sp.wait_ge(g_max_made, 1)
                with nc.allow_non_contiguous_dma(reason="one element per node, once"):
                    sp.dma_start(max_tab.rearrange("(i p) f -> p i f", p=P), g_max.unsqueeze(2)).then_inc(g_tab, 16)
                store_rows(G_FIRST, u_edges, H + 1, UW)
                general_rows(3, row_tab, X[:, :, :])
                general_rows(4, row_tab, HN[:, :, :])
                general_rows(5, hmv_tab, g_hmv)
                store_rows(G_TARGETS, hg_edges, 0, UW)
            sp.wait_ge(rel_stored, 16)
            sp.wait_ge(hmv_made, 1)

            def edge_loads(g, h):
                n0 = g * (2 * HE) + h * HE
                wait(sp, z_used[h], g)
                wait(sp, eq_made[h], g)
                wait(sp, oht_made[h], g)
                sp.dma_start(attr_s[h][0:R, :], attr_t[:, bass.ds(n0, PC)]).then_inc(e_in[h], 16)
                sp.dma_start(attr_s[h][R:2 * R, :], attr_t[:, bass.ds(n0 + (HE - PC), PC)]).then_inc(e_in[h], 16)
                sp.dma_start(src_b[h].rearrange("p a b -> p (a b)").bitcast(I32),
                             src_f[bass.ds(n0, HE)].unsqueeze(0).to_broadcast([P, HE])).then_inc(e_in[h], 16)
                sp.dma_start(rel_b[h], rel_f.rearrange("q w -> (q w)")[bass.ds(n0, HE)].unsqueeze(0).to_broadcast([P, HE])).then_inc(e_in[h], 16)

            def u_loads(g, h):
                wait(sp, msg_made[h], g)
                if not isinstance(g, int):
                    sp.sem_inc(store_turn, 1)
                sp.dma_start(u_s[h].rearrange("p a b -> p (a b)"),
                             u_edges[bass.ds(g * 2 + h, 1)].rearrange("a p f -> (a p) f")).then_inc(u_in[h], 16)

            edge_loads(0, 0)
            u_loads(0, 0)
            edge_loads(0, 1)
            u_loads(0, 1)
            with sp.Fori(1, LOOPS) as g:
                edge_loads(g, 0)
                u_loads(g, 0)
                edge_loads(g, 1)
                u_loads(g, 1)
            for k in range(NTAB):
                sp.wait_ge(scattered[k], 16 * scatters_before(k, LOOPS))
            sp.wait_ge(msg_made[1], LOOPS)
            for k in range(NTAB):
                if k >= 2:
                    sp.wait_ge(sums_added, k - 1)
                sp.dma_start(ld[k % 2], sums[k][0:NP, :].rearrange("(p i) f -> p i f", p=P)).then_inc(sums_in[k % 2], 16)
            with sp.If(path < 1):
                sp.wait_ge(sums_used, 1)
                load_blocks(2)
            with sp.If(path > 0):
                general_rows(6, row_tab, HN[:, :, :])
            sp.wait_ge(out_made, 1)
            full = N // P
            sp.dma_start(out[0:full * P, :].rearrange("(i p) f -> p i f", p=P), X[:, 0:full, :]).then_inc(out_stored, 16)
            sp.dma_start(out[full * P:N, :], X[0:N - full * P, full, :]).then_inc(out_stored, 16)
            sp.wait_ge(out_stored, 32)

        @block.gpsimd
        def _(pool):
            nc.gpsimd.iota(iota_i[:, :], [[1, 2 * P]], base=0, channel_multiplier=0).then_inc(consts_made, 1)
            nc.gpsimd.iota(ip_i[:, :], [[P, 2]], base=0, channel_multiplier=1).then_inc(consts_made, 1)

            def first_gathers():
                pool.wait_ge(xu_stored, 16)
                with pool.Fori(0, LOOPS) as g:
                    for h in range(2):
                        pool.wait_ge(idx_ready[h], g + 1)
                        pool.wait_ge(used[h], g + 1)
                        pool.wait_ge(u_free[h], g + 1)
                        pool.sem_inc(pool_turn, 1)
                        for j in range(HT):
                            pool.indirect_dma_start(G_ring[:, h, j, :], None, xu_tab,
                                                    bass.IndirectOffsetOnAxis(ap=idx_st.bitcast(U32)[:, h, j:j + 1], axis=0)
                                                    ).then_inc(gathered[h], 16)

            path = read_flag(pool)
            with pool.If(path < 1):
                first_gathers()

            def general_gathers(m, table, width, tables):
                pool.wait_ge(g_tab, 16 * tables)
                with pool.Fori(0, T) as t:
                    pool.wait_ge(g_loops[m]["idx"], t + 1)
                    pool.sem_inc(pool_turn, 1)
                    pool.indirect_dma_start(g_rows[:, 0:width], None, table,
                                            bass.IndirectOffsetOnAxis(ap=g_idx_s.bitcast(U32), axis=0)).then_inc(g_loops[m]["row"], 16)

            def node_numbers(n):
                pool.wait_ge(g_ready, n)
                nc.gpsimd.iota(g_nodes.bitcast(I32), [[1, NP]], base=0, channel_multiplier=0).then_inc(g_iota, 1)
                nc.gpsimd.iota(g_node_c.bitcast(I32), [[P, NT]], base=0, channel_multiplier=1).then_inc(g_iota, 1)

            with pool.If(path > 0):
                node_numbers(1)
                general_gathers(G_MAX, max_tab, 1, 1)
                node_numbers(2)
                general_gathers(G_FIRST, xu_tab, UW, 1)
                node_numbers(3)
                general_gathers(2, row_tab, H, 2)
                node_numbers(4)
                general_gathers(3, row_tab, H, 3)
                general_gathers(G_TARGETS, hmv_tab, UW, 4)
            pool.wait_ge(tabs_zeroed, TABLES_ZEROED)

            def scatter(g):
                for h in range(2):
                    pool.wait_ge(sidx_made[h], g + 1)
                    pool.wait_ge(smm_taken, g * 2 + h + 1)
                    for j in range(HT):
                        s = h * HT + j
                        wait(pool, scattered[s % NTAB], scatters_before(s, g) * 16)
                        pool.sem_inc(pool_turn, 1)
                        pool.indirect_dma_start(sums[s % NTAB], bass.IndirectOffsetOnAxis(ap=sidx[h].bitcast(U32)[:, j:j + 1], axis=0),
                                                smm[h][:, j, 0:H + 1], None, compute_op=ALU.add).then_inc(scattered[s % NTAB], 16)
            scatter(0)
            with pool.Fori(1, LOOPS) as g:
                scatter(g)
            with pool.If(path > 0):
                node_numbers(6)
                general_gathers(5, row_tab, H, 5)

        @block.scalar
        def _(act):
            def sqrt_step(n):
                act.wait_ge(sqrt_in, n)
                nc.scalar.activation(st[:, 2, :], st[:, 1, :], ACT.Sqrt).then_inc(sqrt_out, 1)

            def first_pass():

                def indices(g, h):
                    act.wait_ge(used[h], g + 1)
                    nc.scalar.copy(idx_st.bitcast(I32)[:, h, :], src_i[:, bass.ds(g * (2 * HT) + h * HT, HT)]).then_inc(idx_ready[h], 1)

                def columns(g, h):
                    wait(act, win_ready[h], g)
                    nc.scalar.copy(win_s[:, h, :], win_c[:, bass.ds(g * (2 * HT) + h * HT, HT)])
                    nc.scalar.copy(low_s[:, h, :], low_c[:, bass.ds(g * (2 * HT) + h * HT, HT)]).then_inc(stage_step, 1)

                def windows(g, h, first=False):
                    if not first:
                        c = act.value_load(coff[0:1, bass.ds(g * 2 + h, 1)], min_val=0, max_val=(DH - 1) * NT)
                    if isinstance(g, int):
                        act.wait_ge(cleared, 2)
                    else:
                        act.wait_ge(adj_stored, g * 32 + 16 * (TAIL + h - 1))
                    if not first:
                        act.wait_ge(win_taken, g * (2 * HT) + h * HT)
                        nc.scalar.copy(piece[h][:, 0:NT], piece[1 - h][:, bass.ds(c, NT)]).then_inc(carried, 1)
                        act.nop().then_inc(piece_done, 1)
                    else:
                        act.nop().then_inc(carried, 1)
                    for j in range(HT):
                        if j == (HT - 1) // SUMS_STEP + 1:
                            indices(g + h, 1 - h)
                            columns(g + 1, h)
                        c = act.value_load(toff[0:1, bass.ds(g * (2 * HT) + (h * HT + j), 1)], min_val=0, max_val=(DH - 1) * NT)
                        act.wait_ge(win_mm, g * (2 * HT) + (h * HT + j + 1))
                        ins = nc.scalar.copy(piece[h][:, bass.ds(c, WN)], win_ps[window_bank(j)])
                        ins.then_inc(win_taken, 1)

                def both(g, first=False):
                    for h in range(2):
                        windows(g, h, first and h == 0)

                indices(0, 0)
                columns(0, 0)
                columns(0, 1)
                both(0, first=True)
                with act.Fori(1, LOOPS) as g:
                    both(g)
                act.wait_ge(win_taken, T)
                act.nop().then_inc(piece_done, 1)

            def conv(m, K):
                for b in range(13):
                    n = min(4, NT - 4 * b)
                    act.wait_ge(cat_turned, 13 * m + b + 1)
                    nc.scalar.copy(cat_t[0:K, 4 * b:4 * b + n, :].rearrange("p a b -> p (a b)"),
                                   ps[0:K, 512 * (b % 3):512 * (b % 3) + n * P]).then_inc(cat_taken, 1)

            act.wait_ge(rank_arg, 1)
            nc.scalar.activation(rank_w[:, :], rank_w[:, :], ACT.Exp).then_inc(rank_made, 1)
            act.wait_ge(shifted, 1)
            nc.scalar.activation(rst_b, mx_b, ACT.Exp).then_inc(exp_made, 1)
            path = read_flag(act)
            with act.If(path < 1):
                act.wait_ge(ex_taken, 1)
                first_pass()
            with act.If(path > 0):
                act.wait_ge(g_args, 1)
                nc.scalar.activation(ex_c[:, :], ex_c[:, :], ACT.Exp).then_inc(g_exps, 1)
            act.wait_ge(elu_in, 1)
            nc.scalar.activation(tb, tb, ACT.Exp).then_inc(elu_out, 1)
            sqrt_step(1)
            act.wait_ge(cos_arg, 1)
            nc.scalar.activation(edge_b, edge_b, ACT.Sin, scale=-PI / CUTOFF, bias=half_pi[:, :]).then_inc(cos_made, 1)
            conv(0, 2 * H + 1)
            conv(1, 2 * H + 1)
            sqrt_step(2)
            act.wait_ge(s1_ones, 1)
            act.wait_ge(hmv_made, 1)

            def window(g, h):
                c = act.value_load(hcol[0:1, bass.ds(g * 2 + h, 1)], min_val=0, max_val=(NT - 1) * 3 * UW)
                nc.scalar.copy(hwin[h], HMV_flat[:, bass.ds(c, 6 * UW)]).then_inc(hwin_made[h], 1)

            window(0, 0)
            def take_sums(g, h):
                act.wait_ge(summed[h], g + 1)
                for k in range(NTAB):
                    wait(act, scattered[k], scatters_through(k, h, g - 1) * 16 if not (isinstance(g, int) and g == 0) else 0)
                for i, (k0, n, v) in enumerate(sum_runs):
                    ins = nc.scalar.copy(smm[h][:, k0:k0 + n, :], v)
                ins.then_inc(smm_taken, 1)

            def third(g, general, first=False):
                for h in range(2):
                    wait(act, gate_mm[h], g)
                    for c in range(2):
                        act.wait_ge(z_mm, g * 4 + (2 * h + c + 1))
                        nc.scalar.activation(s1t[h][0:2 * H, c * CH:(c + 1) * CH], z_ps[c], ACT.Silu, bias=b1c[:, 0:1]).then_inc(silu_done, 1)
                    act.wait_ge(picked[h], g + 1)
                    wait(act, msg_made[h], g)
                    if general:
                        act.sem_inc(g_turn, 1)
                        nc.scalar.dma_start(hg[h].rearrange("p a b -> p (a b)"),
                                            hg_edges[bass.ds(g * 2 + h, 1)].rearrange("a p f -> (a p) f")).then_inc(g_hg_in, 16)
                        act.wait_ge(g_hg_in, g * 32 + 16 * (h + 1))
                        act.sem_inc(hg_taken, 1)
                    else:
                        for k0, n, v in pick_runs:
                            ins = nc.scalar.copy(hg[h][:, k0:k0 + n, :], v)
                        ins.then_inc(hg_taken, 1)
                    if h == 0:
                        wait(act, picked[1], g)
                    window(g + h, 1 - h)
                    act.wait_ge(gate_mm[h], g + 1)
                    for k0, n, v in gate_runs:
                        ins = nc.scalar.copy(gate[h][:, k0:k0 + n, :], v)
                    ins.then_inc(gates_taken, 1)
                    if h == 1:
                        take_sums(g, 0)
                    elif not first:
                        take_sums(g - 1, 1)

            with act.If(path < 1):
                third(0, False, first=True)
                with act.Fori(1, LOOPS) as g:
                    third(g, False)
            with act.If(path > 0):
                third(0, True, first=True)
                with act.Fori(1, LOOPS) as g:
                    third(g, True)
            take_sums(LOOPS - 1, 1)
            sqrt_step(3)
            sqrt_step(4)
            act.wait_ge(cat_made, 3)
            conv(2, H)
            sqrt_step(5)
            sqrt_step(6)

        @block.tensor
        def _(pe):
            pe.wait_ge(emb_loaded, 16 * 3)
            nc.tensor.matmul(ps[0:NEL, 7 * 512:7 * 512 + G], embt[:, :], adt[:, :], start=True, stop=True).then_inc(ev_mm, 1)
            pe.wait_ge(ev_made, 1)
            pe.wait_ge(ohz_made, 1)
            for i in range(NT):
                ins = nc.tensor.matmul(uv_ps[:, i, :], ohz[:, i * P:(i + 1) * P], ev[:, :], start=True, stop=True)
            ins.then_inc(uv_mm, 1)
            pe.wait_ge(carry_out, 1)
            for c in range(4):
                ins = nc.tensor.transpose(ps[0:1, 7 * 512 + c * Q:7 * 512 + (c + 1) * Q], carry[:, c:c + 1], ident[0:Q, 0:Q])
            ins.then_inc(carry_rows, 1)
            pe.wait_ge(carry_scanned, 1)
            for c in range(2):
                ins = nc.tensor.transpose(ps[0:Q, 7 * 512 + 4 * Q + 4 * c:7 * 512 + 4 * Q + 4 * c + 1], cscan[0:1, c, :], ident[0:1, 0:1])
            nc.tensor.transpose(ps[0:1, 7 * 512:7 * 512 + P], bad_1[:, :], ident[:, :]).then_inc(carry_back, 1)
            pe.wait_ge(exp_made, 1)
            pe.wait_ge(uv_taken, 1)
            for b in range(HT):
                ins = nc.tensor.transpose(ps[:, b * P:b * P + Q], rst_b[:, b * P:(b + 1) * P], ident[0:Q, 0:Q])
            ins.then_inc(ex_turned, 1)

            def first_pass():
                for h in range(2):
                    pe.sem_inc(used[h], 1)
                width = 3 * (H + 1) + 1

                def window_products(g, h, j):
                    nc.tensor.matmul(win_ps[window_bank(j)], low_oh[h][:, j, :], win_oh[h][:, j, :], start=True, stop=False)

                def window_column(g, h, j):
                    return pe.value_load(toff[0:1, bass.ds(g * (2 * HT) + (h * HT + j), 1)], min_val=0, max_val=(DH - 1) * NT)

                def windows(g, h, sums=None):
                    pe.wait_ge(win_ready[h], g + 1)
                    window_products(g, h, 0)
                    window_products(g, h, 1)
                    c = window_column(g, h, 0)
                    next_c = window_column(g, h, 1)
                    for j in range(HT):
                        if 0 < j < HT - 1:
                            window_products(g, h, j + 1)
                            next_c = window_column(g, h, j + 1)
                        if j == 0:
                            pe.wait_ge(carried, g * 2 + (h + 1))
                        else:
                            pe.wait_ge(win_taken, g * (2 * HT) + (h * HT + j))
                        nc.tensor.matmul(win_ps[window_bank(j)][:, 0:NT], ident_b[:, :], piece[h][:, bass.ds(c, NT)],
                                         start=False, stop=True).then_inc(win_mm, 1)
                        c = next_c
                        if sums and j == 0:
                            pe.wait_ge(oh_ready[sums[1]], sums[0] + 1)
                            pe.wait_ge(gathered[sums[1]], (sums[0] + 1) * (16 * HT))
                        if sums and SUMS_STEP * j < HT:
                            tile_sums(sums[1], range(SUMS_STEP * j, min(SUMS_STEP * (j + 1), HT)))

                def tile_sums(h, tiles):
                    for j in tiles:
                        for w in range(2):
                            ins = nc.tensor.matmul(part_sums[h][:, w, 0:width], oh[:, h * HT + j, w * P:(w + 1) * P],
                                                   gw_p[h][:, j, 0:width], start=(j == 0), stop=(j == HT - 1))
                    if tiles[-1] == HT - 1:
                        ins.then_inc(used[h], 1)

                windows(0, 0)
                windows(0, 1, (0, 0))
                with pe.Fori(1, LOOPS) as g:
                    windows(g, 0, (g - 1, 1))
                    windows(g, 1, (g, 0))
                pe.wait_ge(oh_ready[1], LOOPS)
                pe.wait_ge(gathered[1], LOOPS * (16 * HT))
                tile_sums(1, range(HT))

            def product(k):
                pe.wait_ge(rows_made, k + 1)

                def block(i, r, turn):
                    n = k * NT + i
                    pe.wait_ge(block_in[r], turn)
                    wait(pe, block_summed, n - AB + 1)
                    for a in range(NT):
                        ins = nc.tensor.matmul(ps[:, 512 * r:512 * r + 3 * H], blocks[r][:, :, a], parts[:, a, :],
                                               start=(a == 0), stop=(a == NT - 1))
                    ins.then_inc(block_used, 1)

                def turn(n):
                    return (n // AB + 1) * 16
                for i in range(AB):
                    block(i, (k * NT + i) % AB, turn(k * NT + i))
                with pe.Fori(1, NT // AB) as s:
                    for r in range(AB):
                        block(s * AB + r, (k * NT + r) % AB, s * 16 + turn(k * NT + r))
                for i in range(NT // AB * AB, NT):
                    block(i, (k * NT + i) % AB, turn(k * NT + i))

            def conv(m, source, K, rhs):
                pe.wait_ge(cat_made, m + 1)
                for b in range(13 + 1):
                    if b < 13:
                        if b >= 3:
                            pe.wait_ge(cat_taken, 13 * m + b - 2)
                        for i in range(4 * b, min(4 * b + 4, NT)):
                            c = 512 * (b % 3) + (i % 4) * P
                            ins = nc.tensor.transpose(ps[0:K, c:c + P], source[:, i, :], ident[:, :])
                        ins.then_inc(cat_turned, 1)
                    if b >= 1:
                        pe.wait_ge(cat_taken, 13 * m + b)
                        for i in range(4 * b - 4, min(4 * b, NT)):
                            ins = nc.tensor.matmul(conv_ps[i // 10][:, i % 10, :], cat_t[0:K, i, :], rhs, start=True, stop=True)
                ins.then_inc(conv_done, 1)

            path = read_flag(pe)

            def general_sums(m, rows, width):
                pe.wait_ge(g_ready, {G_FIRST: 2, 2: 3, 3: 4, 5: 6}[m])
                for b in range(7):
                    nc.tensor.matmul(ps[:, b * 512:(b + 1) * 512], zero[:, 0:P], zero[:, :], start=True, stop=False,
                                     skip_group_check=True)
                pe.sem_inc(g_loops[m]["mm"], 1)
                with pe.Fori(0, T) as t:
                    pe.wait_ge(g_loops[m]["row"], t * 16 + 16)
                    pe.wait_ge(g_loops[m]["oh"], t + 1)
                    for w in range(NT):
                        ins = nc.tensor.matmul(g_sums[:, w, 0:width], g_oh[:, w * P:(w + 1) * P], rows[:, 0:width],
                                               start=False, stop=False, skip_group_check=True)
                    ins.then_inc(g_loops[m]["mm"], 1)

            pe.wait_ge(wts_loaded, 16 * 18)
            with pe.If(path < 1):
                first_pass()
                product(0)
            with pe.If(path > 0):
                general_sums(G_FIRST, g_wrows, AW)
                general_sums(2, g_rows, H)
            conv(0, cat, 2 * H + 1, wcat[0:2 * H + 1, 0, :])
            with pe.If(path < 1):
                product(1)
            with pe.If(path > 0):
                general_sums(3, g_rows, H)
            conv(1, cat, 2 * H + 1, wcat[0:2 * H + 1, 1, :])

            def first_product(g, h):
                pe.wait_ge(e_in[h], (g + 1) * 64)
                wait(pe, gates_taken, g * 2 + h)
                for c in range(2):
                    ins = nc.tensor.matmul(z_ps[c], w1t[:, :], attr_s[h][:, c * CH:(c + 1) * CH], start=True, stop=True)
                    ins.then_inc(z_mm, 1)
                pe.wait_ge(z_mm, g * 4 + (2 * h + 2))
                pe.nop().then_inc(z_used[h], 1)

            def pick(g, h):
                pe.wait_ge(oht_made[h], g + 1)
                pe.wait_ge(hwin_made[h], g + 1)
                wait(pe, hg_taken, g * 2 + h)
                for j in range(HT):
                    for w in range(2):
                        for part in range(3):
                            ins = nc.tensor.matmul(slot(pick_runs, j), oh_t[h][:, w, j * P:(j + 1) * P],
                                                   hwin[h][:, (3 * w + part) * UW:(3 * w + part + 1) * UW],
                                                   start=(w == 0 and part == 0), stop=(w == 1 and part == 2))
                ins.then_inc(picked[h], 1)

            def combine(g, h):
                pe.wait_ge(msg_made[h], g + 1)
                pe.wait_ge(eq_made[h], g + 1)
                wait(pe, smm_taken, g * 2 + h)
                for j in range(HT):
                    o = slot(sum_runs, j)
                    for part in range(3):
                        nc.tensor.matmul(o[:, 0:H + 1], eq[h][:, j, :], msg_p[h][:, j, part * (H + 1):(part + 1) * (H + 1)],
                                         start=(part == 0), stop=(part == 2))
                    ins = nc.tensor.matmul(o[:, H + 1:H + 2], eq[h][:, j, :], rank_b[:, :], start=True, stop=True)
                ins.then_inc(summed[h], 1)

            def gates(g, h):
                pe.wait_ge(silu_done, g * 4 + (2 * h + 2))
                for q in range(PT):
                    ins = nc.tensor.matmul(gate_pairs[q], s1t[h][:, q * P:(q + 1) * P], w2b[:, :], start=True, stop=True)
                ins.then_inc(gate_mm[h], 1)

            def third(g, first=False):
                for h in range(2):
                    first_product(g, h)
                    pick(g, h)
                    gates(g, h)
                    if h == 1:
                        combine(g, 0)
                    elif not first:
                        combine(g - 1, 1)

            pe.wait_ge(hmv_made, 1)
            third(0, first=True)
            with pe.Fori(1, LOOPS) as g:
                third(g)
            combine(LOOPS - 1, 1)
            conv(2, X, H, w3s[:, :])
            with pe.If(path < 1):
                product(2)
            with pe.If(path > 0):
                general_sums(5, g_rows, H)

        @block.vector
        def _(dve):
            V = nc.vector
            n_step = [0]

            def step(ins):
                n_step[0] += 1
                ins.then_inc(dve_step, 1)
                dve.wait_ge(dve_step, n_step[0])

            def tt(o, x, y, op):
                step(V.tensor_tensor(o, x, y, op))

            def ts(o, x, s1, op0, s2=None, op1=None):
                step(V.tensor_scalar(o, x, s1, s2, op0, op1) if op1 is not None else V.tensor_scalar(o, x, s1, None, op0))

            def split(p, v, rest):
                step(V.tensor_copy(p[0], v))
                tt(rest, v, p[0], ALU.subtract)
                step(V.tensor_copy(p[1], rest))
                tt(p[2], rest, p[1], ALU.subtract)

            V.memset(zero[:, :], 0.0).then_inc(zeros_made, 1)
            step(V.memset(HMV[:, NT, :, :], 0.0))
            step(V.memset(w1t[:, :], 0.0))
            step(V.memset(w2b[:, :], 0.0))
            step(V.memset(row_ends[:, 0:1], -1.0))
            step(V.memset(row_ends[:, 1:2], float(N)))
            step(V.tensor_copy(prev_i[:, :], row_ends[:, 0:1]))
            V.tensor_copy(next_i[:, :], row_ends[:, 1:2]).then_inc(edges_init, 1)
            step(V.memset(half_pi[:, :], PI / 2))
            dve.wait_ge(consts_made, 2)
            step(V.tensor_copy(iota_f[:, :], iota_i[:, :]))
            step(V.tensor_copy(iota_p[:, :], ip_i[:, :]))
            ts(dump_i[:, :], iota_p[:, 0:1], float(NP), ALU.add)
            ts(ident[:, :], iota_f[:, 0:P], iota_p[:, 0:1], ALU.is_equal)
            step(V.tensor_copy(ident_b[:, :], ident[:, :]))
            step(V.tensor_copy(iota_b[:, :], iota_i[:, :]))
            ts(rank_w[:, 0:1], iota_p[:, 0:1], -LN3, ALU.mult, 63 * LN3, ALU.add)
            V.tensor_scalar(rank_w[:, 1:2], iota_p[:, 0:1], LN3, -63 * LN3, ALU.mult, ALU.add).then_inc(rank_arg, 1)
            dve.wait_ge(rank_made, 1)
            step(V.tensor_copy(rank_b[:, :], rank_w[:, 0:1]))
            step(V.tensor_copy(rank_c[:, :], rank_w[:, 1:2]))
            dve.wait_ge(edges_loaded, 16 * 5)
            bi = base_i.bitcast(I32)
            biq = bi.rearrange("p (q k) -> p q k", k=HT)
            ts(hoff[:, :], biq[0:1, :, 0], NT, ALU.mult)
            tt(toff[:, :].rearrange("p (q k) -> p q k", k=HT), biq[0:1, :, :], biq[0:1, :, 0].unsqueeze(2).to_broadcast([1, Q, HT]), ALU.subtract)
            ts(toff[:, :], toff[:, :], NT, ALU.mult)
            step(V.memset(coff[:, :], 0))
            tt(coff[:, 1:Q], hoff[:, 1:Q], hoff[:, 0:Q - 1], ALU.subtract)
            tt(win_c[:, 0:T], dc_i.bitcast(I32), bi, ALU.subtract)
            step(V.memset(src_i[:, T:T + 2 * HT], 0))
            step(V.memset(win_c[:, T:T + 2 * HT], 0.0))
            ts(low_c[:, 0:T].bitcast(I32), src_i[:, 0:T], 7, ALU.logical_shift_right)
            step(V.scalar_tensor_tensor(out=win_c[:, 0:T], in0=win_c[:, 0:T], scalar=float(NT), in1=low_c[:, 0:T].bitcast(I32), op0=ALU.mult, op1=ALU.add))
            ts(low_c.bitcast(I32), src_i[:, 0:T + 2 * HT], P - 1, ALU.bitwise_and)
            step(V.tensor_copy(low_c, low_c.bitcast(I32)))
            ts(base_c[:, :], bi.rearrange("p (q k) -> p q k", k=HT)[:, :, 0], -P, ALU.bitwise_and)
            tt(rel_c[:, :].rearrange("p (q k) -> p q k", k=HT), dc_i.bitcast(I32).rearrange("p (q k) -> p q k", k=HT),
               bc(base_c[:, :], HT), ALU.subtract)
            ts(acol[:, :], base_c[0:1, :], AW / P, ALU.mult)
            step(V.memset(hcol[:, :], 0))
            ts(hcol[:, 0:Q], base_c[0:1, :], 3 * UW / P, ALU.mult)
            dve.wait_ge(types_loaded, 16)
            V.tensor_scalar(ohz, z_b.bitcast(I32), iota_p[0:NEL, 0:1], None, ALU.is_equal).then_inc(ohz_made, 1)
            dve.wait_ge(ev_mm, 1)
            V.tensor_copy(ev[:, G:2 * G], ps[0:NEL, 7 * 512:7 * 512 + G]).then_inc(ev_made, 1)
            dri = dr_i.bitcast(I32)
            ts(base_r[:, :], dri[:, 0:1], -P, ALU.bitwise_and)
            V.tensor_tensor(rel_r[:, :], dri, base_r[:, :].to_broadcast([Q, W]), ALU.subtract).then_inc(rel_rows_made, 1)
            step(V.tensor_copy(dr_f, dri))
            dve.wait_ge(edge_ends, 32)
            step(V.tensor_copy(prev_f[:, :], prev_i[:, :]))
            step(V.tensor_copy(next_f[:, :], next_i[:, :]))
            step(V.memset(bad[:, :], 0.0))
            step(V.tensor_scalar(mx_b, dr_f, float(N - 1), None, ALU.min))
            tiles = mx_b.rearrange("q (b e) -> q b e", e=P)
            tt(mx_f[:, 0:W - 1], mx_b[:, 0:W - 1], mx_b[:, 1:W], ALU.is_gt)
            step(V.tensor_reduce(bad[0:Q, 0:1], mx_f[:, 0:W - 1], AX.X, ALU.max))
            tt(bad[0:Q, 1:2], mx_b[:, W - 1:W], next_f[:, :], ALU.is_gt)
            tt(rst_f[:, 0:HT], tiles[:, :, P - 1], tiles[:, :, 0], ALU.subtract)
            step(V.tensor_reduce(bad[0:Q, 2:3], rst_f[:, 0:HT], AX.X, ALU.max))
            ts(bad[0:Q, 2:3], bad[0:Q, 2:3], float(DW - 1), ALU.is_gt)
            tt(rst_f[:, 0:HT - 1], tiles[:, 1:HT, 0], tiles[:, 0:HT - 1, 0], ALU.subtract)
            tt(rst_f[:, HT - 1:HT], next_f[:, :], tiles[:, HT - 1, 0].unsqueeze(1), ALU.subtract)
            step(V.tensor_reduce(bad[0:Q, 7:8], rst_f[:, 0:HT], AX.X, ALU.max))
            ts(bad[0:Q, 7:8], bad[0:Q, 7:8], float(DW - 1), ALU.is_gt)
            tt(bad[0:Q, 3:4], mx_b[:, W - 1:W], mx_b[:, 0:1], ALU.subtract)
            ts(bad[0:Q, 3:4], bad[0:Q, 3:4], float(DH - 1), ALU.is_gt)
            tt(bad[0:Q, 4:5], next_f[:, :], mx_b[:, 0:1], ALU.subtract)
            ts(bad[0:Q, 4:5], bad[0:Q, 4:5], float(DH), ALU.is_gt)
            ts(bad[0:1, 5:6], mx_b[0:1, 0:1], 0.0, ALU.is_gt)
            tt(tmp_c[:, 0:T - 2], dc_i.bitcast(I32)[:, 2:T], dc_i.bitcast(I32)[:, 0:T - 2], ALU.is_equal)
            step(V.tensor_reduce(bad[:, 6:7], tmp_c[:, 0:T - 2], AX.X, ALU.max))
            step(V.tensor_reduce(bad_1[:, :], bad[:, :], AX.X, ALU.max))
            dve.wait_ge(prep_loaded, 16 * 3)
            dve.wait_ge(uv_mm, 1)
            step(V.tensor_copy(xu[:, :, H + 1:UW], uv_ps[:, :, 0:G]))
            step(V.tensor_copy(xu[:, :, 0:H], X[:, :, :]))
            step(V.memset(xu[:, :, H:H + 1], 1.0))
            V.engine_nop().then_inc(xu_made, 1)
            step(V.memset(rst_b[:, W - 1:W], -BIG))
            tt(rst_b[:, 0:W - 1], dr_f[:, 0:W - 1], dr_f[:, 1:W], ALU.not_equal)
            ts(rst_b[:, 0:W - 1], rst_b[:, 0:W - 1], -BIG, ALU.mult)
            step(V.memset(rst_f[:, 0:1], -BIG))
            step(V.tensor_copy(rst_f[:, 1:W], rst_b[:, 0:W - 1]))
            step(V.tensor_tensor_scan(mx_f, rst_f, e1_s, -BIG, ALU.add, ALU.max))
            step(V.tensor_tensor_scan(mx_b[:, ::-1], rst_b[:, ::-1], e1_s[:, ::-1], -BIG, ALU.add, ALU.max))
            d0, d1 = dr_f[:, 0:1], dr_f[:, W - 1:W]
            tt(pen[:, 0:1], prev_f[:, :], d0, ALU.not_equal)
            tt(pen[:, 1:2], next_f[:, :], d1, ALU.not_equal)
            tt(pen[:, 2:3], d0, d1, ALU.not_equal)
            ts(pen[:, :], pen[:, :], -BIG, ALU.mult)
            step(V.tensor_copy(carry[:, 0:1], mx_f[:, W - 1:W]))
            tt(carry[:, 1:2], pen[:, 0:1], pen[:, 2:3], ALU.add)
            step(V.tensor_copy(carry[:, 2:3], mx_b[:, 0:1]))
            V.tensor_tensor(carry[:, 3:4], pen[:, 1:2], pen[:, 2:3], ALU.add).then_inc(carry_out, 1)
            dve.wait_ge(carry_rows, 1)
            step(V.tensor_copy(crow[:, :, :], ps[0:1, 7 * 512:7 * 512 + 4 * Q].rearrange("p (a b) -> p a b", b=Q)))
            step(V.memset(cscan[:, :, :], -BIG))
            step(V.tensor_tensor_scan(cst[:, 0, :], crow[:, 1, :], crow[:, 0, :], -BIG, ALU.add, ALU.max))
            step(V.tensor_tensor_scan(cst[:, 1, ::-1], crow[:, 3, ::-1], crow[:, 2, ::-1], -BIG, ALU.add, ALU.max))
            step(V.tensor_copy(cscan[:, 0, 1:Q], cst[:, 0, 0:Q - 1]))
            V.tensor_copy(cscan[:, 1, 0:Q - 1], cst[:, 1, 1:Q]).then_inc(carry_scanned, 1)
            dve.wait_ge(carry_back, 1)
            step(V.tensor_reduce(bad_1[0:1, :], ps[0:1, 7 * 512:7 * 512 + P], AX.X, ALU.max))
            step(V.tensor_copy(flag[:, :], bad_1[0:1, :]))
            V.engine_nop().then_inc(flag_made, 1)
            for c in range(2):
                tt(cin[:, c:c + 1], ps[0:Q, 7 * 512 + 4 * Q + 4 * c:7 * 512 + 4 * Q + 4 * c + 1], pen[:, c:c + 1], ALU.add)
            tt(mx_f, mx_f, mx_b, ALU.max)
            for c, d in ((0, d0), (1, d1)):
                ts(mx_b, dr_f, d, ALU.not_equal, -BIG, ALU.mult)
                step(V.scalar_tensor_tensor(out=mx_f, in0=mx_b, scalar=cin[:, c:c + 1], in1=mx_f, op0=ALU.add, op1=ALU.max))
            V.tensor_tensor(mx_b, e1_s, mx_f, ALU.subtract).then_inc(shifted, 1)
            dve.wait_ge(shifted, 1)
            dve.wait_ge(xu_stored, 16)
            split([HMV[:, 0:NT, c, H + 1:UW] for c in range(3)], uv_ps[:, :, G:2 * G], v_rest)
            V.engine_nop().then_inc(uv_taken, 1)
            dve.wait_ge(ex_turned, 1)
            step(V.tensor_copy(ex_c[:, :].rearrange("p (q b) -> p b q", b=HT),
                               ps[:, 0:HT * P].rearrange("p (b q) -> p b q", q=P)[:, :, 0:Q]))
            V.memset(idx_st.rearrange("p a b -> p (a b)"), 0.0).then_inc(ex_taken, 1)

            def first_pass():

                def fold(g, h):
                    n = (g * 2 + h) * 3
                    dve.wait_ge(used[h], g + 2)
                    c = dve.value_load(acol[0:1, bass.ds(g * 2 + h, 1)], min_val=0, max_val=(NT - 1) * AW)
                    v = part_sums[h][:, :, 0:3 * (H + 1)].rearrange("p w (c f) -> p w f c", c=3)
                    V.tensor_copy(fold_s[h][:, :, H + 1], part_sums[h][:, :, 3 * (H + 1)]).then_inc(fold_step, 1)
                    V.tensor_reduce(fold_s[h][:, :, 0:H + 1], v, AX.X, ALU.add).then_inc(fold_step, 1)
                    dve.wait_ge(fold_step, n + 2)
                    V.tensor_tensor(ACC_flat[:, bass.ds(c, 2 * AW)], ACC_flat[:, bass.ds(c, 2 * AW)],
                                    fold_s[h].rearrange("p a b -> p (a b)"), ALU.add).then_inc(fold_step, 1)

                def window_operands(g, h):
                    dve.wait_ge(stage_step, g * 2 + (h + 1))
                    wait(dve, win_mm, g * (2 * HT) + (h - 1) * HT)
                    for j in range(HT):
                        V.tensor_scalar(win_oh[h][:, j, :], iota_h, win_s[:, h, j:j + 1], None, ALU.is_equal)
                        ins = V.tensor_scalar(low_oh[h][:, j, :], iota_b[:, 0:P], low_s[:, h, j:j + 1], None, ALU.is_equal)
                    ins.then_inc(win_ready[h], 1)

                def operands(g, h, first=False, last=False):
                    t0 = g * (2 * HT) + h * HT
                    if not last:
                        window_operands(g + h, 1 - h)
                    dve.wait_ge(used[h], g + 1)
                    V.tensor_tensor(oh[:, h * HT:(h + 1) * HT, 0:OW], bm(iota_b[:, 0:OW], HT), bc(rel_c[:, bass.ds(t0, HT)], OW), ALU.is_equal)
                    if h == 1:
                        fold(g, 0)
                    elif not first:
                        fold(g - 1, 1)
                    n = g * 2 + h
                    dve.wait_ge(gathered[h], (g + 1) * (16 * HT))
                    p = [gw_p[h][:, :, c * (H + 1):(c + 1) * (H + 1)] for c in range(3)]
                    V.tensor_tensor(gw[h], G_ring[:, h, :, 0:H + 1], bc(ex_c[:, bass.ds(t0, HT)], H + 1), ALU.mult).then_inc(gw_step, 1)
                    dve.wait_ge(gw_step, n * 4 + 1)
                    V.tensor_copy(p[0], gw[h]).then_inc(gw_step, 1)
                    dve.wait_ge(gw_step, n * 4 + 2)
                    V.tensor_tensor(gw_r, gw[h], p[0], ALU.subtract).then_inc(gw_step, 1)
                    dve.wait_ge(gw_step, n * 4 + 3)
                    V.tensor_copy(p[1], gw_r).then_inc(gw_step, 1)
                    dve.wait_ge(gw_step, n * 4 + 4)
                    V.tensor_tensor(p[2], gw_r, p[1], ALU.subtract).then_inc(oh_ready[h], 1)

                step(V.memset(ACC[:, :, :], 0.0))
                for c in range(0, WN, P):
                    n = min(P, WN - c)
                    ts(iota_h[:, c:c + n], iota_f[:, 0:n], float(c), ALU.add)
                step(V.memset(oh[:, :, OW:2 * P], 0.0))
                for h in range(2):
                    V.memset(piece[h].bitcast(F32), 0.0).then_inc(cleared, 1)
                for h in range(2):
                    step(V.memset(fold_s[h], 0.0))
                    step(V.memset(gw_p[h][:, :, 3 * (H + 1)], 1.0))
                window_operands(0, 0)
                operands(0, 0, first=True)
                operands(0, 1)
                with dve.Fori(1, LOOPS - 1) as g:
                    operands(g, 0)
                    operands(g, 1)
                operands(LOOPS - 1, 0)
                operands(LOOPS - 1, 1, last=True)
                fold(LOOPS - 1, 1)
                dve.wait_ge(fold_step, 2 * LOOPS * 3)
                dve.wait_ge(u_stored[0], 16 * LOOPS)
                dve.wait_ge(u_stored[1], 16 * LOOPS)
                dve.wait_ge(adj_stored, 16 * (TAIL + 2 * LOOPS))

            def table_rows(v):
                split([parts[:, :, c * H:(c + 1) * H] for c in range(3)], v, tb)

            def take_products(k):
                def take(i, r):
                    n = k * NT + i
                    dve.wait_ge(block_used, n + 1)
                    v = ps[:, 512 * r:512 * r + 3 * H].rearrange("p (c f) -> p f c", c=3)
                    V.tensor_reduce(ACC_flat[:, bass.ds(i * AW, H)], v, AX.X, ALU.add).then_inc(block_summed, 1)
                with dve.Fori(0, NT // AB) as s:
                    for r in range(AB):
                        take(s * AB + r, (k * NT + r) % AB)
                for i in range(NT // AB * AB, NT):
                    take(i, (k * NT + i) % AB)
                dve.wait_ge(block_summed, (k + 1) * NT)

            n_norm = [0]

            def layernorm(v, o, sq, gain=None, shift=None):
                n_norm[0] += 1
                step(V.tensor_reduce(st[:, 0, :], v, AX.X, ALU.add))
                ts(st[:, 0, :], st[:, 0, :], -1.0 / H, ALU.mult)
                tt(v, v, bc(st[:, 0, :], H), ALU.add)
                tt(sq, v, v, ALU.mult)
                step(V.tensor_reduce(st[:, 1, :], sq, AX.X, ALU.add))
                V.tensor_scalar(st[:, 1, :], st[:, 1, :], 1.0 / H, EPS, ALU.mult, ALU.add).then_inc(sqrt_in, 1)
                dve.wait_ge(sqrt_out, n_norm[0])
                step(V.reciprocal(st[:, 3, :], st[:, 2, :]))
                tt(o, v, bc(st[:, 3, :], H), ALU.mult)
                if gain is not None:
                    tt(o, o, bm(gain, NT), ALU.mult)
                    tt(o, o, bm(shift, NT), ALU.add)

            path = read_flag(dve)
            g_steps = [0]

            def gs(ins):
                g_steps[0] += 1
                ins.then_inc(g_step, 1)
                dve.wait_ge(g_step, g_steps[0])

            def general_start(n, tables=True):
                V.engine_nop().then_inc(g_ready, 1)
                if tables:
                    dve.wait_ge(g_iota, 2 * (n - (1 if n > 5 else 0)))
                    gs(V.tensor_copy(g_nodes, g_nodes.bitcast(I32)))
                    gs(V.tensor_copy(g_node_c, g_node_c.bitcast(I32)))
                gs(V.tensor_copy(g_src, src_i[:, 0:T]))
                gs(V.memset(g_zero, 0.0))

            def general_loop(m, index, body):
                lp = g_loops[m]
                with dve.Fori(0, T) as t:
                    if m != G_MAX and m != G_TARGETS:
                        dve.wait_ge(lp["mm"], t + 1)
                    if m == G_FIRST or m == G_TARGETS:
                        dve.wait_ge(lp["st"], t * 16 + 16)
                    V.tensor_tensor(g_idx_s.bitcast(I32), index[:, bass.ds(t, 1)], g_zero, ALU.add).then_inc(lp["idx"], 1)
                    body(t)

            def one_hot_rows(t):
                return V.tensor_tensor(g_oh, g_nodes, g_dst[:, bass.ds(t, 1)].to_broadcast([P, NP]), ALU.is_equal)

            def max_body(t):
                dve.wait_ge(g_loops[G_MAX]["row"], t * 16 + 16)
                V.tensor_tensor(ex_c[:, bass.ds(t, 1)], g_e1[:, bass.ds(t, 1)], g_rows[:, 0:1], ALU.subtract)

            def first_body(t):
                one_hot_rows(t)
                dve.wait_ge(g_loops[G_FIRST]["row"], t * 16 + 16)
                V.tensor_tensor(g_wrows[:, 0:H + 1], g_rows[:, 0:H + 1], ex_c[:, bass.ds(t, 1)].to_broadcast([P, H + 1]),
                                ALU.mult).then_inc(g_loops[G_FIRST]["oh"], 1)

            def no_body(t):
                pass

            def general_layer(n, m, inputs):
                general_start(n)
                dve.wait_ge(g_in, 16 * inputs)
                gs(V.tensor_copy(g_dst, g_dst_i.bitcast(I32)))

                def body(t):
                    one_hot_rows(t).then_inc(g_loops[m]["oh"], 1)
                general_loop(m, g_src, body)
                dve.wait_ge(g_loops[m]["mm"], T + 1)
                gs(V.tensor_copy(ACC[:, 0:NT, 0:H], g_sums[:, :, 0:H]))

            def general_first():
                general_start(1)
                dve.wait_ge(g_in, 32)
                gs(V.tensor_copy(g_dst, g_dst_i.bitcast(I32)))
                gs(V.memset(g_max, -BIG))
                V.engine_nop().then_inc(g_seg_used, 1)
                per = 1 + 3 * NT
                with dve.Fori(0, Q) as q:
                    k = [0]

                    def ms(ins):
                        k[0] += 1
                        ins.then_inc(g_max_step, 1)
                        dve.wait_ge(g_max_step, q * per + k[0])
                    dve.wait_ge(g_seg_in, q * 32 + 32)
                    ms(V.tensor_copy(g_dst_b, g_dst_b.bitcast(I32)))
                    for w in range(NT):
                        ms(V.tensor_scalar(g_pen, g_dst_b, g_node_c[:, w:w + 1], -BIG, ALU.not_equal, ALU.mult))
                        ms(V.tensor_tensor(g_pen, g_pen, g_e1_b, ALU.add))
                        ms(V.tensor_reduce(g_max_q[:, w:w + 1], g_pen, AX.X, ALU.max))
                    V.tensor_tensor(g_max, g_max, g_max_q, ALU.max).then_inc(g_seg_used, 1)
                V.engine_nop().then_inc(g_max_made, 1)
                general_loop(G_MAX, g_dst, max_body)
                V.engine_nop().then_inc(g_args, 1)
                dve.wait_ge(g_exps, 1)
                general_start(2)
                gs(V.memset(g_wrows[:, H + 1:H + 2], 1.0))
                general_loop(G_FIRST, g_src, first_body)
                dve.wait_ge(g_loops[G_FIRST]["mm"], T + 1)
                dve.wait_ge(g_loops[G_FIRST]["st"], 16 * (T + 1))
                gs(V.tensor_copy(ACC[:, 0:NT, :], g_sums[:, :, 0:AW]))

            steps_before = n_step[0]
            with dve.If(path < 1):
                first_pass()
                V.engine_nop().then_inc(first_pass_over, 1)
            with dve.If(path > 0):
                general_first()
                dve.sem_inc(dve_step, n_step[0] - steps_before)
            ts(deg[:, :], ACC[:, 0:NT, H + 1], 1.0, ALU.add)
            ts(st[:, 4, :], ACC[:, 0:NT, H], 1e-30, ALU.max)
            step(V.reciprocal(st[:, 5, :], st[:, 4, :]))
            tt(ta, ACC[:, 0:NT, 0:H], bc(st[:, 5, :], H), ALU.mult)
            V.tensor_scalar(tb, ta, 0.0, None, ALU.min).then_inc(elu_in, 1)
            dve.wait_ge(elu_in, 1)
            ts(ta, ta, 0.0, ALU.max)
            dve.wait_ge(elu_out, 1)
            step(V.scalar_tensor_tensor(out=ta, in0=tb, scalar=-1.0, in1=ta, op0=ALU.add, op1=ALU.add))
            tt(ta, ta, X[:, :, :], ALU.add)
            layernorm(ta, X[:, :, :], tb)
            table_rows(X[:, :, :])
            V.engine_nop().then_inc(rows_made, 1)

            def make_cat(first):
                step(V.tensor_copy(cat[:, :, 0:H], ACC[:, 0:NT, 0:H]))
                step(V.tensor_copy(cat[:, :, H:2 * H], (X if first else HN)[:, :, :]))
                V.memset(cat[:, :, 2 * H:2 * H + 1], 1.0).then_inc(cat_made, 1)

            periods = edge_a.bitcast(I32)
            ts(periods, cw_c[:, :], 0.5 / CUTOFF, ALU.mult)
            step(V.scalar_tensor_tensor(out=edge_b, in0=periods, scalar=-2 * CUTOFF, in1=cw_c[:, :], op0=ALU.mult, op1=ALU.add))
            step(V.scalar_tensor_tensor(out=edge_b, in0=edge_b, scalar=-1.0, in1=edge_b, op0=ALU.mult, op1=ALU.max))
            ts(edge_b, edge_b, -CUTOFF, ALU.add)
            V.scalar_tensor_tensor(out=edge_b, in0=edge_b, scalar=-1.0, in1=edge_b, op0=ALU.mult, op1=ALU.max).then_inc(cos_arg, 1)
            dve.wait_ge(cos_made, 1)
            ts(edge_b, edge_b, -0.5, ALU.mult, 0.5, ALU.add)
            step(V.scalar_tensor_tensor(out=cw_c[:, :], in0=cw_c[:, :], scalar=CUTOFF, in1=edge_b, op0=ALU.is_lt, op1=ALU.mult))
            ts(edge_a.bitcast(I32), src_i[:, 0:T], P - 1, ALU.bitwise_and)
            ts(edge_b.bitcast(I32), src_i[:, 0:T], 7, ALU.logical_shift_right)
            step(V.scalar_tensor_tensor(out=sum_row, in0=edge_a.bitcast(I32), scalar=float(NT), in1=edge_b.bitcast(I32), op0=ALU.mult, op1=ALU.add))
            with dve.If(path < 1):
                take_products(0)
            with dve.If(path > 0):
                general_layer(3, 2, 3)
            make_cat(True)
            dve.wait_ge(conv_done, 1)
            for b in range(5):
                n = min(10, NT - 10 * b)
                ts(HN[:, 10 * b:10 * b + n, :], conv_ps[b][:, 0:n, :], 0.0, ALU.max)
            table_rows(HN[:, :, :])
            V.engine_nop().then_inc(rows_made, 1)
            with dve.If(path < 1):
                take_products(1)
            with dve.If(path > 0):
                general_layer(4, 3, 4)
            make_cat(False)
            dve.wait_ge(conv_done, 2)
            for b in range(5):
                n = min(10, NT - 10 * b)
                tt(ta[:, 10 * b:10 * b + n, :], conv_ps[b][:, 0:n, :], X[:, 10 * b:10 * b + n, :], ALU.add)
            layernorm(ta, X[:, :, :], tb)
            tt(ta, X[:, :, :], bc(nv[:, :], H), ALU.mult)
            for v, c0, c1, rest in ((ta, 0, H, tb), (nv[:, :].unsqueeze(2), H, H + 1, st[:, 0, :].unsqueeze(2))):
                split([HMV[:, 0:NT, c, c0:c1] for c in range(3)], v, rest)
            with dve.If(path > 0):
                gs(V.tensor_tensor(g_hmv, HMV[:, 0:NT, 0, :], HMV[:, 0:NT, 1, :], ALU.add))
                gs(V.tensor_tensor(g_hmv, g_hmv, HMV[:, 0:NT, 2, :], ALU.add))
                general_start(5, tables=False)
                dve.wait_ge(g_in, 16 * 5)
                gs(V.tensor_copy(g_dst, g_dst_i.bitcast(I32)))
                general_loop(G_TARGETS, g_dst, no_body)
                dve.wait_ge(g_loops[G_TARGETS]["st"], 16 * (T + 1))
            step(V.memset(s1t[0], 1.0))
            V.memset(s1t[1], 1.0).then_inc(s1_ones, 1)
            V.engine_nop().then_inc(hmv_made, 1)

            def own(s, v):
                dve.wait_ge(s, v)

            def turned_one_hots(g, h):
                dve.wait_ge(e_in[h], (g + 1) * 64)
                wait(dve, picked[h], g)
                V.tensor_scalar(oh_t[h][:, 0, :], rel_b[h], iota_p[:, 0:1], None, ALU.is_equal)
                V.tensor_scalar(oh_t[h][:, 1, :], rel_b[h], iota_p[:, 1:2], None, ALU.is_equal).then_inc(oht_made[h], 1)

            def equals(g, h):
                t0 = g * (2 * HT) + h * HT
                dve.wait_ge(e_in[h], (g + 1) * 64)
                wait(dve, summed[h], g)
                V.tensor_tensor(eq[h], src_b[h].bitcast(I32), bc(src_i[:, bass.ds(t0, HT)], P), ALU.is_equal).then_inc(eq_made[h], 1)

            def targets(g, h):
                n = g * 2 + h
                t0 = g * (2 * HT) + h * HT
                dve.wait_ge(smm_taken, n + 1)
                V.tensor_scalar(first, smm[h][:, :, H + 1], rank_c[:, 0:1], 2.0, ALU.mult, ALU.is_gt).then_inc(idx_step, 1)
                V.tensor_copy(srcf, sum_row[:, bass.ds(t0, HT)]).then_inc(idx_step, 1)
                own(idx_step, n * 4 + 2)
                V.tensor_scalar(to_dump, srcf, -1.0, dump_i[:, 0:1], ALU.mult, ALU.add).then_inc(idx_step, 1)
                own(idx_step, n * 4 + 3)
                V.tensor_tensor(moved, first, to_dump, ALU.mult).then_inc(idx_step, 1)
                own(idx_step, n * 4 + 4)
                if not (isinstance(g, int) and g == 0):
                    for k in range(NTAB):
                        dve.wait_ge(scattered[k], scatters_through(k, h, g - 1) * 16)
                V.tensor_tensor(sidx[h].bitcast(I32), moved, srcf, ALU.add).then_inc(sidx_made[h], 1)

            def messages(g, h):
                n = g * 2 + h
                t0 = g * (2 * HT) + h * HT
                dve.wait_ge(hg_taken, n + 1)
                dve.wait_ge(u_in[h], (g + 1) * 16)
                m = msg
                V.tensor_tensor(uv, u_s[h], hg[h][:, :, H + 1:UW], ALU.mult).then_inc(msg_step, 1)
                own(msg_step, n * 8 + 1)
                V.tensor_reduce(adp, uv, AX.X, ALU.add).then_inc(msg_step, 1)
                own(msg_step, n * 8 + 2)
                dve.wait_ge(gates_taken, n + 1)
                V.tensor_tensor(m[:, :, 0:H], gate[h], bc(adp, H), ALU.add).then_inc(msg_step, 1)
                own(msg_step, n * 8 + 3)
                V.tensor_tensor(m[:, :, 0:H], m[:, :, 0:H], hg[h][:, :, 0:H], ALU.mult).then_inc(msg_step, 1)
                V.tensor_copy(m[:, :, H], hg[h][:, :, H])
                own(msg_step, n * 8 + 4)
                V.tensor_tensor(m[:, :, 0:H], m[:, :, 0:H], bc(cw_c[:, bass.ds(t0, HT)], H), ALU.mult).then_inc(msg_step, 1)
                own(msg_step, n * 8 + 5)
                wait(dve, summed[h], g)
                p = [msg_p[h][:, :, c * (H + 1):(c + 1) * (H + 1)] for c in range(3)]
                V.tensor_copy(p[0], m).then_inc(msg_step, 1)
                own(msg_step, n * 8 + 6)
                V.tensor_tensor(msg_r, m, p[0], ALU.subtract).then_inc(msg_step, 1)
                own(msg_step, n * 8 + 7)
                V.tensor_copy(p[1], msg_r).then_inc(msg_step, 1)
                own(msg_step, n * 8 + 8)
                V.tensor_tensor(p[2], msg_r, p[1], ALU.subtract).then_inc(msg_made[h], 1)

            def third(g, first=False, last=False):
                for h in range(2):
                    if not (last and h == 1):
                        turned_one_hots(g + h, 1 - h)
                    messages(g, h)
                    if not (last and h == 1):
                        equals(g + h, 1 - h)
                    if h == 1:
                        targets(g, 0)
                    elif not first:
                        targets(g - 1, 1)

            turned_one_hots(0, 0)
            equals(0, 0)
            third(0, first=True)
            with dve.Fori(1, LOOPS - 1) as g:
                third(g)
            third(LOOPS - 1, last=True)
            dve.wait_ge(sidx_made[0], LOOPS)
            targets(LOOPS - 1, 1)
            for k in range(NTAB):
                dve.wait_ge(sums_in[k % 2], 16 * (k // 2 + 1))
                if k == 0:
                    V.tensor_copy(agg, ld[0]).then_inc(sums_added, 1)
                else:
                    V.tensor_tensor(agg, agg, ld[k % 2], ALU.add).then_inc(sums_added, 1)
                dve.wait_ge(sums_added, k + 1)
            ts(st[:, 4, :], agg[:, :, H], 1e-8, ALU.max)
            step(V.reciprocal(st[:, 5, :], st[:, 4, :]))
            tt(ta, agg[:, :, 0:H], bc(st[:, 5, :], H), ALU.mult)
            V.engine_nop().then_inc(sums_used, 1)
            tt(ta, ta, X[:, :, :], ALU.add)
            layernorm(ta, tb, tc, gam[:, :], bet[:, :])
            tt(ta, tb, X[:, :, :], ALU.add)
            layernorm(ta, X[:, :, :], tb)
            V.engine_nop().then_inc(cat_made, 1)
            V.tensor_copy(st[:, 1, :], deg[:, :]).then_inc(sqrt_in, 1)
            n_norm[0] += 1
            dve.wait_ge(sqrt_out, n_norm[0])
            step(V.reciprocal(dinv[:, :], st[:, 2, :]))
            dve.wait_ge(conv_done, 3)
            for b in range(5):
                n = min(10, NT - 10 * b)
                tt(HN[:, 10 * b:10 * b + n, :], conv_ps[b][:, 0:n, :], bc(dinv[:, 10 * b:10 * b + n], H), ALU.mult)
            table_rows(HN[:, :, :])
            V.engine_nop().then_inc(rows_made, 1)
            with dve.If(path < 1):
                take_products(2)
            with dve.If(path > 0):
                general_layer(6, 5, 6)
            tt(ta, ACC[:, 0:NT, 0:H], HN[:, :, :], ALU.add)
            tt(ta, ta, bc(dinv[:, :], H), ALU.mult)
            tt(ta, ta, bm(b3b[:, :], NT), ALU.add)
            tt(ta, ta, X[:, :, :], ALU.add)
            layernorm(ta, X[:, :, :], tb)
            V.engine_nop().then_inc(out_made, 1)


_INS = ["x_n", "dst_r", "dst_c", "src_c", "src_f", "e1_r", "e1_c", "ew_c", "attr_t", "z_f", "nv_n",
        "emb_t", "emb", "adapt_t", "w_rel1", "w_root1", "b1", "w_rel2", "w_root2", "b2",
        "m_w1t", "m_b1", "m_w2t", "m_b2", "gamma", "beta", "w3", "b3"]


def kernel(**inputs):
    import numpy as _np
    import concourse.bacc as _bacc
    from concourse import mybir as _mybir
    from concourse.bass_utils import run_bass_kernel_spmd as _run

    def arr(name):
        return _np.asarray(inputs[name])

    def pad(a, n, fill=0):
        return _np.concatenate([a, _np.full((n - a.shape[0],) + a.shape[1:], fill, a.dtype)])

    dst, src = pad(arr("dst"), EP, PADN), pad(arr("src"), EP, PADN)
    lay = {
        "x_n": pad(arr("x"), NP).reshape(NT, P, H).transpose(1, 0, 2),
        "dst_r": dst.reshape(Q, W), "dst_c": dst.reshape(T, P).T, "src_c": src.reshape(T, P).T,
        "src_f": src,
        "e1_r": pad(arr("edge_weight1")[:, 0], EP).reshape(Q, W),
        "e1_c": pad(arr("edge_weight1")[:, 0], EP).reshape(T, P).T,
        "ew_c": pad(arr("edge_weight"), EP).reshape(T, P).T,
        "attr_t": pad(arr("edge_attr_40"), EP).T,
        "z_f": pad(arr("node_type_119"), NP), "nv_n": pad(arr("node_vec"), NP).reshape(NT, P).T,
        "emb_t": arr("L2_gnn_emb").T, "emb": arr("L2_gnn_emb"), "adapt_t": arr("L2_gnn_adaptW").T,
        "w_rel1": arr("L1_gnn_w_rel1"), "w_root1": arr("L1_gnn_w_root1"), "b1": arr("L1_gnn_b1"),
        "w_rel2": arr("L1_gnn_w_rel2"), "w_root2": arr("L1_gnn_w_root2"), "b2": arr("L1_gnn_b2"),
        "m_w1t": arr("L2_gnn_W1").T, "m_b1": arr("L2_gnn_b1"), "m_w2t": arr("L2_gnn_W2").T,
        "m_b2": arr("L2_gnn_b2"), "gamma": arr("L2_gnn_gamma"), "beta": arr("L2_gnn_beta"),
        "w3": arr("L3_gnn_W"), "b3": arr("L3_gnn_b"),
    }
    nc = _bacc.Bacc("TRN2", target_bir_lowering=False, num_devices=1)
    arrays, args = {}, []
    for name in _INS:
        a = _np.ascontiguousarray(lay[name])
        arrays[f"in_{name}_dram"] = a
        args.append(nc.dram_tensor(f"in_{name}_dram", a.shape, _mybir.dt.from_np(a.dtype), kind="ExternalInput").ap())
    args.append(nc.dram_tensor("out_0_dram", (N, H), _mybir.dt.float32, kind="ExternalOutput").ap())
    build(nc, *args)
    r = _run(nc, [arrays], core_ids=[0])
    return r.results[0]["out_0_dram"]
```
